# Optimizing a Trainium2 kernel written in Bass

```python
import numpy as np
import jax
import jax.numpy as jnp

def _softmax(x, axis=-1):
    return jax.nn.softmax(x, axis=axis)

def _gelu(x):
    return jax.nn.gelu(x, approximate=True)

def _silu(x):
    return jax.nn.silu(x)

def _sigmoid(x):
    return jax.nn.sigmoid(x)

def _layernorm(x, axis=-1, eps=1e-05):
    m = jnp.mean(x, axis=axis, keepdims=True)
    v = jnp.var(x, axis=axis, keepdims=True)
    return (x - m) / jnp.sqrt(v + eps)

def _scatter_add(tgt, idx, src, axis=0):
    return tgt.at[idx].add(src)

def _segment_sum(src, seg, n):
    return jax.ops.segment_sum(src, seg, n)
kernel_name = 'mk_macaron_d2_jaxref_r8_988ce7'

def setup_inputs(seed: int=0):
    np.random.seed(seed)
    _w = jnp.asarray

    def _L0_attn_setup():
        import jax, jax.numpy as jnp
        import numpy as np
        import math
        NUM_HEADS = 16
        TPMS_WEIGHT = 0.3
        TWO_PI = 2.0 * math.pi

        def _tpms_mask(L, phase, threshold, temperature):
            pos = jnp.arange(L, dtype=jnp.float32) / L * TWO_PI
            pq = pos[None, :, None] + phase[:, 0][:, None, None]
            pk = pos[None, None, :] + phase[:, 1][:, None, None]
            pz = (pos[None, :, None] + pos[None, None, :]) * 0.5 + phase[:, 2][:, None, None]
            t = jax.lax.stop_gradient(threshold)
            val = jnp.sin(pq) * jnp.cos(pk) + jnp.sin(pk) * jnp.cos(pz) + jnp.sin(pz) * jnp.cos(pq) - t
            return jax.nn.sigmoid(val / (temperature + 1e-06))
        key = jax.random.key(seed)
        ks = jax.random.split(key, 8)
        B, L, H = (2, 256, 128)
        nh = NUM_HEADS
        std = 0.02
        x = jax.random.normal(ks[0], (B, L, H), dtype=jnp.float32)
        Wq = jax.random.normal(ks[1], (H, H), dtype=jnp.float32) * std
        Wk = jax.random.normal(ks[2], (H, H), dtype=jnp.float32) * std
        Wv = jax.random.normal(ks[3], (H, H), dtype=jnp.float32) * std
        Wo = jax.random.normal(ks[4], (H, H), dtype=jnp.float32) * std
        bq = jnp.zeros((H,), jnp.float32)
        bk = jnp.zeros((H,), jnp.float32)
        bv = jnp.zeros((H,), jnp.float32)
        bo = jnp.zeros((H,), jnp.float32)
        phase = jax.random.normal(ks[5], (nh, 3), dtype=jnp.float32) * 0.5
        threshold = jnp.array(0.0, jnp.float32)
        temperature = jnp.array(1.0, jnp.float32)
        return {'x': x, 'Wq': Wq, 'bq': bq, 'Wk': Wk, 'bk': bk, 'Wv': Wv, 'bv': bv, 'Wo': Wo, 'bo': bo, 'phase': phase, 'threshold': threshold, 'temperature': temperature}
    _L0_attn_in = _L0_attn_setup()

    def _L0_ffn_setup():
        import jax, jax.numpy as jnp
        import numpy as np
        DIM = 128
        DEPTH = 2
        HEADS = 8
        DIM_HEAD = 64
        WINDOW = 64
        INNER = HEADS * DIM_HEAD
        HID = int(DIM * 4 * 2 / 3)
        B, N = (2, 1024)
        QK_SCALE = 8.0

        def shift_token(t):
            t1, t2 = jnp.split(t, 2, axis=-1)
            t2 = jnp.pad(t2, ((0, 0), (1, 0), (0, 0)))[:, :-1]
            return jnp.concatenate([t1, t2], axis=-1)

        def l2norm(t):
            return t / jnp.clip(jnp.linalg.norm(t, axis=-1, keepdims=True), 1e-12)

        def rotate_half(x):
            x1, x2 = jnp.split(x, 2, axis=-1)
            return jnp.concatenate([-x2, x1], axis=-1)

        def rotary_xpos(q, k):
            n = q.shape[-2]
            half_idx = jnp.arange(0, DIM_HEAD, 2, dtype=jnp.float32)
            inv_freq = 1.0 / 10000.0 ** (half_idx / DIM_HEAD)
            t = jnp.arange(n, dtype=jnp.float32)
            freqs = t[:, None] * inv_freq[None, :]
            freqs = jnp.concatenate([freqs, freqs], axis=-1)
            base = (half_idx + 0.4 * DIM_HEAD) / (1.4 * DIM_HEAD)
            power = (t - n // 2) / float(WINDOW // 2)
            scale = base[None, :] ** power[:, None]
            scale = jnp.concatenate([scale, scale], axis=-1)
            cos, sin = (jnp.cos(freqs), jnp.sin(freqs))
            q = q * cos * scale + rotate_half(q) * sin * scale
            k = k * cos / scale + rotate_half(k) * sin / scale
            return (q, k)

        def local_attention(q, k, v):
            b, h, n, d = q.shape
            w = n // WINDOW
            bq = q.reshape(b, h, w, WINDOW, d) * QK_SCALE
            bk = k.reshape(b, h, w, WINDOW, d)
            bv = v.reshape(b, h, w, WINDOW, d)

            def look_around(t):
                p = jnp.pad(t, ((0, 0), (0, 0), (1, 0), (0, 0), (0, 0)))
                return jnp.concatenate([p[:, :, :w], p[:, :, 1:]], axis=3)
            bk, bv = (look_around(bk), look_around(bv))
            bt = jnp.arange(n).reshape(w, WINDOW)
            btp = jnp.pad(bt, ((1, 0), (0, 0)), constant_values=-1)
            btk = jnp.concatenate([btp[:w], btp[1:]], axis=1)
            sim = jnp.einsum('bhwid,bhwjd->bhwij', bq, bk)
            i = bt[:, :, None]
            j = btk[:, None, :]
            mask = (i < j) | (i > j + WINDOW) | (j == -1)
            sim = jnp.where(mask, -jnp.finfo(sim.dtype).max, sim)
            attn = jax.nn.softmax(sim, axis=-1)
            out = jnp.einsum('bhwij,bhwjd->bhwid', attn, bv)
            return out.reshape(b, h, n, d)

        def _layer(x, wqkv, qs, ksc, wo, lg, lb, w1, b1, w2, b2):
            b, n, _ = x.shape
            h = shift_token(x)
            qkv = h @ wqkv
            q, k, v = jnp.split(qkv, 3, axis=-1)
            to_heads = lambda t: t.reshape(b, n, HEADS, DIM_HEAD).transpose(0, 2, 1, 3)
            q, k, v = (to_heads(q), to_heads(k), to_heads(v))
            q = l2norm(q) * qs
            k = l2norm(k) * ksc
            q, k = rotary_xpos(q, k)
            o = local_attention(q, k, v)
            o = o.transpose(0, 2, 1, 3).reshape(b, n, INNER)
            x = x + o @ wo
            h = shift_token(x)
            mu = h.mean(-1, keepdims=True)
            var = h.var(-1, keepdims=True)
            h = (h - mu) / jnp.sqrt(var + 1e-05) * lg + lb
            h = h @ w1 + b1
            a, g = jnp.split(h, 2, axis=-1)
            h = a * jax.nn.gelu(g, approximate=False)
            x = x + h @ w2 + b2
            return x
        key = jax.random.key(seed)
        ks = jax.random.split(key, 6)
        return {'x': jax.random.normal(ks[0], (B, N, DIM), jnp.float32), 'wqkv': jax.random.normal(ks[1], (DEPTH, DIM, 3 * INNER), jnp.float32) * 0.02, 'q_scale': jnp.ones((DEPTH, DIM_HEAD), jnp.float32), 'k_scale': jnp.ones((DEPTH, DIM_HEAD), jnp.float32), 'wo': jax.random.normal(ks[2], (DEPTH, INNER, DIM), jnp.float32) * 0.02, 'ln_g': jnp.ones((DEPTH, DIM), jnp.float32), 'ln_b': jnp.zeros((DEPTH, DIM), jnp.float32), 'w1': jax.random.normal(ks[3], (DEPTH, DIM, 2 * HID), jnp.float32) * 0.02, 'b1': jnp.zeros((DEPTH, 2 * HID), jnp.float32), 'w2': jax.random.normal(ks[4], (DEPTH, HID, DIM), jnp.float32) * 0.02, 'b2': jnp.zeros((DEPTH, DIM), jnp.float32)}
    _L0_ffn_in = _L0_ffn_setup()

    def _L1_attn_setup():
        import jax, jax.numpy as jnp
        import numpy as np
        DIM = 128
        HEADS = 16
        HD = DIM // HEADS
        HID = 4 * DIM
        TPF = 1374
        LR = 0.1
        NS_ITERS = 5
        TTT_STEPS = 2
        B, S = (2, 4)
        SN = S * TPF

        def _newton_schulz(G, iters=NS_ITERS):
            a, b, c = (3.4445, -4.775, 2.0315)
            X = G / (jnp.linalg.norm(G) + 1e-07)
            transposed = G.shape[0] > G.shape[1]
            if transposed:
                X = X.T
            for _ in range(iters):
                A = X @ X.T
                X = a * X + (b * A + c * (A @ A)) @ X
            return X.T if transposed else X

        def _muon_update(p, g):
            return p - LR * _newton_schulz(g)
        key = jax.random.key(seed)
        ks = jax.random.split(key, 8)
        inp = {'x': jax.random.normal(ks[0], (B, SN, DIM), jnp.float32), 'qkv_w': jax.random.normal(ks[1], (DIM, 3 * DIM), jnp.float32) * DIM ** (-0.5), 'qkv_b': jnp.zeros((3 * DIM,), jnp.float32), 'qn_scale': jnp.ones((HD,), jnp.float32), 'qn_bias': jnp.zeros((HD,), jnp.float32), 'kn_scale': jnp.ones((HD,), jnp.float32), 'kn_bias': jnp.zeros((HD,), jnp.float32), 'ttt_gate': jax.random.normal(ks[2], (DIM, HID), jnp.float32) * DIM ** (-0.5), 'ttt_val': jax.random.normal(ks[3], (DIM, HID), jnp.float32) * DIM ** (-0.5), 'ttt_proj': jax.random.normal(ks[4], (HID, DIM), jnp.float32) * HID ** (-0.5), 'proj_w': jax.random.normal(ks[5], (DIM, DIM), jnp.float32) * DIM ** (-0.5), 'proj_b': jnp.zeros((DIM,), jnp.float32)}
        return inp
    _L1_attn_in = _L1_attn_setup()

    def _L1_ffn_setup():
        import jax, jax.numpy as jnp
        import numpy as np
        B, S, D, F, E, K = (4, 256, 128, 512, 8, 2)
        FS = 128
        LN_EPS = 1e-05

        def _swiglu(x, gu_w, dn_w):
            gate, up = jnp.split(x @ gu_w, 2, axis=-1)
            gate = jnp.clip(gate, -10.0, 10.0)
            return jax.nn.silu(gate) * up @ dn_w
        key = jax.random.key(seed)
        ks = jax.random.split(key, 6)
        s = 0.02
        return {'x': jax.random.normal(ks[0], (B, S, D), jnp.float32), 'ln_gamma': jnp.ones((D,), jnp.float32), 'ln_beta': jnp.zeros((D,), jnp.float32), 'router_w': jax.random.normal(ks[1], (D, E), jnp.float32) * s, 'gate_up_w': jax.random.normal(ks[2], (E, D, 2 * F), jnp.float32) * s, 'down_w': jax.random.normal(ks[3], (E, F, D), jnp.float32) * s, 'shared_gate_up_w': jax.random.normal(ks[4], (D, 2 * FS), jnp.float32) * s, 'shared_down_w': jax.random.normal(ks[5], (FS, D), jnp.float32) * s}
    _L1_ffn_in = _L1_ffn_setup()
    _d = {'L0_attn_x': _L0_attn_in['x'], 'L0_attn_Wq': _L0_attn_in['Wq'], 'L0_attn_bq': _L0_attn_in['bq'], 'L0_attn_Wk': _L0_attn_in['Wk'], 'L0_attn_bk': _L0_attn_in['bk'], 'L0_attn_Wv': _L0_attn_in['Wv'], 'L0_attn_bv': _L0_attn_in['bv'], 'L0_attn_Wo': _L0_attn_in['Wo'], 'L0_attn_bo': _L0_attn_in['bo'], 'L0_attn_phase': _L0_attn_in['phase'], 'L0_attn_threshold': _L0_attn_in['threshold'], 'L0_attn_temperature': _L0_attn_in['temperature'], 'L0_ffn_wqkv': _L0_ffn_in['wqkv'], 'L0_ffn_q_scale': _L0_ffn_in['q_scale'], 'L0_ffn_k_scale': _L0_ffn_in['k_scale'], 'L0_ffn_wo': _L0_ffn_in['wo'], 'L0_ffn_ln_g': _L0_ffn_in['ln_g'], 'L0_ffn_ln_b': _L0_ffn_in['ln_b'], 'L0_ffn_w1': _L0_ffn_in['w1'], 'L0_ffn_b1': _L0_ffn_in['b1'], 'L0_ffn_w2': _L0_ffn_in['w2'], 'L0_ffn_b2': _L0_ffn_in['b2'], 'L1_attn_qkv_w': _L1_attn_in['qkv_w'], 'L1_attn_qkv_b': _L1_attn_in['qkv_b'], 'L1_attn_qn_scale': _L1_attn_in['qn_scale'], 'L1_attn_qn_bias': _L1_attn_in['qn_bias'], 'L1_attn_kn_scale': _L1_attn_in['kn_scale'], 'L1_attn_kn_bias': _L1_attn_in['kn_bias'], 'L1_attn_ttt_gate': _L1_attn_in['ttt_gate'], 'L1_attn_ttt_val': _L1_attn_in['ttt_val'], 'L1_attn_ttt_proj': _L1_attn_in['ttt_proj'], 'L1_attn_proj_w': _L1_attn_in['proj_w'], 'L1_attn_proj_b': _L1_attn_in['proj_b'], 'L1_ffn_ln_gamma': _L1_ffn_in['ln_gamma'], 'L1_ffn_ln_beta': _L1_ffn_in['ln_beta'], 'L1_ffn_router_w': _L1_ffn_in['router_w'], 'L1_ffn_gate_up_w': _L1_ffn_in['gate_up_w'], 'L1_ffn_down_w': _L1_ffn_in['down_w'], 'L1_ffn_shared_gate_up_w': _L1_ffn_in['shared_gate_up_w'], 'L1_ffn_shared_down_w': _L1_ffn_in['shared_down_w']}
    _x0 = _d['L0_attn_x']
    _d['L0_attn_x'] = jax.random.normal(jax.random.fold_in(jax.random.key(seed), 1), (4, 512, 128), dtype=_x0.dtype)
    del _x0
    return _d

def reference(L0_attn_x, L0_attn_Wq, L0_attn_bq, L0_attn_Wk, L0_attn_bk, L0_attn_Wv, L0_attn_bv, L0_attn_Wo, L0_attn_bo, L0_attn_phase, L0_attn_threshold, L0_attn_temperature, L0_ffn_wqkv, L0_ffn_q_scale, L0_ffn_k_scale, L0_ffn_wo, L0_ffn_ln_g, L0_ffn_ln_b, L0_ffn_w1, L0_ffn_b1, L0_ffn_w2, L0_ffn_b2, L1_attn_qkv_w, L1_attn_qkv_b, L1_attn_qn_scale, L1_attn_qn_bias, L1_attn_kn_scale, L1_attn_kn_bias, L1_attn_ttt_gate, L1_attn_ttt_val, L1_attn_ttt_proj, L1_attn_proj_w, L1_attn_proj_b, L1_ffn_ln_gamma, L1_ffn_ln_beta, L1_ffn_router_w, L1_ffn_gate_up_w, L1_ffn_down_w, L1_ffn_shared_gate_up_w, L1_ffn_shared_down_w):

    def _L0_attn_ref(x, Wq, bq, Wk, bk, Wv, bv, Wo, bo, phase, threshold, temperature):
        import jax, jax.numpy as jnp
        import numpy as np
        import math
        NUM_HEADS = 16
        TPMS_WEIGHT = 0.3
        TWO_PI = 2.0 * math.pi

        def _tpms_mask(L, phase, threshold, temperature):
            pos = jnp.arange(L, dtype=jnp.float32) / L * TWO_PI
            pq = pos[None, :, None] + phase[:, 0][:, None, None]
            pk = pos[None, None, :] + phase[:, 1][:, None, None]
            pz = (pos[None, :, None] + pos[None, None, :]) * 0.5 + phase[:, 2][:, None, None]
            t = jax.lax.stop_gradient(threshold)
            val = jnp.sin(pq) * jnp.cos(pk) + jnp.sin(pk) * jnp.cos(pz) + jnp.sin(pz) * jnp.cos(pq) - t
            return jax.nn.sigmoid(val / (temperature + 1e-06))
        B, L, H = x.shape
        nh = NUM_HEADS
        hd = H // nh
        scale = math.sqrt(hd)
        Q = (x @ Wq + bq).reshape(B, L, nh, hd).transpose(0, 2, 1, 3)
        K = (x @ Wk + bk).reshape(B, L, nh, hd).transpose(0, 2, 1, 3)
        V = (x @ Wv + bv).reshape(B, L, nh, hd).transpose(0, 2, 1, 3)
        scores = jnp.einsum('bhqd,bhkd->bhqk', Q, K) / scale
        mask = _tpms_mask(L, phase, threshold, temperature)
        scores = scores + TPMS_WEIGHT * jnp.log(mask + 1e-06)[None]
        attn = jax.nn.softmax(scores, axis=-1)
        out = jnp.einsum('bhqk,bhkd->bhqd', attn, V)
        out = out.transpose(0, 2, 1, 3).reshape(B, L, H)
        return out @ Wo + bo

    def _L0_ffn_ref(x, wqkv, q_scale, k_scale, wo, ln_g, ln_b, w1, b1, w2, b2):
        import jax, jax.numpy as jnp
        import numpy as np
        DIM = 128
        DEPTH = 2
        HEADS = 8
        DIM_HEAD = 64
        WINDOW = 64
        INNER = HEADS * DIM_HEAD
        HID = int(DIM * 4 * 2 / 3)
        B, N = (2, 1024)
        QK_SCALE = 8.0

        def shift_token(t):
            t1, t2 = jnp.split(t, 2, axis=-1)
            t2 = jnp.pad(t2, ((0, 0), (1, 0), (0, 0)))[:, :-1]
            return jnp.concatenate([t1, t2], axis=-1)

        def l2norm(t):
            return t / jnp.clip(jnp.linalg.norm(t, axis=-1, keepdims=True), 1e-12)

        def rotate_half(x):
            x1, x2 = jnp.split(x, 2, axis=-1)
            return jnp.concatenate([-x2, x1], axis=-1)

        def rotary_xpos(q, k):
            n = q.shape[-2]
            half_idx = jnp.arange(0, DIM_HEAD, 2, dtype=jnp.float32)
            inv_freq = 1.0 / 10000.0 ** (half_idx / DIM_HEAD)
            t = jnp.arange(n, dtype=jnp.float32)
            freqs = t[:, None] * inv_freq[None, :]
            freqs = jnp.concatenate([freqs, freqs], axis=-1)
            base = (half_idx + 0.4 * DIM_HEAD) / (1.4 * DIM_HEAD)
            power = (t - n // 2) / float(WINDOW // 2)
            scale = base[None, :] ** power[:, None]
            scale = jnp.concatenate([scale, scale], axis=-1)
            cos, sin = (jnp.cos(freqs), jnp.sin(freqs))
            q = q * cos * scale + rotate_half(q) * sin * scale
            k = k * cos / scale + rotate_half(k) * sin / scale
            return (q, k)

        def local_attention(q, k, v):
            b, h, n, d = q.shape
            w = n // WINDOW
            bq = q.reshape(b, h, w, WINDOW, d) * QK_SCALE
            bk = k.reshape(b, h, w, WINDOW, d)
            bv = v.reshape(b, h, w, WINDOW, d)

            def look_around(t):
                p = jnp.pad(t, ((0, 0), (0, 0), (1, 0), (0, 0), (0, 0)))
                return jnp.concatenate([p[:, :, :w], p[:, :, 1:]], axis=3)
            bk, bv = (look_around(bk), look_around(bv))
            bt = jnp.arange(n).reshape(w, WINDOW)
            btp = jnp.pad(bt, ((1, 0), (0, 0)), constant_values=-1)
            btk = jnp.concatenate([btp[:w], btp[1:]], axis=1)
            sim = jnp.einsum('bhwid,bhwjd->bhwij', bq, bk)
            i = bt[:, :, None]
            j = btk[:, None, :]
            mask = (i < j) | (i > j + WINDOW) | (j == -1)
            sim = jnp.where(mask, -jnp.finfo(sim.dtype).max, sim)
            attn = jax.nn.softmax(sim, axis=-1)
            out = jnp.einsum('bhwij,bhwjd->bhwid', attn, bv)
            return out.reshape(b, h, n, d)

        def _layer(x, wqkv, qs, ksc, wo, lg, lb, w1, b1, w2, b2):
            b, n, _ = x.shape
            h = shift_token(x)
            qkv = h @ wqkv
            q, k, v = jnp.split(qkv, 3, axis=-1)
            to_heads = lambda t: t.reshape(b, n, HEADS, DIM_HEAD).transpose(0, 2, 1, 3)
            q, k, v = (to_heads(q), to_heads(k), to_heads(v))
            q = l2norm(q) * qs
            k = l2norm(k) * ksc
            q, k = rotary_xpos(q, k)
            o = local_attention(q, k, v)
            o = o.transpose(0, 2, 1, 3).reshape(b, n, INNER)
            x = x + o @ wo
            h = shift_token(x)
            mu = h.mean(-1, keepdims=True)
            var = h.var(-1, keepdims=True)
            h = (h - mu) / jnp.sqrt(var + 1e-05) * lg + lb
            h = h @ w1 + b1
            a, g = jnp.split(h, 2, axis=-1)
            h = a * jax.nn.gelu(g, approximate=False)
            x = x + h @ w2 + b2
            return x
        for l in range(DEPTH):
            x = _layer(x, wqkv[l], q_scale[l], k_scale[l], wo[l], ln_g[l], ln_b[l], w1[l], b1[l], w2[l], b2[l])
        return x

    def _L1_attn_ref(x, qkv_w, qkv_b, qn_scale, qn_bias, kn_scale, kn_bias, ttt_gate, ttt_val, ttt_proj, proj_w, proj_b):
        import jax, jax.numpy as jnp
        import numpy as np
        DIM = 128
        HEADS = 16
        HD = DIM // HEADS
        HID = 4 * DIM
        TPF = 1374
        LR = 0.1
        NS_ITERS = 5
        TTT_STEPS = 2
        B, S = (2, 4)
        SN = S * TPF

        def _newton_schulz(G, iters=NS_ITERS):
            a, b, c = (3.4445, -4.775, 2.0315)
            X = G / (jnp.linalg.norm(G) + 1e-07)
            transposed = G.shape[0] > G.shape[1]
            if transposed:
                X = X.T
            for _ in range(iters):
                A = X @ X.T
                X = a * X + (b * A + c * (A @ A)) @ X
            return X.T if transposed else X

        def _muon_update(p, g):
            return p - LR * _newton_schulz(g)
        Bx, SNx, _ = x.shape
        qkv = x @ qkv_w + qkv_b
        q, k, v = jnp.split(qkv, 3, axis=-1)
        q = q.reshape(Bx, SNx, HEADS, HD)
        k = k.reshape(Bx, SNx, HEADS, HD)
        q = q / (jnp.linalg.norm(q, axis=-1, keepdims=True) + 1e-06) * qn_scale + qn_bias
        k = k / (jnp.linalg.norm(k, axis=-1, keepdims=True) + 1e-06) * kn_scale + kn_bias
        q_ttt = q.reshape(-1, DIM)
        k_ttt = k.reshape(-1, DIM)
        v_ttt = v.reshape(-1, DIM)
        theta = {'gate': ttt_gate, 'val': ttt_val, 'proj': ttt_proj}

        def loss_fn(p):
            h = jax.nn.swish(k_ttt @ p['gate']) * (k_ttt @ p['val'])
            pred = h @ p['proj']
            return jnp.mean((pred - v_ttt) ** 2)
        for _ in range(TTT_STEPS):
            grads = jax.grad(loss_fn)(theta)
            theta = {kk: _muon_update(theta[kk], grads[kk]) for kk in theta}
        h_q = jax.nn.swish(q_ttt @ theta['gate']) * (q_ttt @ theta['val'])
        o = h_q @ theta['proj'] @ proj_w + proj_b
        return o.reshape(Bx, SNx, DIM)

    def _L1_ffn_ref(x, ln_gamma, ln_beta, router_w, gate_up_w, down_w, shared_gate_up_w, shared_down_w):
        import jax, jax.numpy as jnp
        import numpy as np
        B, S, D, F, E, K = (4, 256, 128, 512, 8, 2)
        FS = 128
        LN_EPS = 1e-05

        def _swiglu(x, gu_w, dn_w):
            gate, up = jnp.split(x @ gu_w, 2, axis=-1)
            gate = jnp.clip(gate, -10.0, 10.0)
            return jax.nn.silu(gate) * up @ dn_w
        b, s, d = x.shape
        xf = x.reshape(-1, d)
        mu = jnp.mean(xf, axis=-1, keepdims=True)
        var = jnp.var(xf, axis=-1, keepdims=True)
        xn = (xf - mu) * jax.lax.rsqrt(var + LN_EPS) * ln_gamma + ln_beta
        logits = xn @ router_w
        probs = jax.nn.softmax(logits, axis=-1)
        topv, topi = jax.lax.top_k(probs, K)
        topv = topv / jnp.sum(topv, axis=-1, keepdims=True)
        comb = jnp.sum(jax.nn.one_hot(topi, E, dtype=xn.dtype) * topv[..., None], axis=1)
        out = jnp.zeros_like(xf)
        for e in range(E):
            out = out + comb[:, e:e + 1] * _swiglu(xn, gate_up_w[e], down_w[e])
        out = out + _swiglu(xn, shared_gate_up_w, shared_down_w)
        return out.reshape(b, s, d)
    x = L0_attn_x
    x = x + 0.5 * _L0_ffn_ref(_layernorm(x, axis=-1), L0_ffn_wqkv, L0_ffn_q_scale, L0_ffn_k_scale, L0_ffn_wo, L0_ffn_ln_g, L0_ffn_ln_b, L0_ffn_w1, L0_ffn_b1, L0_ffn_w2, L0_ffn_b2)
    x = x + _L0_attn_ref(_layernorm(x, axis=-1), L0_attn_Wq, L0_attn_bq, L0_attn_Wk, L0_attn_bk, L0_attn_Wv, L0_attn_bv, L0_attn_Wo, L0_attn_bo, L0_attn_phase, L0_attn_threshold, L0_attn_temperature)
    x = x + 0.5 * _L0_ffn_ref(_layernorm(x, axis=-1), L0_ffn_wqkv, L0_ffn_q_scale, L0_ffn_k_scale, L0_ffn_wo, L0_ffn_ln_g, L0_ffn_ln_b, L0_ffn_w1, L0_ffn_b1, L0_ffn_w2, L0_ffn_b2)
    x = x + 0.5 * _L1_ffn_ref(_layernorm(x, axis=-1), L1_ffn_ln_gamma, L1_ffn_ln_beta, L1_ffn_router_w, L1_ffn_gate_up_w, L1_ffn_down_w, L1_ffn_shared_gate_up_w, L1_ffn_shared_down_w)
    x = x + _L1_attn_ref(_layernorm(x, axis=-1), L1_attn_qkv_w, L1_attn_qkv_b, L1_attn_qn_scale, L1_attn_qn_bias, L1_attn_kn_scale, L1_attn_kn_bias, L1_attn_ttt_gate, L1_attn_ttt_val, L1_attn_ttt_proj, L1_attn_proj_w, L1_attn_proj_b)
    x = x + 0.5 * _L1_ffn_ref(_layernorm(x, axis=-1), L1_ffn_ln_gamma, L1_ffn_ln_beta, L1_ffn_router_w, L1_ffn_gate_up_w, L1_ffn_down_w, L1_ffn_shared_gate_up_w, L1_ffn_shared_down_w)
    return x

_drawn_inputs = setup_inputs


def setup_inputs(seed=0):
    import zlib

    import numpy as np

    out = dict(_drawn_inputs(seed))
    spreads = {'L0_attn_bq': (0.0, 0.8),
     'L0_attn_bk': (0.0, 2.0),
     'L0_attn_bv': (0.0, 0.568),
     'L0_attn_bo': (0.0, 0.1),
     'L0_ffn_q_scale': (1.0, 0.6),
     'L0_ffn_k_scale': (1.0, 0.6),
     'L0_ffn_ln_g': (1.0, 0.6),
     'L0_ffn_ln_b': (0.0, 0.8),
     'L0_ffn_b1': (0.0, 0.8),
     'L0_ffn_b2': (0.0, 0.1),
     'L1_attn_qkv_b': (0.0, 0.8),
     'L1_attn_qn_scale': (1.0, 0.6),
     'L1_attn_qn_bias': (0.0, 2.0),
     'L1_attn_kn_scale': (1.0, 0.6),
     'L1_attn_kn_bias': (0.0, 2.0),
     'L1_attn_proj_b': (0.0, 0.313),
     'L1_ffn_ln_gamma': (1.0, 0.6),
     'L1_ffn_ln_beta': (0.0, 0.8)}
    factors = {'L0_attn_Wq': 8.0,
     'L0_attn_Wk': 8.0,
     'L0_attn_Wv': 8.0,
     'L0_attn_Wo': 4.349,
     'L0_attn_phase': 8.0,
     'L0_ffn_wqkv': 3.176,
     'L0_ffn_wo': 3.181,
     'L0_ffn_w1': 5.305,
     'L0_ffn_w2': 5.223,
     'L1_ffn_router_w': 8.0,
     'L1_ffn_gate_up_w': 8.0,
     'L1_ffn_down_w': 8.0,
     'L1_ffn_shared_gate_up_w': 8.0,
     'L1_ffn_shared_down_w': 8.0}
    for name, (base, spread) in spreads.items():
        noise = np.random.default_rng([zlib.crc32(name.encode()), seed]).standard_normal(out[name].shape)
        drawn = base * np.exp(spread * noise) if base else spread * noise
        out[name] = jnp.asarray(drawn.astype(out[name].dtype))
    for name, factor in factors.items():
        out[name] = (out[name] * factor).astype(out[name].dtype)
    return out
```

```python
import numpy as np
import concourse.bass as bass
from concourse import mybir
from contextlib import ExitStack

F32 = mybir.dt.float32
BF16 = mybir.dt.bfloat16
U32 = mybir.dt.uint32
I32 = mybir.dt.int32
ALU = mybir.AluOpType
ACT = mybir.ActivationFunctionType
AX = mybir.AxisListType

B, L, D = 4, 512, 128
P = 128
TPB = L // P
LN_EPS = 1e-5

DEPTH, HEADS, DH, WINDOW = 2, 8, 64, 64
INNER = HEADS * DH
QK_SCALE = 8.0
HID = 341
HCH = [(0, 128), (128, 128), (256, HID - 256)]
NCH = INNER // P
UNITS = 2 * TPB

NH, HD = 16, 8
SPLIT_Q = (0, 0, 1, 1, 0, 2)
SPLIT_K = (0, 1, 0, 1, 2, 0)
KS = HD * len(SPLIT_Q)
A_SCALE = float(1.0 / np.sqrt(HD))
MASK_CLAMP = 40.0
MF = 6

E, F, FS = 8, 512, 128
FCH = F // P

TH = 4 * D
LR, NS_ITERS, TTT_STEPS = 0.1, 5, 2
NS_A, NS_B, NS_C = 3.4445, -4.775, 2.0315
GRAD_SCALE = 2.0 / (B * L * D)

LS = 36
LN2 = float(np.log(2.0))

C_ID, C_ONES, C_BLK64, C_BLK8, C_MASK, C_IOTA, C_SEL = 0, 128, 256, 384, 512, 768, 800
C_N = C_SEL + E * 128


def shape_constants():
    c = np.zeros((P, C_N), np.float32)
    r = np.arange(P)
    c[:, C_ID:C_ID + P] = np.eye(P)
    c[:, C_ONES:C_ONES + P] = 1.0
    c[:, C_BLK64:C_BLK64 + P] = (r[:, None] // DH == r[None] // DH)
    c[:, C_BLK8:C_BLK8 + P] = (r[:, None] // HD == r[None] // HD)
    i, j = r[:, None] % WINDOW, r[None]
    ok = (j >= i) & (j <= i + WINDOW)
    first = ok & ((r[:, None] >= WINDOW) | (j >= WINDOW))
    c[:, C_MASK:C_MASK + P] = np.where(first, 0.0, -1e30)
    c[:, C_MASK + P:C_MASK + 2 * P] = np.where(ok, 0.0, -1e30)
    c[:, C_IOTA:C_IOTA + TPB * E] = np.tile(np.arange(E), TPB)
    for e in range(E):
        c[[e, 32 + e, 64 + e], C_SEL + e * P:C_SEL + (e + 1) * P] = 1.0
    return c


def rotary_tables():
    half = np.arange(0, DH, 2, dtype=np.float32)
    inv = (np.float32(1.0) / np.float32(10000.0) ** (half / np.float32(DH))).astype(np.float32)
    t = np.arange(L, dtype=np.float32)
    fr = (t[:, None] * inv[None]).astype(np.float32).astype(np.float64)
    base = (half + np.float32(0.4 * DH)) / np.float32(1.4 * DH)
    power = (t - L // 2) / np.float32(WINDOW // 2)
    sc = base[None].astype(np.float64) ** power[:, None].astype(np.float64)
    two = lambda a: np.concatenate([a, a], 1).T
    cos, sin, sc = two(np.cos(fr)), two(np.sin(fr)), two(sc)
    sign = np.where(np.arange(DH) < DH // 2, -1.0, 1.0)[:, None]
    tabs = [cos * sc * QK_SCALE, sign * sin * sc * QK_SCALE, cos / sc, sign * sin / sc]
    return np.stack([np.tile(a, (2, 1)) for a in tabs], 1).astype(np.float32)


def position_tables():
    pos = (np.arange(L, dtype=np.float32) / np.float32(L) * np.float32(2 * np.pi)).astype(np.float64)
    t = np.stack([np.sin(pos), np.cos(pos), np.sin(pos / 2), np.cos(pos / 2)])
    return np.tile(t[None], (NH, 1, 1)).astype(np.float32)


START = 1


def at(n, per, k=0):
    return n * per + k


def reuse(n, per, k, depth):
    return at(n, per, k - depth + 1 if k >= depth else 0)


def build(nc, I, out, stop=None):
    ctx = ExitStack()
    with ctx:
        sems = {}

        def s(name):
            if name not in sems:
                sems[name] = ctx.enter_context(nc.semaphore(name))
            return sems[name]

        def sb(name, shape, dt=F32):
            return ctx.enter_context(nc.sbuf_tensor(name, shape, dt))

        PS = ctx.enter_context(nc.psum_tensor("PS", [P, 8, 512], F32))
        q_dram = nc.dram_tensor("q_split", (3, D, B, L), BF16).ap()
        k_dram = nc.dram_tensor("k_split", (3, D, B, L), BF16).ap()
        mq_dram = nc.dram_tensor("mask_q", (NH, MF, L), F32).ap()
        mk_dram = nc.dram_tensor("mask_k", (NH, MF, L), F32).ap()
        o_dram = nc.dram_tensor("heads_out", (2, D, B, L), F32).ap()

        xT = sb("xT", [P, B, L])
        con = sb("con", [P, C_N])
        ident, ones = con[:, C_ID:C_ID + P], con[:, C_ONES:C_ONES + P]
        blk64, blk8 = con[:, C_BLK64:C_BLK64 + P], con[:, C_BLK8:C_BLK8 + P]
        mean_w = sb("mean_w", [P, P])
        ident_b = sb("ident_b", [P, P], BF16)
        mask_b = sb("mask_b", [P, 2, 4, P], BF16)
        sel_b = sb("sel_b", [P, E, P], BF16)
        col = sb("col", [P, 8])
        c_eps, c_tiny, c_norm, c_1e6, c_one, c_zero, c_neg = (col[:, i:i + 1] for i in range(7))
        fcol = sb("fcol", [P, DEPTH, 16])
        aw = sb("aw", [P, 4, D])
        acol = sb("acol", [P, 8])
        bv_row = sb("bv_row", [P, D])
        sgu = sb("sgu", [P, 2 * FS])
        sdn = sb("sdn", [P, D])
        rw = sb("rw", [P, E])
        mcol = sb("mcol", [P, 2])
        tqkv = sb("tqkv", [P, 3 * D])
        tcol = sb("tcol", [P, 8])
        th_g = sb("th_g", [P, TH])
        th_v = sb("th_v", [P, TH])
        th_pT = sb("th_pT", [P, TH])
        th_p = sb("th_p", [P, 4, D])
        tpw = sb("tpw", [P, D])
        lnc, lnq, lnr, lnt = (sb(n, [P, L]) for n in ("ln_centered", "ln_square", "ln_rstd", "ln_scaled"))
        big = sb("big", [P, 12400])
        arena = sb("arena", [P, 29800])
        memory, taken = [big], [0]

        def stage_memory(m=arena):
            memory[0], taken[0] = m, 0

        def carve(shape, dt=F32):
            n = int(np.prod(shape))
            w = (n + 1) // 2 if dt == BF16 else n
            a = memory[0][:, taken[0]:taken[0] + w]
            taken[0] += w
            assert taken[0] <= memory[0].shape[1], taken
            if dt != F32:
                a = a.bitcast(dt)
            if len(shape) == 1:
                return a
            names = "abcd"[:len(shape)]
            return a.rearrange(f"p ({' '.join(names)}) -> p {' '.join(names)}", **dict(zip(names, shape)))

        stage_memory(big)
        rot = carve([DEPTH, 4, L])
        wqkv = carve([DEPTH, 3 * INNER])
        wswap = carve([DEPTH, 2 * HEADS, 2, DH // 2])
        wo = carve([DEPTH, NCH, D])
        w1 = carve([DEPTH, 2 * HID])
        w2 = carve([DEPTH, 3, D])
        stage_memory(big)
        gu = carve([E, 2 * F])
        dn = carve([E, FCH, D])

        STAGES = ["load", "ffn0", "attn", "ffn1", "moe0", "ttt", "moe1"]
        if stop:
            STAGES = STAGES[:STAGES.index(stop) + 1]
        first_ln = {"ffn0": 0, "attn": 12, "ffn1": 16, "moe0": 28, "ttt": 32, "moe1": 36}

        def x_of(name):
            return B * STAGES.index(name)

        def plain_wait(eng):
            eng.sem_inc(s("passed"), 1)

        def ln_pe(src, e, mean_bank, var_bank):
            pe = nc.tensor
            pe.matmul(PS[:, mean_bank, :], mean_w[:], src, start=True, stop=True).then_inc(s("ln_sums"), 1)
            pe.wait_ge(s("ln_squared"), START + e + 1)
            pe.matmul(PS[:, var_bank, :], mean_w[:], lnq[:], start=True, stop=True).then_inc(s("ln_sums"), 1)

        def ln_act(e, var_bank):
            act = nc.scalar
            act.wait_ge(s("ln_centred"), START + e + 1)
            act.activation(lnq[:], lnc[:], ACT.Square).then_inc(s("ln_squared"), 1)
            act.wait_ge(s("ln_sums"), START + at(e, 2, 2))
            act.activation(lnr[:], PS[:, var_bank, :], ACT.Ln, bias=c_eps).then_inc(s("ln_rstd_step"), 1)
            act.wait_ge(s("ln_rstd_step"), START + at(e, 2, 1))
            act.activation(lnr[:], lnr[:], ACT.Exp, scale=-0.5).then_inc(s("ln_rstd_step"), 1)

        def ln_dve(src, e, mean_bank, gamma, beta, dst, free=()):
            v = nc.vector
            v.wait_ge(s("ln_sums"), START + at(e, 2, 1))
            v.tensor_tensor(lnc[:], src, PS[:, mean_bank, :], ALU.subtract).then_inc(s("ln_centred"), 1)
            v.wait_ge(s("ln_rstd_step"), START + at(e, 2, 2))
            v.scalar_tensor_tensor(lnt[:], lnc[:], gamma, lnr[:], ALU.mult, ALU.mult).then_inc(s("ln_scaled_done"), 1)
            v.wait_ge(s("ln_scaled_done"), START + e + 1)
            for name, count in free:
                v.wait_ge(s(name), START + count)
            v.tensor_scalar(dst, lnt[:], beta, None, ALU.add).then_inc(s("ln_done"), 1)

        stage_memory()
        y = carve([B, L])
        h_pad = carve([WINDOW + L])
        t_cos, t_sin, t_rot, t_rn, t_sq = (carve([2, L]) for _ in range(5))
        t_ln = carve([2, L])
        qs = carve([NCH, L])
        ks = carve([NCH, WINDOW + L])
        vs = carve([2, TPB, INNER])
        pr = carve([2, 4, P])
        pn = carve([2, 4, P])
        pT = carve([2, 4, P])
        nmax, psum_, pinv = (carve([2, 4]) for _ in range(3))
        oT = carve([NCH, L])
        h2 = carve([L])
        ln2 = carve([L])
        gl = carve([2, L])
        hid = carve([3, L])

        def ffn_counts(f, layer, b):
            N = b + 4 * (2 * f + layer)
            if layer == 0:
                e = b * 2 + (first_ln[f"ffn{f}"])
                return N, e, e + 1
            return N, None, b + (first_ln[f"ffn{f}"] + 8)

        def ffn_pe(pe, f, layer):
            with pe.Fori(0, B) as b:
                N, e_in, e_h2 = ffn_counts(f, layer, b)
                if layer == 0:
                    ln_pe(xT[:, b, :], e_in, 4, 5)
                pe.wait_ge(s("h_ready"), START + at(N, 2, 2))
                pe.wait_ge(s("hid_ready"), START + at(N, 3))
                for c in range(2 * NCH):
                    j = at(N, 2 * NCH, c)
                    if c >= 2:
                        pe.wait_ge(s("rot_products"), START + j - 1)
                        pe.wait_ge(s("qk_squared"), START + j - 1)
                    w = wqkv[:, layer, c * P:(c + 1) * P]
                    pe.matmul(PS[:, c % 2, :], w, h_pad[:, WINDOW:], start=True, stop=True).then_inc(s("proj"), 1)
                    w = wswap[:, layer, 2 * c:2 * c + 2, :, :].rearrange("p a b c -> p (a b c)")
                    pe.matmul(PS[:, 2 + c % 2, :], w, h_pad[:, WINDOW:], start=True, stop=True).then_inc(s("proj"), 1)
                    if c >= 1:
                        head_norm(pe, N, c - 1)
                head_norm(pe, N, 2 * NCH - 1)
                pe.wait_ge(s("y_added"), START + at(N, 1))
                for i in range(2 * TPB):
                    off = WINDOW + (i % TPB) * P if i < TPB else (i % TPB) * P
                    if i >= 2:
                        pe.wait_ge(s("v_act" if i % 2 == 0 else "v_dve"), START + at(N, TPB, i // 2))
                    pe.matmul(PS[:, 6 + i % 2, :], h_pad[:, off:off + P], wqkv[:, layer, 2 * INNER:], start=True,
                              stop=True).then_inc(s("v_proj"), 1)
                pe.wait_ge(s("qk_scaled"), START + at(N, 2 * NCH, 2 * NCH))
                for u in range(UNITS + 2):
                    if u < UNITS:
                        scores(pe, N, u)
                    if 1 <= u <= UNITS:
                        p_transposes(pe, N, u - 1)
                    if u >= 2:
                        values(pe, N, u - 2)
                pe.wait_ge(s("oT_ready"), START + at(N, TPB, TPB))
                pe.wait_ge(s("p_exp"), START + at(N, 4 * UNITS, 4 * UNITS))
                for c in range(NCH):
                    mm = pe.matmul(PS[:, 0, :], wo[:, layer, c, :], oT[:, c, :], start=c == 0, stop=c == NCH - 1)
                mm.then_inc(s("wo_ready"), 1)
                pe.wait_ge(s("h2_ready"), START + at(N, 2, 2))
                ln_pe(h2[:], e_h2, 4, 5)
                pe.wait_ge(s("ln_done"), START + e_h2 + 1)
                for c, (o, n) in enumerate(HCH):
                    if c >= 2:
                        pe.wait_ge(s("hid_ready"), START + at(N, 3, c - 1))
                    pe.matmul(PS[0:n, c % 2, :], w1[:, layer, o:o + n], ln2[:], start=True, stop=True).then_inc(s("ffn_proj"), 1)
                    pe.matmul(PS[0:n, 2 + c % 2, :], w1[:, layer, HID + o:HID + o + n], ln2[:], start=True,
                              stop=True).then_inc(s("ffn_proj"), 1)
                for c, (o, n) in enumerate(HCH):
                    pe.wait_ge(s("hid_ready"), START + at(N, 3, c + 1))
                    mm = pe.matmul(PS[:, 6, :], w2[0:n, layer, c, :], hid[0:n, c, :], start=c == 0, stop=c == 2)
                mm.then_inc(s("ffn_out"), 1)

        def head_norm(pe, N, c):
            j = at(N, 2 * NCH, c)
            pe.wait_ge(s("qk_squared"), START + j + 1)
            if c >= 2:
                pe.wait_ge(s("qk_log"), START + j - 1)
            pe.matmul(PS[:, 4 + c % 2, :], blk64, t_sq[:, c % 2, :], start=True, stop=True).then_inc(s("qk_sums"), 1)

        def scores(pe, N, u):
            t, par = u // 2, u % 2
            if u >= 4:
                pe.wait_ge(s("p_exp"), START + at(N, 4 * UNITS, 4 * (u - 3)))
            bank = PS[:, u % 4, :]
            m = mask_b[:, 0 if t == 0 else 1, :, :].rearrange("p a b -> p (a b)")
            pe.matmul(bank, ident_b[:], m, start=True, stop=False, skip_group_check=True)
            r = slice(DH * par, DH * par + DH)
            for c in range(NCH):
                for w in range(2):
                    a = t * P + w * WINDOW
                    mm = pe.matmul(PS[w * WINDOW:(w + 1) * WINDOW, u % 4, c * P:(c + 1) * P], qs[r, c, a:a + WINDOW],
                                   ks[r, c, a:a + 2 * WINDOW], start=False, stop=True, skip_group_check=True)
            mm.then_inc(s("scores_ready"), 1)

        def p_transposes(pe, N, u):
            pe.wait_ge(s("p_normed"), START + at(N, UNITS, u + 1))
            if u >= 2:
                pe.wait_ge(s("pT_ready"), START + at(N, UNITS, u - 1))
            for c in range(4):
                tr = pe.transpose(PS[:, 4 + u % 2, c * P:(c + 1) * P], pn[:, u % 2, c, :], ident)
            tr.then_inc(s("pT_done"), 1)

        def values(pe, N, u):
            t, par = u // 2, u % 2
            pe.wait_ge(s("pT_ready"), START + at(N, UNITS, u + 1))
            if u == 0:
                pe.wait_ge(s("v_act"), START + at(N, TPB, TPB))
                pe.wait_ge(s("v_dve"), START + at(N, TPB, TPB))
            if par == 0 and t >= 2:
                pe.wait_ge(s("oT_ready"), START + at(N, TPB, t - 1))
            for c in range(NCH):
                for w in range(2):
                    h = 2 * c + par
                    mm = pe.matmul(PS[DH * par:DH * par + DH, 6 + t % 2, c * P + w * WINDOW:c * P + (w + 1) * WINDOW],
                                   vs[:, 1 - w, t, h * DH:(h + 1) * DH], pT[:, u % 2, c, w * WINDOW:(w + 1) * WINDOW],
                                   start=True, stop=True)
            mm.then_inc(s("pv_done"), 1)

        def ffn_act(act, f, layer):
            with act.Fori(0, B) as b:
                N, e_in, e_h2 = ffn_counts(f, layer, b)
                act.preload_act_table_set("natural_log_exp_and_others")
                if layer == 0:
                    ln_act(e_in, 5)
                    act.wait_ge(s("ln_done"), START + e_in + 1)
                else:
                    act.wait_ge(s("y_added"), START + at(N, 1, -3))
                act.wait_ge(s("v_proj"), START + at(N, 2 * TPB))
                plain_wait(act)
                act.activation(h_pad[64:128, WINDOW + 1:WINDOW + L], y[64:128, b, 0:L - 1], ACT.Copy).then_inc(s("h_ready"), 1)
                for c in range(2 * NCH):
                    j = at(N, 2 * NCH, c)
                    act.wait_ge(s("rot_cos"), START + j + 1)
                    if c >= 2:
                        act.wait_ge(s("qk_sums"), START + j - 1)
                    act.activation(t_sq[:, c % 2, :], PS[:, c % 2, :], ACT.Square).then_inc(s("qk_squared"), 1)
                    if c >= 1:
                        head_rnorm(act, N, c - 1)
                head_rnorm(act, N, 2 * NCH - 1)
                for i in range(0, 2 * TPB, 2):
                    act.wait_ge(s("v_proj"), START + at(N, 2 * TPB, i + 1))
                    if i == 0:
                        act.wait_ge(s("pv_done"), START + at(N, UNITS))
                    act.activation(vs[:, i // TPB, i % TPB, :], PS[:, 6, :], ACT.Copy).then_inc(s("v_act"), 1)
                for u in range(UNITS + 3):
                    if u < UNITS:
                        act.wait_ge(s("nmax_ready"), START + at(N, UNITS, u + 1))
                        act.wait_ge(s("p_normed"), START + reuse(N, UNITS, u, 2))
                        for c in range(4):
                            act.activation(pr[:, u % 2, c, :], PS[:, u % 4, c * P:(c + 1) * P], ACT.Exp,
                                           bias=nmax[:, u % 2, c:c + 1],
                                           accum_out=psum_[:, u % 2, c:c + 1]).then_inc(s("p_exp"), 1)
                    if u >= 4 and u % 2 == 0:
                        heads_out(act, N, (u - 4) // 2)
                act.wait_ge(s("wo_added"), START + at(N, 1, 1))
                plain_wait(act)
                act.activation(h2[64:128, 1:L], y[64:128, b, 0:L - 1], ACT.Copy).then_inc(s("h2_ready"), 1)
                ln_act(e_h2, 5)
                for c, (o, n) in enumerate(HCH):
                    act.wait_ge(s("ffn_proj"), START + at(N, 6, 2 * c + 2))
                    act.wait_ge(s("hid_ready"), START + reuse(N, 3, c, 2))
                    act.activation(gl[0:n, c % 2, :], PS[0:n, 2 + c % 2, :], ACT.Gelu,
                                   bias=fcol[0:n, layer, 10 + c:11 + c]).then_inc(s("gelu_ready"), 1)

        def head_rnorm(act, N, c):
            j = at(N, 2 * NCH, c)
            act.wait_ge(s("qk_sums"), START + j + 1)
            act.wait_ge(s("qk_rnorm"), START + reuse(N, 2 * NCH, c, 2))
            act.activation(t_ln[:, c % 2, :], PS[:, 4 + c % 2, :], ACT.Ln, bias=c_tiny, scale=2.0 ** LS).then_inc(s("qk_log"), 1)
            act.wait_ge(s("qk_log"), START + j + 1)
            act.wait_ge(s("qk_scaled"), START + reuse(N, 2 * NCH, c, 2))
            act.activation(t_rn[:, c % 2, :], t_ln[:, c % 2, :], ACT.Exp, bias=c_norm, scale=-0.5).then_inc(s("qk_rnorm"), 1)

        def heads_out(act, N, t):
            act.wait_ge(s("pv_done"), START + at(N, UNITS, 2 * t + 2))
            if t == 0:
                act.wait_ge(s("wo_ready"), START + at(N, 1))
            act.activation(oT[:, :, t * P:(t + 1) * P], PS[:, 6 + t % 2, :].rearrange("p (a b) -> p a b", a=NCH),
                           ACT.Copy).then_inc(s("oT_ready"), 1)

        def ffn_dve(v, f, layer):
            with v.Fori(0, B) as b:
                N, e_in, e_h2 = ffn_counts(f, layer, b)
                if layer == 0:
                    ln_dve(xT[:, b, :], e_in, 4, c_one, c_zero, y[:, b, :])
                    v.wait_ge(s("ln_done"), START + e_in + 1)
                else:
                    v.wait_ge(s("y_added"), START + at(N, 1, -3))
                v.wait_ge(s("v_proj"), START + at(N, 2 * TPB))
                plain_wait(v)
                v.tensor_copy(h_pad[0:64, WINDOW:], y[0:64, b, :]).then_inc(s("h_ready"), 1)
                for c in range(2 * NCH):
                    tab = 0 if c < NCH else 2
                    v.wait_ge(s("qk_rotated"), START + reuse(N, 2 * NCH, c, 2))
                    v.wait_ge(s("proj"), START + at(N, 4 * NCH, 2 * c + 1))
                    v.tensor_tensor(t_cos[:, c % 2, :], PS[:, c % 2, :], rot[:, layer, tab, :], ALU.mult).then_inc(s("rot_cos"), 1)
                    v.wait_ge(s("proj"), START + at(N, 4 * NCH, 2 * c + 2))
                    v.tensor_tensor(t_sin[:, c % 2, :], PS[:, 2 + c % 2, :], rot[:, layer, tab + 1, :],
                                    ALU.mult).then_inc(s("rot_products"), 1)
                    if c >= 1:
                        normed_head(v, N, c - 1)
                normed_head(v, N, 2 * NCH - 1)
                v.wait_ge(s("pv_done"), START + at(N, UNITS))
                for i in range(1, 2 * TPB, 2):
                    v.wait_ge(s("v_proj"), START + at(N, 2 * TPB, i + 1))
                    v.tensor_copy(vs[:, i // TPB, i % TPB, :], PS[:, 7, :]).then_inc(s("v_dve"), 1)
                for u in range(UNITS + 2):
                    if u < UNITS:
                        v.wait_ge(s("scores_ready"), START + at(N, UNITS, u + 1))
                        v.wait_ge(s("p_exp"), START + at(N, 4 * UNITS, 4 * (u - 1) if u >= 2 else 0))
                        v.tensor_reduce(nmax[:, u % 2, :], PS[:, u % 4, :].rearrange("p (a b) -> p a b", a=4), AX.X,
                                        ALU.max, negate=True).then_inc(s("nmax_ready"), 1)
                    if 1 <= u <= UNITS:
                        w = u - 1
                        v.wait_ge(s("p_exp"), START + at(N, 4 * UNITS, 4 * w + 4))
                        v.wait_ge(s("p_normed"), START + reuse(N, UNITS, w, 2))
                        v.reciprocal(pinv[:, w % 2, :], psum_[:, w % 2, :]).then_inc(s("pinv_ready"), 1)
                    if u >= 2:
                        w = u - 2
                        v.wait_ge(s("pT_done"), START + at(N, UNITS, w + 1))
                        v.wait_ge(s("pv_done"), START + reuse(N, UNITS, w, 2))
                        v.tensor_copy(pT[:, w % 2, :, :].rearrange("p a b -> p (a b)"), PS[:, 4 + w % 2, :]).then_inc(s("pT_ready"), 1)
                v.wait_ge(s("wo_ready"), START + at(N, 1, 1))
                v.tensor_tensor(y[:, b, :], y[:, b, :], PS[:, 0, :], ALU.add).then_inc(s("wo_added"), 1)
                v.wait_ge(s("wo_added"), START + at(N, 1, 1))
                plain_wait(v)
                v.tensor_copy(h2[0:64], y[0:64, b, :]).then_inc(s("h2_ready"), 1)
                v.wait_ge(s("h2_ready"), START + at(N, 2, 2))
                ln_dve(h2, e_h2, 4, fcol[:, layer, 4:5], fcol[:, layer, 5:6], ln2)
                for c, (o, n) in enumerate(HCH):
                    v.wait_ge(s("gelu_ready"), START + at(N, 3, c + 1))
                    v.scalar_tensor_tensor(hid[0:n, c, :], PS[0:n, c % 2, :], fcol[0:n, layer, 7 + c:8 + c],
                                           gl[0:n, c % 2, :], ALU.add, ALU.mult).then_inc(s("hid_ready"), 1)
                v.wait_ge(s("ffn_out"), START + at(N, 1, 1))
                v.scalar_tensor_tensor(y[:, b, :], PS[:, 6, :], fcol[:, layer, 6:7], y[:, b, :], ALU.add,
                                       ALU.add).then_inc(s("y_added"), 1)
                if layer == DEPTH - 1:
                    v.wait_ge(s("y_added"), START + at(N, 1, 1))
                    v.scalar_tensor_tensor(xT[:, b, :], y[:, b, :], 0.5, xT[:, b, :], ALU.mult, ALU.add).then_inc(s("x_ready"), 1)

        def normed_head(v, N, c):
            j = at(N, 2 * NCH, c)
            v.wait_ge(s("qk_rotated"), START + j + 1)
            v.wait_ge(s("qk_rnorm"), START + j + 1)
            if c == 0:
                v.wait_ge(s("scores_ready"), START + at(N, UNITS))
            dst = qs[:, c, :] if c < NCH else ks[:, c - NCH, WINDOW:]
            v.scalar_tensor_tensor(dst, t_rn[:, c % 2, :], 1e12, t_rot[:, c % 2, :], ALU.min,
                                   ALU.mult).then_inc(s("qk_scaled"), 1)

        def ffn_pool(g, f, layer):
            with g.Fori(0, B) as b:
                N = b + 4 * (2 * f + layer)
                for c in range(2 * NCH):
                    g.wait_ge(s("rot_cos"), START + at(N, 2 * NCH, c + 1))
                    g.wait_ge(s("rot_products"), START + at(N, 2 * NCH, c + 1))
                    g.wait_ge(s("qk_scaled"), START + reuse(N, 2 * NCH, c, 2))
                    g.tensor_tensor(t_rot[:, c % 2, :], t_cos[:, c % 2, :], t_sin[:, c % 2, :], ALU.add).then_inc(s("qk_rotated"), 1)
                for u in range(UNITS):
                    g.wait_ge(s("pinv_ready"), START + at(N, UNITS, u + 1))
                    g.wait_ge(s("pT_done"), START + reuse(N, UNITS, u, 2))
                    g.tensor_tensor(pn[:, u % 2, :, :], pr[:, u % 2, :, :],
                                    pinv[:, u % 2, :].unsqueeze(2).broadcast_to([P, 4, P]), ALU.mult).then_inc(s("p_normed"), 1)


        def ffn_zero_pads(g, f):
            g.wait_ge(s("x_ready"), START + x_of(f"ffn{f}"))
            if f == 0:
                g.wait_ge(s("mask_stored"), START + 32)
            g.memset(h_pad[:, 0:WINDOW + 1], 0.0).then_inc(s("pads_zero"), 1)
            g.memset(ks[:, :, 0:WINDOW], 0.0).then_inc(s("pads_zero"), 1)
            g.memset(h2[:, 0:1], 0.0).then_inc(s("pads_zero"), 1)

        stage_memory()
        pos = carve([4, L])
        m_q = carve([MF, L])
        m_k = carve([MF, L])
        m_t = carve([6, L])
        ang, turns, ang_f, sc = (carve([8]) for _ in range(4))
        turns_i = turns.bitcast(I32)
        phase = carve([8])

        def load_sync(sp):
            for name, dst in (("xT", xT[:]), ("con", con[:]), ("fcol", fcol[:]), ("wqkv", wqkv), ("wswap", wswap)):
                sp.dma_start(dst, I[name]).then_inc(s("first_loads"), 16)
            for layer in range(DEPTH):
                sp.dma_start(rot[:, layer, :, :], I["rot"]).then_inc(s("first_loads"), 16)
            sp.dma_start(phase[0:NH, :], I["phase"]).then_inc(s("phase_loaded"), 16)
            sp.dma_start(pos[0:NH, :, :], I["pos"]).then_inc(s("phase_loaded"), 16)
            sp.dma_start(wo, I["wo"]).then_inc(s("ffn_loaded"), 16)
            sp.dma_start(w1, I["w1"]).then_inc(s("ffn_loaded"), 16)
            sp.dma_start(w2, I["w2"]).then_inc(s("ffn_loaded"), 16)
            for name, dst in (("aw", aw), ("acol", acol), ("bv_row", bv_row)):
                sp.dma_start(dst[:], I[name]).then_inc(s("attn_loaded"), 16)
            sp.wait_ge(s("mask_rows"), START + 2)
            sp.dma_start(mq_dram.rearrange("h f n -> h (f n)"), m_q[0:NH].rearrange("p a b -> p (a b)")).then_inc(s("mask_stored"), 16)
            sp.dma_start(mk_dram.rearrange("h f n -> h (f n)"), m_k[0:NH].rearrange("p a b -> p (a b)")).then_inc(s("mask_stored"), 16)
            for name, dst in (("sgu", sgu), ("sdn", sdn), ("rw", rw), ("mcol", mcol)):
                sp.dma_start(dst[:], I[name]).then_inc(s("moe_loaded"), 16)
            for name, dst in (("tqkv", tqkv), ("tcol", tcol), ("th_g", th_g), ("th_v", th_v), ("th_pT", th_pT),
                              ("th_p", th_p), ("tpw", tpw)):
                sp.dma_start(dst[:], I[name]).then_inc(s("ttt_loaded"), 16)

        def load_experts(sp):
            sp.wait_ge(s("x_ready"), START + x_of("moe0"))
            for e in range(E):
                sp.dma_start(gu[:, e, :], I["gu"][:, e, :]).then_inc(s(f"experts{e // 2}_loaded"), 16)
                sp.dma_start(dn[:, e, :, :], I["dn"][:, e, :, :]).then_inc(s(f"experts{e // 2}_loaded"), 16)

        def load_dve(v):
            for i, val in enumerate((LN_EPS, 2.0 ** -60, 0.5 * LS * LN2, 1e-6, 1.0, 0.0, -0.5 * LS * LN2)):
                v.memset(col[:, i:i + 1], val).then_inc(s("columns"), 1)
            v.wait_ge(s("columns"), START + 7)
            v.wait_ge(s("first_loads"), START + 112)
            v.tensor_scalar(mean_w[:], ones, 1.0 / D, None, ALU.mult).then_inc(s("consts"), 1)
            v.tensor_copy(ident_b[:], ident).then_inc(s("consts"), 1)
            m = con[:, C_MASK:C_MASK + 2 * P].rearrange("p (a b) -> p a b", a=2)
            for c in range(4):
                v.tensor_copy(mask_b[:, :, c, :], m).then_inc(s("consts"), 1)
            v.tensor_copy(sel_b[:].rearrange("p a b -> p (a b)"), con[:, C_SEL:]).then_inc(s("consts"), 1)
            v.tensor_copy(col[:, 7:8], c_one).then_inc(s("x_ready"), B)
            for layer in range(DEPTH):
                for i in range(4):
                    v.tensor_scalar(rot[:, layer, i, :], rot[:, layer, i, :], fcol[:, layer, i:i + 1], None,
                                    ALU.mult).then_inc(s("rot_scaled"), 1)
            mask_factors(v)

        def mask_factors(v):
            steps = [0]

            def then(ins):
                steps[0] += 1
                ins.then_inc(s("mask_step"), 1)
                v.wait_ge(s("mask_step"), START + steps[0])

            h = slice(0, NH)
            pi = float(np.pi)
            two_pi_hi = float(np.float32(2 * np.pi))
            two_pi_lo = float(2 * np.pi - two_pi_hi)
            v.wait_ge(s("phase_loaded"), START + 32)
            then(v.tensor_copy(ang[h, 0:3], phase[h, 0:3]))
            then(v.tensor_scalar(ang[h, 3:6], phase[h, 0:3], pi / 2, None, ALU.add))
            then(v.tensor_scalar(ang_f[h, 0:6], ang[h, 0:6], 1.0 / (2 * pi), None, ALU.mult))
            then(v.tensor_copy(turns_i[h, 0:6], ang_f[h, 0:6]))
            then(v.tensor_copy(ang_f[h, 0:6], turns_i[h, 0:6]))
            for part in (two_pi_hi, two_pi_lo):
                then(v.scalar_tensor_tensor(ang[h, 0:6], ang_f[h, 0:6], -part, ang[h, 0:6], ALU.mult, ALU.add))
            for op, bound, turn in ((ALU.is_gt, pi, -two_pi_hi), (ALU.is_lt, -pi, two_pi_hi)):
                then(v.tensor_scalar(ang_f[h, 0:6], ang[h, 0:6], bound, turn, op, ALU.mult))
                then(v.tensor_tensor(ang[h, 0:6], ang[h, 0:6], ang_f[h, 0:6], ALU.add))
            then(v.tensor_scalar(ang[h, 0:6], ang[h, 0:6], 3.1415925, -3.1415925, ALU.min, ALU.max))
            v.tensor_copy(sc[h, 6:7], ang[h, 0:1]).then_inc(s("angles"), 1)
            v.wait_ge(s("sines"), START + 1)
            s0, s1, s2, c0, c1, c2 = (sc[h, i:i + 1] for i in range(6))
            sa, ca, sh, ch = (pos[h, i, :] for i in range(4))

            def angle_sum(dst, t, a, x, b, y, op):
                then(v.tensor_scalar(t, a, x, None, ALU.mult))
                then(v.scalar_tensor_tensor(dst, b, y, t, ALU.mult, op))

            t = m_t[h, 5, :]
            sin_q, cos_q, sin_z, cos_z, sin_k = m_q[h, 0, :], m_t[h, 1, :], m_t[h, 2, :], m_q[h, 1, :], m_t[h, 4, :]
            angle_sum(sin_q, t, ca, s0, sa, c0, ALU.add)
            angle_sum(cos_q, t, sa, s0, ca, c0, ALU.subtract)
            angle_sum(cos_z, t, sh, s2, ch, c2, ALU.subtract)
            angle_sum(sin_z, t, ch, s2, sh, c2, ALU.add)
            angle_sum(m_k[h, 0, :], t, sa, s1, ca, c1, ALU.subtract)
            angle_sum(sin_k, t, ca, s1, sa, c1, ALU.add)
            then(v.tensor_scalar(m_q[h, 2, :], sin_z, -1.0, None, ALU.mult))
            then(v.tensor_tensor(m_q[h, 3, :], cos_q, sin_z, ALU.mult))
            then(v.tensor_tensor(m_q[h, 4, :], cos_q, cos_z, ALU.mult))
            then(v.tensor_scalar(m_q[h, 5, :], sa, 0.0, phase[h, 3:4], ALU.mult, ALU.subtract))
            then(v.tensor_tensor(m_k[h, 1, :], sin_k, ch, ALU.mult))
            then(v.tensor_tensor(m_k[h, 2, :], sin_k, sh, ALU.mult))
            then(v.tensor_copy(m_k[h, 3, :], ch))
            then(v.tensor_copy(m_k[h, 4, :], sh))
            v.memset(m_k[h, 5, :], 1.0).then_inc(s("mask_rows"), 1)
            v.wait_ge(s("attn_loaded"), START + 48)
            then(v.tensor_scalar(acol[:, 4:5], acol[:, 3:4], 1e-6, -1.0, ALU.add, ALU.mult))
            then(v.tensor_scalar(acol[:, 6:7], acol[:, 0:1], A_SCALE, None, ALU.mult))
            v.reciprocal(acol[:, 5:6], acol[:, 4:5]).then_inc(s("mask_rows"), 1)

        def load_act(act):
            act.wait_ge(s("angles"), START + 1)
            act.activation(sc[0:NH, 0:6], ang[0:NH, 0:6], ACT.Sin).then_inc(s("sines"), 1)
            act.wait_ge(s("columns"), START + 7)
            act.wait_ge(s("consts"), START + 7)

        stage_memory()
        xn = carve([L])
        f_qk = carve([2, L])
        rest = carve([2, 2, L])
        parts = carve([2, 3, L], BF16)
        v_all = carve([B * TPB, D])
        v_head = carve([2, B * TPB, 2 * HD])
        q_st = [carve([B, L], BF16) for _ in range(2)]
        k_st = [carve([B, L], BF16) for _ in range(2)]
        mq_st = [carve([L]) for _ in range(2)]
        mk_st = [carve([L]) for _ in range(2)]
        mk = carve([2, TPB, L])
        pp = carve([2, TPB, L])
        ppT = carve([TPB, L])
        a_nmax = carve([2, TPB])
        o_sb = carve([2, L])
        o_all, s_all = pp[:, 0, :, :], pp[:, 1, :, :]
        att = f_qk[:, 0, :]
        inv = f_qk[:, 1, :]

        def attn_proj_pe(pe):
            pe.wait_ge(s("x_ready"), START + x_of("attn"))
            pe.wait_ge(s("attn_loaded"), START + 48)
            with pe.Fori(0, B) as b:
                e = b + first_ln["attn"]
                ln_pe(xT[:, b, :], e, 4, 5)
                pe.wait_ge(s("ln_done"), START + e + 1)
                pe.wait_ge(s("a_biased"), START + at(b, 2))
                for i in range(2):
                    pe.matmul(PS[:, i, :], aw[:, i, :], xn, start=True, stop=True).then_inc(s("a_proj"), 1)
                pe.wait_ge(s("a_values"), START + at(b, 1))
                for t in range(TPB):
                    mm = pe.matmul(PS[:, 2, t * P:(t + 1) * P], xn[:, t * P:(t + 1) * P], aw[:, 2, :], start=True, stop=True)
                mm.then_inc(s("a_vproj"), 1)

        def attn_proj_act(act):
            act.wait_ge(s("x_ready"), START + x_of("attn"))
            with act.Fori(0, B) as b:
                e = b + first_ln["attn"]
                ln_act(e, 5)
                for i in range(2):
                    act.wait_ge(s("a_proj"), START + at(b, 2, i + 1))
                    act.wait_ge(s("a_split"), START + at(b, 10))
                    act.activation(f_qk[:, i, :], PS[:, i, :], ACT.Identity, bias=acol[:, 6:7] if i == 0 else acol[:, 1:2],
                                   scale=A_SCALE if i == 0 else 1.0).then_inc(s("a_biased"), 1)

        def attn_proj_dve(v):
            v.wait_ge(s("x_ready"), START + x_of("attn"))
            with v.Fori(0, B) as b:
                e = b + first_ln["attn"]
                ln_dve(xT[:, b, :], e, 4, c_one, c_zero, xn, free=[("a_vproj", at(b, 1))])
                v.wait_ge(s("a_vproj"), START + at(b, 1, 1))
                v.tensor_tensor(v_all[:, bass.ds(b * TPB, TPB), :], PS[:, 2, :].rearrange("p (a b) -> p a b", a=TPB),
                                bv_row[:].unsqueeze(1).broadcast_to([P, TPB, P]), ALU.add).then_inc(s("a_values"), 1)
                v.wait_ge(s("parts_stored"), START + at(b, 96))
                for st in range(5):
                    for i in range(2):
                        if st == 0:
                            v.wait_ge(s("a_biased"), START + at(b, 2, i + 1))
                        else:
                            v.wait_ge(s("a_split"), START + at(b, 10, 2 * (st - 1) + i + 1))
                        src = f_qk[:, i, :] if st < 2 else rest[:, i, (st - 2) // 2, :]
                        if st % 2 == 0:
                            ins = v.tensor_copy(parts[:, i, st // 2, :], src)
                        else:
                            ins = v.tensor_tensor(rest[:, i, st // 2, :], src, parts[:, i, st // 2, :], ALU.subtract)
                        ins.then_inc(s("a_split"), 1)
            for hp in range(2):
                v.memset(v_head[:, hp, :, HD:], 1.0).then_inc(s("a_values"), 1)

        def attn_proj_sync(sp):
            with sp.Fori(0, B) as b:
                sp.wait_ge(s("a_split"), START + at(b, 10, 10))
                for i, dst in enumerate((q_dram, k_dram)):
                    for part in range(3):
                        sp.dma_start(dst[part, :, b, :], parts[:, i, part, :]).then_inc(s("parts_stored"), 16)

        HEADS_PER_PASS = 2
        STEPS = HEADS_PER_PASS * B
        PASSES = NH // HEADS_PER_PASS
        MASK_OPS = 5

        def attn_sync(sp):
            sp.wait_ge(s("parts_stored"), START + B * 96)
            sp.wait_ge(s("mask_stored"), START + 32)

            def load_head(i, hp):
                h = i * HEADS_PER_PASS + hp
                for st, src, split in ((q_st[hp], q_dram, SPLIT_Q), (k_st[hp], k_dram, SPLIT_K)):
                    for g, part in enumerate(split):
                        sp.dma_start(st[g * HD:(g + 1) * HD], src[part, bass.ds(h * HD, HD), :, :]).then_inc(s(f"head{hp}_loaded"), 16)

            def load_mask_factors(i, hp):
                h = i * HEADS_PER_PASS + hp
                sp.dma_start(mq_st[hp][0:MF], mq_dram[bass.ds(h, 1), :, :].rearrange("a f n -> (a f) n")).then_inc(s(f"factors{hp}_loaded"), 16)
                sp.dma_start(mk_st[hp][0:MF], mk_dram[bass.ds(h, 1), :, :].rearrange("a f n -> (a f) n")).then_inc(s(f"factors{hp}_loaded"), 16)

            def store(i, st):
                hp, b = st // B, st % B
                h = i * HEADS_PER_PASS + hp
                sp.wait_ge(s("o_copied"), START + at(i, STEPS, st + 1))
                for w in range(2):
                    sp.dma_start(o_dram[w, bass.ds(h * HD, HD), b, :], o_sb[w * HD:(w + 1) * HD, st % 2, :]).then_inc(s("o_stored%d" % (st % 2)), 16)

            for hp in range(HEADS_PER_PASS):
                load_mask_factors(0, hp)
                load_head(0, hp)

            def one(i, last):
                for st in range(STEPS):
                    store(i, st)
                    if st % B == 0 and not last:
                        load_mask_factors(i + 1, st // B)
                    if st % B == 1 and not last:
                        load_head(i + 1, st // B)

            with sp.Fori(0, PASSES - 1) as i:
                one(i, False)
            one(PASSES - 1, True)
            sp.wait_ge(s("o_stored0"), START + 16 * NH * B)
            sp.wait_ge(s("o_stored1"), START + 16 * NH * B)
            sp.dma_start(o_all, o_dram[0]).then_inc(s("o_loaded"), 16)
            sp.dma_start(s_all, o_dram[1]).then_inc(s("o_loaded"), 16)

        def stepping(eng, scored, quarter, values, turned):
            for tile in range(TPB):
                quarter(0, tile)
            for st in range(2):
                scored(0, st)
                quarter(0, st + TPB)
            turned(0, 0)

            def one(i, last):
                def of(k):
                    return (i, k) if k < STEPS else (i + 1, k - STEPS)
                for st in range(STEPS):
                    if not (last and st + 2 >= STEPS):
                        scored(*of(st + 2))
                        if not (last and st + 2 + TPB >= STEPS):
                            quarter(*of(st + 2 + TPB))
                    values(i, st)
                    if not (last and st + 1 >= STEPS):
                        turned(*of(st + 1))

            with eng.Fori(0, PASSES - 1) as i:
                one(i, False)
            one(PASSES - 1, True)

        def nothing(i, st):
            pass

        def attn_pe(pe):
            pe.wait_ge(s("a_biased"), START + 2 * B)
            pe.wait_ge(s("a_values"), START + B + 2)

            def scored(i, st):
                hp, b = st // B, st % B
                if b == 0:
                    pe.wait_ge(s(f"head{hp}_loaded"), START + at(i, 12 * 16, 12 * 16))
                for t in range(TPB):
                    pe.wait_ge(s("a_exp"), START + at(i, TPB * STEPS, TPB * (st - 1) + t + 1) if st or type(i) is not int or i else START)
                    pe.matmul(PS[:, t, :], q_st[hp][0:KS, b, t * P:(t + 1) * P], k_st[hp][0:KS, b, :], start=True,
                              stop=True).then_inc(s("a_scores"), 1)

            def quarter(i, q):
                hp, tile = q // TPB, q % TPB
                if tile == 0:
                    pe.wait_ge(s(f"factors{hp}_loaded"), START + at(i, 32, 32))
                pe.wait_ge(s("mask_clamped"), START + at(i, STEPS, q))
                pe.matmul(PS[:, 7, :], mq_st[hp][0:MF, tile * P:(tile + 1) * P], mk_st[hp][0:MF, :], start=True,
                          stop=True).then_inc(s("mask_arg"), 1)

            def turned(i, st):
                for t in range(TPB):
                    if t % 2 == 0:
                        pe.wait_ge(s("a_masked"), START + at(i, 2 * STEPS, 2 * st + t // 2 + 1))
                    pe.wait_ge(s("ppT_ready"), START + at(i, TPB * STEPS, TPB * st + t - 1) if st or t or type(i) is not int else START)
                    for kt in range(TPB):
                        tr = pe.transpose(PS[:, 4 + t % 2, kt * P:(kt + 1) * P], pp[:, st % 2, t, kt * P:(kt + 1) * P], ident)
                    tr.then_inc(s("a_transposed"), 1)

            def values(i, st):
                hp, b = st // B, st % B
                pe.wait_ge(s("ppT_ready"), START + at(i, TPB * STEPS, TPB * st + TPB))
                pe.wait_ge(s("v_head_ready"), START + at(i, HEADS_PER_PASS, hp + 1))
                pe.wait_ge(s("o_copied"), START + at(i, STEPS, st))
                for kt in range(TPB):
                    mm = pe.matmul(PS[0:2 * HD, 6, :], v_head[:, hp, b * TPB + kt, :], ppT[:, kt, :],
                                   start=kt == 0, stop=kt == TPB - 1)
                mm.then_inc(s("a_pv"), 1)

            stepping(pe, scored, quarter, values, turned)

        def attn_act(act):
            act.wait_ge(s("mask_rows"), START + 2)

            def scored(i, st):
                for t in range(TPB):
                    if t == 0:
                        act.wait_ge(s("a_nmax"), START + at(i, STEPS, st + 1))
                        if st >= 2 or type(i) is not int or i:
                            act.wait_ge(s("a_transposed"), START + at(i, TPB * STEPS, TPB * (st - 1)))
                    act.activation(pp[:, st % 2, t, :], PS[:, t, :], ACT.Exp, bias=a_nmax[:, st % 2, t:t + 1]).then_inc(s("a_exp"), 1)

            def quarter(i, q):
                hp, tile = q // TPB, q % TPB
                act.wait_ge(s("mask_clamped"), START + at(i, STEPS, q + 1))
                z = mk[:, hp, tile, :]
                for k, (func, bias, scale) in enumerate(((ACT.Exp, 0.0, 1.0), (ACT.Ln, 1.0, 1.0), (ACT.Exp, 0.0, -1.0),
                                                         (ACT.Ln, c_1e6, 1.0), (ACT.Exp, 0.0, 0.3))):
                    if k:
                        act.wait_ge(s("mask_stage"), START + at(i, MASK_OPS * STEPS, MASK_OPS * q + k))
                    act.activation(z, z, func, bias=bias, scale=scale).then_inc(s("mask_stage"), 1)

            def values(i, st):
                act.wait_ge(s("a_pv"), START + at(i, STEPS, st + 1))
                act.wait_ge(s("o_stored%d" % (st % 2)), START + at(i, 32 * STEPS // 2, 32 * (st // 2)))
                act.activation(o_sb[0:2 * HD, st % 2, :], PS[0:2 * HD, 6, :], ACT.Copy).then_inc(s("o_copied"), 1)

            act.preload_act_table_set("natural_log_exp_and_others")
            stepping(act, scored, quarter, values, nothing)

        def attn_dve(v):
            v.wait_ge(s("a_values"), START + B + 2)
            v.wait_ge(s("mask_rows"), START + 2)

            def scored(i, st):
                v.wait_ge(s("a_scores"), START + at(i, TPB * STEPS, TPB * (st + 1)))
                v.wait_ge(s("a_exp"), START + at(i, TPB * STEPS, TPB * (st - 1)) if st or type(i) is not int or i else START)
                v.tensor_reduce(a_nmax[:, st % 2, :], PS[:, 0:TPB, :], AX.X, ALU.max, negate=True).then_inc(s("a_nmax"), 1)

            def quarter(i, q):
                hp, tile = q // TPB, q % TPB
                v.wait_ge(s("mask_arg"), START + at(i, STEPS, q + 1))
                if q >= 2 * B or type(i) is not int or i:
                    v.wait_ge(s("a_masked"), START + at(i, 2 * STEPS, 2 * B * (hp - 1)))
                v.tensor_scalar(mk[:, hp, tile, :], PS[:, 7, :], acol[:, 5:6], MASK_CLAMP, ALU.mult,
                                ALU.min).then_inc(s("mask_clamped"), 1)

            def turned(i, st):
                hp, b = st // B, st % B
                v.wait_ge(s("a_pv"), START + at(i, STEPS, st))
                if b == 0:
                    h = i * HEADS_PER_PASS + hp
                    plain_wait(v)
                    v.tensor_copy(v_head[:, hp, :, 0:HD], v_all[:, :, bass.ds(h * HD, HD)]).then_inc(s("v_head_ready"), 1)
                for t in range(TPB):
                    v.wait_ge(s("a_transposed"), START + at(i, TPB * STEPS, TPB * st + t + 1))
                    v.tensor_copy(ppT[:, :, t * P:(t + 1) * P],
                                  PS[:, 4 + t % 2, :].rearrange("p (a b) -> p a b", a=TPB)).then_inc(s("ppT_ready"), 1)

            stepping(v, scored, quarter, nothing, turned)

        def attn_pool(g):
            with g.Fori(0, PASSES) as i:
                for st in range(STEPS):
                    hp = st // B
                    if st % B == 0:
                        g.wait_ge(s("mask_stage"), START + at(i, MASK_OPS * STEPS, MASK_OPS * TPB * (hp + 1)))
                    for half in range(2):
                        g.wait_ge(s("a_exp"), START + at(i, TPB * STEPS, TPB * st + 2 * half + 2))
                        a = pp[:, st % 2, 2 * half:2 * half + 2, :]
                        g.tensor_tensor(a, a, mk[:, hp, 2 * half:2 * half + 2, :], ALU.mult).then_inc(s("a_masked"), 1)

        def attn_out_pe(pe):
            with pe.Fori(0, B) as b:
                pe.wait_ge(s("att_ready"), START + at(b, 2, 2))
                pe.matmul(PS[:, 0, :], aw[:, 3, :], att, start=True, stop=True).then_inc(s("a_out"), 1)

        def attn_out_dve(v):
            v.wait_ge(s("o_loaded"), START + 32)
            with v.Fori(0, B) as b:
                v.reciprocal(inv, s_all[:, b, :]).then_inc(s("att_ready"), 1)
                v.wait_ge(s("att_ready"), START + at(b, 2, 1))
                v.tensor_tensor(att, o_all[:, b, :], inv, ALU.mult).then_inc(s("att_ready"), 1)
                v.wait_ge(s("a_out"), START + at(b, 1, 1))
                v.scalar_tensor_tensor(xT[:, b, :], PS[:, 0, :], acol[:, 2:3], xT[:, b, :], ALU.add, ALU.add).then_inc(s("x_ready"), 1)

        stage_memory()
        m_xn = carve([L])
        lg = carve([3, TPB, E])
        tops = carve([TPB, E])
        top_i = carve([TPB, E])
        top_u = top_i.bitcast(U32)
        top_f = carve([TPB, E])
        e_small = carve([6, TPB])
        eq = carve([3, TPB, E])
        comb = carve([TPB, E])
        c_rest = carve([2, L])
        comb3 = carve([L], BF16)
        c_two = carve([L], BF16)
        cb = carve([2, L])
        gc, sl = carve([2, L]), carve([2, L])
        mh = carve([3, L])
        weighted = carve([2, L])
        acc = carve([L])
        MOE_CHUNKS = [(e, c) for e in range(E) for c in range(FCH)] + [(E, 0)]
        LAG = 2
        NMC = len(MOE_CHUNKS)

        def moe_weights(e, c):
            if e == E:
                return sgu[:, 0:FS], sgu[:, FS:2 * FS], sdn[:]
            return gu[:, e, c * P:(c + 1) * P], gu[:, e, F + c * P:F + (c + 1) * P], dn[:, e, c, :]

        def moe_pe(pe, m):
            pe.wait_ge(s("x_ready"), START + x_of(f"moe{m}"))
            pe.wait_ge(s("moe_loaded"), START + 64)
            with pe.Fori(0, B) as b:
                n = b + B * m
                e0 = b + first_ln[f"moe{m}"]
                pe.wait_ge(s("cb_ready"), START + at(n, E))
                ln_pe(xT[:, b, :], e0, 6, 7)
                pe.wait_ge(s("ln_done"), START + e0 + 1)
                for t in range(TPB):
                    mm = pe.matmul(PS[:, 6, t * E:(t + 1) * E], m_xn[:, t * P:(t + 1) * P], rw[:], start=True, stop=True)
                mm.then_inc(s("logits"), 1)

                def down(k):
                    e, c = MOE_CHUNKS[k]
                    pe.wait_ge(s("moe_hidden"), START + at(n, NMC, k + 1))
                    if c == 0:
                        pe.wait_ge(s("moe_weighted"), START + at(n, E + 1, max(e - 1, 0)))
                    last = c == FCH - 1 or e == E
                    mm = pe.matmul(PS[:, 4 + e % 2, :], moe_weights(e, c)[2], mh[:, k % 3, :], start=c == 0, stop=last)
                    mm.then_inc(s("moe_down"), 1)

                def comb_rows():
                    pe.wait_ge(s("comb_ready"), START + n + 1)
                    for t in range(TPB):
                        tr = pe.transpose(PS[0:E, 7, t * P:(t + 1) * P], comb[:, t, :], ident)
                    tr.then_inc(s("combT"), 1)

                def comb_bcast(e):
                    if e == 0:
                        pe.wait_ge(s("comb_split"), START + at(n, 6, 6))
                    pe.wait_ge(s("cb_ready"), START + at(n, E, e))
                    pe.matmul(PS[:, 6, :], sel_b[0:96, e, :], comb3[0:96, :], start=True, stop=True).then_inc(s("cb_done"), 1)

                for k in range(NMC + LAG):
                    if k < NMC:
                        e, c = MOE_CHUNKS[k]
                        wg, wu, _ = moe_weights(e, c)
                        if c == 0 and e < E:
                            pe.wait_ge(s(f"experts{e // 2}_loaded"), START + 64)
                        pe.wait_ge(s("moe_clipped"), START + reuse(n, NMC, k, 2))
                        pe.matmul(PS[:, k % 2, :], wg, m_xn, start=True, stop=True).then_inc(s("moe_gate"), 1)
                        pe.wait_ge(s("moe_hidden"), START + reuse(n, NMC, k, 2))
                        pe.matmul(PS[:, 2 + k % 2, :], wu, m_xn, start=True, stop=True).then_inc(s("moe_up"), 1)
                    if k == 1:
                        comb_rows()
                    if k >= LAG:
                        down(k - LAG)
                        e, c = MOE_CHUNKS[k - LAG]
                        if c == 1:
                            comb_bcast(e)

        def moe_act(act, m):
            act.wait_ge(s("x_ready"), START + x_of(f"moe{m}"))
            with act.Fori(0, B) as b:
                n = b + B * m
                act.preload_act_table_set("natural_log_exp_and_others")
                ln_act(b + first_ln[f"moe{m}"], 7)
                act.wait_ge(s("logits_shifted"), START + n + 1)
                act.activation(lg[:, 1, :, :], lg[:, 0, :, :], ACT.Exp).then_inc(s("logits_exp"), 1)
                for k in range(NMC + 3):
                    if k < NMC:
                        act.wait_ge(s("moe_clipped"), START + at(n, NMC, k + 1))
                        act.wait_ge(s("moe_hidden"), START + reuse(n, NMC, k, 2))
                        act.activation(sl[:, k % 2, :], gc[:, k % 2, :], ACT.Silu).then_inc(s("moe_silu"), 1)
                    if k >= 3 and MOE_CHUNKS[k - 3][1] == 1:
                        e = MOE_CHUNKS[k - 3][0]
                        act.wait_ge(s("cb_done"), START + at(n, E, e + 1))
                        act.wait_ge(s("moe_weighted"), START + at(n, E + 1, max(e - 1, 0)))
                        act.activation(cb[:, e % 2, :], PS[:, 6, :], ACT.Copy).then_inc(s("cb_ready"), 1)

        def moe_dve(v, m):
            v.wait_ge(s("x_ready"), START + x_of(f"moe{m}"))
            with v.Fori(0, B) as b:
                n = b + B * m
                chain = [0]

                def then(ins):
                    chain[0] += 1
                    ins.then_inc(s("route_step"), 1)
                    v.wait_ge(s("route_step"), START + at(n, ROUTE_STEPS, chain[0]))

                ln_dve(xT[:, b, :], b + first_ln[f"moe{m}"], 6, mcol[:, 0:1], mcol[:, 1:2], m_xn)

                def bc(a):
                    return a.unsqueeze(2).broadcast_to([P, TPB, E])

                def softmax_top2():
                    v.wait_ge(s("logits"), START + n + 1)
                    logits = PS[:, 6, 0:TPB * E].rearrange("p (a b) -> p a b", a=TPB)
                    then(v.tensor_reduce(e_small[:, 0, :], logits, AX.X, ALU.max))
                    v.tensor_tensor(lg[:, 0, :, :], logits, bc(e_small[:, 0, :]), ALU.subtract).then_inc(s("logits_shifted"), 1)
                    v.wait_ge(s("logits_exp"), START + n + 1)
                    then(v.tensor_reduce(e_small[:, 1, :], lg[:, 1, :, :], AX.X, ALU.add))
                    then(v.reciprocal(e_small[:, 2, :], e_small[:, 1, :]))
                    then(v.tensor_tensor(lg[:, 2, :, :], lg[:, 1, :, :], bc(e_small[:, 2, :]), ALU.mult))
                    for t in range(TPB):
                        plain_wait(v)
                        then(v.max(tops[:, t, :], lg[:, 2, t, :]))
                        plain_wait(v)
                        then(v.max_index(top_u[:, t, :], tops[:, t, :], lg[:, 2, t, :]))
                    then(v.tensor_copy(top_f, top_u))
                    then(v.tensor_tensor(e_small[:, 3, :], tops[:, :, 0], tops[:, :, 1], ALU.add))
                    then(v.reciprocal(e_small[:, 4, :], e_small[:, 3, :]))
                    iota = con[:, C_IOTA:C_IOTA + TPB * E].rearrange("p (a b) -> p a b", a=TPB)
                    for i in range(2):
                        then(v.tensor_tensor(e_small[:, 5, :], tops[:, :, i], e_small[:, 4, :], ALU.mult))
                        then(v.tensor_tensor(eq[:, i, :, :], iota, bc(top_f[:, :, i]), ALU.is_equal))
                        then(v.tensor_tensor(eq[:, i, :, :], eq[:, i, :, :], bc(e_small[:, 5, :]), ALU.mult))
                    v.tensor_tensor(comb, eq[:, 0, :, :], eq[:, 1, :, :], ALU.add).then_inc(s("comb_ready"), 1)

                def comb_parts():
                    v.wait_ge(s("combT"), START + n + 1)
                    T, c1, c2 = PS[0:E, 7, :], comb3[0:E], c_two[0:E]
                    r1, r2 = c_rest[0:E, 0], c_rest[0:E, 1]
                    for st, (dst, a, part) in enumerate(((c1, T, None), (r1, T, c1), (c2, r1, None), (r2, r1, c2),
                                                         (comb3[32:32 + E], c2, None), (comb3[64:64 + E], r2, None))):
                        if st:
                            v.wait_ge(s("comb_split"), START + at(n, 6, st))
                        ins = v.tensor_copy(dst, a) if part is None else v.tensor_tensor(dst, a, part, ALU.subtract)
                        ins.then_inc(s("comb_split"), 1)

                def weigh(e):
                    last = at(n, NMC, min((e + 1) * FCH, NMC))
                    v.wait_ge(s("moe_down"), START + last)
                    v.wait_ge(s("moe_acc"), START + at(n, E, max(e - 1, 0) if e < E else E))
                    if e < E:
                        v.wait_ge(s("cb_ready"), START + at(n, E, e + 1))
                        v.tensor_tensor(weighted[:, e % 2, :], PS[:, 4 + e % 2, :], cb[:, e % 2, :], ALU.mult).then_inc(s("moe_weighted"), 1)
                    else:
                        v.tensor_tensor(weighted[:, 0, :], PS[:, 4, :], acc, ALU.add).then_inc(s("moe_weighted"), 1)

                for k in range(NMC + LAG + 1):
                    if k == 0:
                        softmax_top2()
                    if k == 2:
                        comb_parts()
                    if k < NMC:
                        v.wait_ge(s("moe_gate"), START + at(n, NMC, k + 1))
                        v.wait_ge(s("moe_silu"), START + reuse(n, NMC, k, 2))
                        v.tensor_scalar(gc[:, k % 2, :], PS[:, k % 2, :], 10.0, -10.0, ALU.min, ALU.max).then_inc(s("moe_clipped"), 1)
                    if 1 <= k <= NMC:
                        j = k - 1
                        v.wait_ge(s("moe_silu"), START + at(n, NMC, j + 1))
                        v.wait_ge(s("moe_up"), START + at(n, NMC, j + 1))
                        v.wait_ge(s("moe_down"), START + reuse(n, NMC, j, 3))
                        v.tensor_tensor(mh[:, j % 3, :], sl[:, j % 2, :], PS[:, 2 + j % 2, :], ALU.mult).then_inc(s("moe_hidden"), 1)
                    if k >= 3 and k - 3 < NMC and k - 3 >= 1 and MOE_CHUNKS[k - 3][1] == 0 and MOE_CHUNKS[k - 3][0] > 0:
                        weigh(MOE_CHUNKS[k - 3][0] - 1)
                weigh(E)
                v.wait_ge(s("moe_weighted"), START + at(n, E + 1, E + 1))
                v.scalar_tensor_tensor(xT[:, b, :], weighted[:, 0, :], 0.5, xT[:, b, :], ALU.mult, ALU.add).then_inc(s("x_ready"), 1)
                assert chain[0] == ROUTE_STEPS, chain[0]

        ROUTE_STEPS = 4 + 2 * TPB + 3 + 6

        def moe_pool(g, m):
            g.memset(comb3[0:96, :].bitcast(F32), 0.0).then_inc(s("comb3_zero"), 1)
            with g.Fori(0, B) as b:
                n = b + B * m
                for e in range(E):
                    g.wait_ge(s("moe_weighted"), START + at(n, E + 1, e + 1))
                    g.wait_ge(s("moe_acc"), START + at(n, E, e))
                    if e == 0:
                        plain_wait(g)
                        g.tensor_copy(acc, weighted[:, 0, :]).then_inc(s("moe_acc"), 1)
                    else:
                        g.tensor_tensor(acc, acc, weighted[:, e % 2, :], ALU.add).then_inc(s("moe_acc"), 1)

        stage_memory()
        t_xn = carve([L])
        qT, kT, vT = (carve([B, L]) for _ in range(3))
        k_tok = carve([B * TPB, D])
        raw, rsq, rlog = carve([2, L]), carve([2, L]), carve([2, L])
        k_s = carve([L])
        kt_s = carve([TPB, D])
        sg, g_m, g_d = carve([2, TH]), carve([2, TH]), carve([2, TH])
        start = taken[0]
        th_h, th_s, th_w = (carve([TPB, TH]) for _ in range(3))
        end, taken[0] = taken[0], start
        X = [carve([TH]) for _ in range(3)]
        XT = [carve([4, D]) for _ in range(3)]
        A_s, A_b, B_s = ([carve([D]) for _ in range(3)] for _ in range(3))
        gsq = carve([TH])
        assert taken[0] <= end
        taken[0] = end
        hT = carve([4, L])
        dp = carve([L])
        dp_tok = carve([TPB, D])
        du, dg = carve([2, TH]), carve([2, TH])
        grad = carve([3, TH])
        nrm = carve([4, 4])
        a_ident = carve([D])
        v_bias = carve([1])

        def ttt_proj_pe(pe):
            pe.wait_ge(s("x_ready"), START + x_of("ttt"))
            pe.wait_ge(s("ttt_loaded"), START + 112)
            with pe.Fori(0, B) as b:
                e = b + first_ln["ttt"]
                ln_pe(xT[:, b, :], e, 6, 7)
                pe.wait_ge(s("ln_done"), START + e + 1)
                pe.wait_ge(s("t_biased"), START + at(b, 3))
                for i in range(3):
                    pe.matmul(PS[:, i, :], tqkv[:, i * D:(i + 1) * D], t_xn, start=True, stop=True).then_inc(s("t_proj"), 1)
                for i in range(2):
                    pe.wait_ge(s("t_squared"), START + at(b, 2, i + 1))
                    pe.matmul(PS[:, 3 + i, :], blk8, rsq[:, i, :], start=True, stop=True).then_inc(s("t_sums"), 1)
                pe.wait_ge(s("k_staged"), START + at(b, 1, 1))
                pe.wait_ge(s("k_tok_ready"), START + at(b, 1))
                for t in range(TPB):
                    tr = pe.transpose(PS[:, 5, t * P:(t + 1) * P], k_s[:, t * P:(t + 1) * P], ident)
                tr.then_inc(s("k_transposed"), 1)

        def ttt_proj_act(act):
            act.wait_ge(s("x_ready"), START + x_of("ttt"))
            act.wait_ge(s("ttt_consts"), START + 2)
            act.preload_act_table_set("natural_log_exp_and_others")
            with act.Fori(0, B) as b:
                e = b + first_ln["ttt"]
                ln_act(e, 7)
                for i in range(3):
                    act.wait_ge(s("t_proj"), START + at(b, 3, i + 1))
                    act.wait_ge(s("t_scaled"), START + at(b, 2))
                    dst = raw[:, i, :] if i < 2 else vT[:, b, :]
                    plain_wait(act)
                    act.activation(dst, PS[:, i, :], ACT.Identity, bias=tcol[:, 4 + i:5 + i] if i < 2 else v_bias,
                                   scale=1.0 if i < 2 else GRAD_SCALE).then_inc(s("t_biased"), 1)
                for i in range(2):
                    act.wait_ge(s("t_biased"), START + at(b, 3, i + 1))
                    act.activation(rsq[:, i, :], raw[:, i, :], ACT.Square).then_inc(s("t_squared"), 1)
                for i in range(2):
                    act.wait_ge(s("t_sums"), START + at(b, 2, i + 1))
                    c = at(b, 8, 4 * i)
                    act.activation(rlog[:, i, :], PS[:, 3 + i, :], ACT.Ln, bias=c_tiny, scale=2.0 ** LS).then_inc(s("t_norm_step"), 1)
                    act.wait_ge(s("t_norm_step"), START + c + 1)
                    act.activation(rlog[:, i, :], rlog[:, i, :], ACT.Exp, bias=c_neg, scale=0.5).then_inc(s("t_norm_step"), 1)
                    act.wait_ge(s("t_norm_step"), START + c + 2)
                    act.activation(rlog[:, i, :], rlog[:, i, :], ACT.Ln, bias=c_1e6).then_inc(s("t_norm_step"), 1)
                    act.wait_ge(s("t_norm_step"), START + c + 3)
                    act.activation(rlog[:, i, :], rlog[:, i, :], ACT.Exp, scale=-1.0).then_inc(s("t_norm_step"), 1)

        def ttt_proj_dve(v):
            v.wait_ge(s("x_ready"), START + x_of("ttt"))
            v.wait_ge(s("ttt_loaded"), START + 112)
            v.tensor_scalar(v_bias, tcol[:, 6:7], GRAD_SCALE, None, ALU.mult).then_inc(s("ttt_consts"), 1)
            v.tensor_scalar(a_ident, ident, NS_A, None, ALU.mult).then_inc(s("ttt_consts"), 1)
            with v.Fori(0, B) as b:
                e = b + first_ln["ttt"]
                ln_dve(xT[:, b, :], e, 6, c_one, c_zero, t_xn)
                for i, dst in enumerate((qT, kT)):
                    v.wait_ge(s("t_norm_step"), START + at(b, 8, 4 * i + 4))
                    v.scalar_tensor_tensor(raw[:, i, :], raw[:, i, :], tcol[:, 2 * i:2 * i + 1], rlog[:, i, :], ALU.mult,
                                           ALU.mult).then_inc(s("t_scaled"), 1)
                    v.wait_ge(s("t_scaled"), START + at(b, 2, i + 1))
                    v.tensor_scalar(dst[:, b, :], raw[:, i, :], tcol[:, 2 * i + 1:2 * i + 2], None, ALU.add)
                v.wait_ge(s("k_transposed"), START + at(b, 1))
                v.tensor_scalar(k_s, raw[:, 1, :], tcol[:, 3:4], None, ALU.add).then_inc(s("k_staged"), 1)
                v.wait_ge(s("k_transposed"), START + at(b, 1, 1))
                plain_wait(v)
                v.tensor_copy(k_tok[:, bass.ds(b * TPB, TPB), :], PS[:, 5, :].rearrange("p (a b) -> p a b", a=TPB)).then_inc(s("k_tok_ready"), 1)

        def grad_pe(pe, step):
            with pe.Fori(0, B) as b:
                n = b + B * step
                pe.wait_ge(s("staged"), START + at(n, 2, 2))
                pe.wait_ge(s("theta_ready"), START + 4 * step)

                def turn(t):
                    pe.wait_ge(s("g_h"), START + at(n, TPB, t + 1))
                    pe.wait_ge(s("hT_ready"), START + at(n, TPB, t))
                    for c in range(4):
                        tr = pe.transpose(PS[:, 4, c * P:(c + 1) * P], th_h[:, t, c * P:(c + 1) * P], ident)
                    tr.then_inc(s("h_turned"), 1)

                for t in range(TPB):
                    kt = k_s[:, t * P:(t + 1) * P]
                    pe.wait_ge(s("g_w"), START + at(n, TPB, max(t - 1, 0)))
                    if t < 2:
                        pe.wait_ge(s("g_dg"), START + at(n, TPB))
                    pe.matmul(PS[:, t % 2, :], kt, th_g[:], start=True, stop=True).then_inc(s("g_gate"), 1)
                    pe.matmul(PS[:, 2 + t % 2, :], kt, th_v[:], start=True, stop=True).then_inc(s("g_val"), 1)
                    if t >= 1:
                        turn(t - 1)
                turn(TPB - 1)
                pe.wait_ge(s("hT_ready"), START + at(n, TPB, TPB))
                pe.wait_ge(s("grad_added"), START + at(n, 3))
                for c in range(4):
                    mm = pe.matmul(PS[:, 5, :], th_p[:, c, :], hT[:, c, :], start=c == 0, stop=c == 3)
                mm.then_inc(s("predicted"), 1)
                pe.wait_ge(s("dp_ready"), START + at(n, 1, 1))
                for t in range(TPB):
                    tr = pe.transpose(PS[:, 4, t * P:(t + 1) * P], dp[:, t * P:(t + 1) * P], ident)
                tr.then_inc(s("dp_turned"), 1)

                def dh(t):
                    pe.wait_ge(s("g_w"), START + at(n, TPB, TPB))
                    pe.wait_ge(s("g_dg"), START + at(n, TPB, max(t - 1, 0)))
                    pe.matmul(PS[:, t % 2, :], dp[:, t * P:(t + 1) * P], th_pT[:], start=True, stop=True).then_inc(s("g_dh"), 1)

                dh(0)
                pe.wait_ge(s("dp_tok_ready"), START + at(n, 1, 1))
                for t in range(TPB):
                    if t < TPB - 1:
                        dh(t + 1)
                    st, sp_ = t == 0, t == TPB - 1
                    mm = pe.matmul(PS[:, 5, :], dp_tok[:, t, :], th_h[:, t, :], start=st, stop=sp_)
                    if sp_:
                        mm.then_inc(s("grads"), 1)
                    pe.wait_ge(s("g_du"), START + at(n, TPB, t + 1))
                    mm = pe.matmul(PS[:, 6, :], kt_s[:, t, :], du[:, t % 2, :], start=st, stop=sp_)
                    if sp_:
                        mm.then_inc(s("grads"), 1)
                    pe.wait_ge(s("g_dg"), START + at(n, TPB, t + 1))
                    pe.matmul(PS[:, 7, :], kt_s[:, t, :], dg[:, t % 2, :], start=st, stop=sp_).then_inc(s("g_used"), 1)

        def grad_act(act, step):
            with act.Fori(0, B) as b:
                n = b + B * step
                for t in range(TPB + 1):
                    if t < TPB:
                        act.wait_ge(s("g_gate"), START + at(n, TPB, t + 1))
                        act.wait_ge(s("g_w"), START + at(n, TPB, max(t - 1, 0)))
                        act.activation(sg[:, t % 2, :], PS[:, t % 2, :], ACT.Sigmoid).then_inc(s("g_sig"), 1)
                    if t >= 1:
                        act.wait_ge(s("h_turned"), START + at(n, TPB, t))
                        if t == 1:
                            act.wait_ge(s("predicted"), START + n)
                        act.activation(hT[:, :, (t - 1) * P:t * P], PS[:, 4, :].rearrange("p (a b) -> p a b", a=4),
                                       ACT.Copy).then_inc(s("hT_ready"), 1)
                act.wait_ge(s("dp_turned"), START + n + 1)
                act.wait_ge(s("grads"), START + at(n, 2))
                act.activation(dp_tok.rearrange("p a b -> p (a b)"), PS[:, 4, :], ACT.Copy).then_inc(s("dp_tok_ready"), 1)

        def grad_dve(v, step):
            if step == 0:
                v.memset(grad, 0.0).then_inc(s("grad_zero"), 1)
            else:
                v.wait_ge(s("theta_ready"), START + 4 * step)
                v.memset(grad, 0.0).then_inc(s("grad_zero"), 1)
            v.wait_ge(s("grad_zero"), START + step + 1)
            with v.Fori(0, B) as b:
                n = b + B * step
                for t in range(TPB):
                    j = t % 2
                    u = PS[:, 2 + j, :]
                    v.wait_ge(s("g_sig"), START + at(n, TPB, t + 1))
                    v.wait_ge(s("g_val"), START + at(n, TPB, t + 1))
                    if t == 0:
                        v.wait_ge(s("g_used"), START + at(n, TPB))
                    v.tensor_tensor(th_s[:, t, :], PS[:, j, :], sg[:, j, :], ALU.mult).then_inc(s("g_silu"), 1)
                    v.wait_ge(s("g_silu"), START + at(n, TPB, t + 1))
                    v.scalar_tensor_tensor(g_m[:, j, :], sg[:, j, :], 1.0, th_s[:, t, :], ALU.subtract, ALU.mult).then_inc(s("g_slope"), 1)
                    v.tensor_tensor(th_h[:, t, :], th_s[:, t, :], u, ALU.mult).then_inc(s("g_h"), 1)
                    v.wait_ge(s("g_slope"), START + at(n, 2 * TPB, 2 * t + 1))
                    v.tensor_tensor(g_d[:, j, :], sg[:, j, :], g_m[:, j, :], ALU.subtract).then_inc(s("g_slope"), 1)
                    v.wait_ge(s("g_slope"), START + at(n, 2 * TPB, 2 * t + 2))
                    v.tensor_tensor(th_w[:, t, :], g_d[:, j, :], u, ALU.mult).then_inc(s("g_w"), 1)
                v.wait_ge(s("predicted"), START + n + 1)
                v.wait_ge(s("grads"), START + at(n, 2))
                v.scalar_tensor_tensor(dp, PS[:, 5, :], GRAD_SCALE, vT[:, b, :], ALU.mult, ALU.subtract).then_inc(s("dp_ready"), 1)
                for t in range(TPB):
                    v.wait_ge(s("g_dh"), START + at(n, TPB, t + 1))
                    v.wait_ge(s("g_used"), START + at(n, TPB, max(t - 1, 0)))
                    v.tensor_tensor(du[:, t % 2, :], PS[:, t % 2, :], th_s[:, t, :], ALU.mult).then_inc(s("g_du"), 1)
                    v.tensor_tensor(dg[:, t % 2, :], PS[:, t % 2, :], th_w[:, t, :], ALU.mult).then_inc(s("g_dg"), 1)
                v.wait_ge(s("grads"), START + at(n, 2, 2))
                v.wait_ge(s("g_used"), START + at(n, TPB, TPB))
                v.wait_ge(s("grad_added"), START + at(n, 3))
                for i, bank in enumerate((7, 6, 5)):
                    v.tensor_tensor(grad[:, i, :], grad[:, i, :], PS[:, bank, :], ALU.add).then_inc(s("grad_added"), 1)

        def grad_pool(g, step):
            with g.Fori(0, B) as b:
                n = b + B * step
                g.wait_ge(s("k_tok_ready"), START + B)
                g.wait_ge(s("g_used"), START + at(n, TPB))
                plain_wait(g)
                g.tensor_copy(k_s, kT[:, b, :]).then_inc(s("staged"), 1)
                plain_wait(g)
                g.tensor_copy(kt_s, k_tok[:, bass.ds(b * TPB, TPB), :]).then_inc(s("staged"), 1)

        def ns_pe(pe, step):
            pe.wait_ge(s("ns_sumsq"), START + 3 * (step + 1))
            pe.matmul(PS[:, 0, 0:3], ones, nrm[:, 0, 0:3], start=True, stop=True).then_inc(s("ns_norm"), 1)
            for j in range(3):
                pe.wait_ge(s("ns_X0"), START + 3 * step + j + 1)
                for c in range(4):
                    tr = pe.transpose(PS[:, 3 + j, c * P:(c + 1) * P], X[j][:, c * P:(c + 1) * P], ident)
                tr.then_inc(s("ns_T0"), 1)
            with pe.Fori(0, NS_ITERS) as it:
                n = it + NS_ITERS * step
                for j in range(3):
                    if j == 0:
                        pe.wait_ge(s("ns_T0_copied"), START + 3 * (step + 1))
                    pe.wait_ge(s("ns_XT"), START + at(n, 3))
                    for c in range(4):
                        mm = pe.matmul(PS[:, j, 0:P], XT[j][:, c, :], XT[j][:, c, :], start=c == 0, stop=c == 3)
                    mm.then_inc(s("ns_A"), 1)
                for j in range(3):
                    pe.wait_ge(s("ns_A_copied"), START + at(n, 3, j + 1))
                    pe.wait_ge(s("ns_A_poly"), START + at(n, 3, j + 1))
                    pe.matmul(PS[:, j, P:2 * P], A_s[j], A_s[j], start=True, stop=True).then_inc(s("ns_A2"), 1)
                for j in range(3):
                    pe.wait_ge(s("ns_B"), START + at(n, 3, j + 1))
                    pe.wait_ge(s("ns_X"), START + at(n, 3))
                    pe.matmul(PS[:, 3 + j, :], B_s[j], X[j], start=True, stop=True).then_inc(s("ns_BX"), 1)
                    if j >= 1:
                        pe.wait_ge(s("ns_XT"), START + (at(n, 3, j - 1) if j >= 2 else at(n, 3)))
                    for c in range(4):
                        mm = pe.matmul(PS[:, 6 + j % 2, c * P:(c + 1) * P], X[j][:, c * P:(c + 1) * P], B_s[j], start=True, stop=True)
                    mm.then_inc(s("ns_XTB"), 1)

        def ns_act(act, step):
            v3 = 3 * step
            act.preload_act_table_set("natural_log_exp_and_others")
            act.wait_ge(s("grad_added"), START + 3 * B * (step + 1))
            for j in range(3):
                if j:
                    act.wait_ge(s("ns_sumsq"), START + v3 + j)
                act.activation(gsq, grad[:, j, :], ACT.Square, accum_out=nrm[:, 0, j:j + 1]).then_inc(s("ns_sumsq"), 1)
            act.wait_ge(s("ns_norm"), START + step + 1)
            act.activation(nrm[:, 1, 0:3], PS[:, 0, 0:3], ACT.Ln, bias=c_tiny, scale=2.0 ** LS).then_inc(s("ns_scale_step"), 1)
            act.wait_ge(s("ns_scale_step"), START + 4 * step + 1)
            act.activation(nrm[:, 2, 0:3], nrm[:, 1, 0:3], ACT.Exp, bias=c_neg, scale=0.5).then_inc(s("ns_scale_step"), 1)
            for j in range(3):
                act.wait_ge(s("ns_T0"), START + v3 + j + 1)
                act.activation(XT[j].rearrange("p a b -> p (a b)"), PS[:, 3 + j, :], ACT.Copy).then_inc(s("ns_T0_copied"), 1)
            with act.Fori(0, NS_ITERS) as it:
                n = it + NS_ITERS * step
                for j in range(3):
                    act.wait_ge(s("ns_A"), START + at(n, 3, j + 1))
                    act.activation(A_s[j], PS[:, j, 0:P], ACT.Copy).then_inc(s("ns_A_copied"), 1)
                for j in range(3):
                    act.wait_ge(s("ns_XTB"), START + at(n, 3, j + 1))
                    act.activation(XT[j].rearrange("p a b -> p (a b)"), PS[:, 6 + j % 2, :], ACT.Copy).then_inc(s("ns_XT"), 1)

        def ns_dve(v, step):
            v3 = 3 * step
            v.wait_ge(s("ns_scale_step"), START + 4 * step + 2)
            v.tensor_scalar(nrm[:, 3, 0:3], nrm[:, 2, 0:3], 1e-7, None, ALU.add).then_inc(s("ns_scale_step"), 1)
            v.wait_ge(s("ns_scale_step"), START + 4 * step + 3)
            v.reciprocal(nrm[:, 1, 0:3], nrm[:, 3, 0:3]).then_inc(s("ns_scale_step"), 1)
            v.wait_ge(s("ns_scale_step"), START + 4 * step + 4)
            for j in range(3):
                v.tensor_scalar(X[j], grad[:, j, :], nrm[:, 1, j:j + 1], None, ALU.mult).then_inc(s("ns_X0"), 1)
            with v.Fori(0, NS_ITERS) as it:
                n = it + NS_ITERS * step
                for j in range(3):
                    v.wait_ge(s("ns_A_copied"), START + at(n, 3, j + 1))
                    v.scalar_tensor_tensor(A_b[j], A_s[j], NS_B, a_ident, ALU.mult, ALU.add).then_inc(s("ns_A_poly"), 1)
                for j in range(3):
                    v.wait_ge(s("ns_A2"), START + at(n, 3, j + 1))
                    v.wait_ge(s("ns_A_poly"), START + at(n, 3, j + 1))
                    v.scalar_tensor_tensor(B_s[j], PS[:, j, P:2 * P], NS_C, A_b[j], ALU.mult, ALU.add).then_inc(s("ns_B"), 1)
                for j in range(3):
                    v.wait_ge(s("ns_XTB"), START + at(n, 3, j + 1))
                    v.tensor_copy(X[j], PS[:, 3 + j, :]).then_inc(s("ns_X"), 1)
            n = NS_ITERS * (step + 1)
            v.wait_ge(s("ns_X"), START + 3 * n)
            v.wait_ge(s("ns_XT"), START + 3 * n)
            flat = lambda a: a.rearrange("p a b -> p (a b)")
            for dst, src in ((th_g[:], X[0]), (th_v[:], X[1]), (th_pT[:], X[2]), (flat(th_p[:]), flat(XT[2]))):
                v.scalar_tensor_tensor(dst, src, -LR, dst, ALU.mult, ALU.add).then_inc(s("theta_ready"), 1)

        def apply_pe(pe):
            pe.wait_ge(s("theta_ready"), START + 8)
            with pe.Fori(0, B) as b:
                def down(c):
                    pe.wait_ge(s("q_hidden"), START + at(b, 4, c + 1))
                    if c == 0:
                        pe.wait_ge(s("q_down_copied"), START + b)
                    mm = pe.matmul(PS[:, 4, :], th_p[:, c, :], hT[:, c, :], start=c == 0, stop=c == 3)
                    if c == 3:
                        mm.then_inc(s("q_down"), 1)

                for c in range(4):
                    pe.wait_ge(s("q_hidden"), START + reuse(b, 4, c, 2))
                    pe.matmul(PS[:, c % 2, :], th_g[:, c * P:(c + 1) * P], qT[:, b, :], start=True, stop=True).then_inc(s("q_proj"), 1)
                    pe.matmul(PS[:, 2 + c % 2, :], th_v[:, c * P:(c + 1) * P], qT[:, b, :], start=True, stop=True).then_inc(s("q_proj"), 1)
                    if c >= 1:
                        down(c - 1)
                down(3)
                pe.wait_ge(s("q_down_copied"), START + b + 1)
                pe.wait_ge(s("x_ready"), START + x_of("ttt") + b)
                pe.matmul(PS[:, 5, :], tpw[:], dp, start=True, stop=True).then_inc(s("q_out"), 1)

        def apply_act(act):
            with act.Fori(0, B) as b:
                for c in range(4):
                    act.wait_ge(s("q_proj"), START + at(b, 8, 2 * c + 1))
                    act.wait_ge(s("q_hidden"), START + reuse(b, 4, c, 2))
                    act.activation(sg[:, c % 2, :], PS[:, c % 2, :], ACT.Silu).then_inc(s("q_silu"), 1)
                act.wait_ge(s("q_down"), START + b + 1)
                act.wait_ge(s("q_out"), START + b)
                act.activation(dp, PS[:, 4, :], ACT.Copy).then_inc(s("q_down_copied"), 1)

        def apply_dve(v):
            with v.Fori(0, B) as b:
                for c in range(4):
                    v.wait_ge(s("q_silu"), START + at(b, 4, c + 1))
                    v.wait_ge(s("q_proj"), START + at(b, 8, 2 * c + 2))
                    if c == 0:
                        v.wait_ge(s("q_down"), START + b)
                    v.tensor_tensor(hT[:, c, :], sg[:, c % 2, :], PS[:, 2 + c % 2, :], ALU.mult).then_inc(s("q_hidden"), 1)
                v.wait_ge(s("q_out"), START + b + 1)
                v.scalar_tensor_tensor(xT[:, b, :], PS[:, 5, :], tcol[:, 7:8], xT[:, b, :], ALU.add, ALU.add).then_inc(s("x_ready"), 1)

        block = ctx.enter_context(nc.Block())
        run = STAGES[1:]

        @block.sync
        def _(sp):
            load_sync(sp)
            if "attn" in run:
                attn_proj_sync(sp)
                attn_sync(sp)
            if "moe0" in run:
                load_experts(sp)
            sp.wait_ge(s("x_ready"), START + B * len(STAGES))
            sp.dma_start(out, xT[:]).then_inc(s("out_stored"), 16)
            sp.wait_ge(s("out_stored"), START + 16)
            sp.wait_ge(s("mask_stored"), START + 32)

        @block.tensor
        def _(pe):
            pe.wait_ge(s("consts"), START + 7)
            for st in run:
                if st[:3] == "ffn":
                    f = int(st[3])
                    pe.wait_ge(s("x_ready"), START + x_of(st))
                    pe.wait_ge(s("ffn_loaded"), START + 48)
                    pe.wait_ge(s("pads_zero"), START + 3 * (f + 1))
                    ffn_pe(pe, f, 0)
                    ffn_pe(pe, f, 1)
                elif st == "attn":
                    attn_proj_pe(pe)
                    attn_pe(pe)
                    attn_out_pe(pe)
                elif st[:3] == "moe":
                    pe.wait_ge(s("comb3_zero"), START + int(st[3]) + 1)
                    moe_pe(pe, int(st[3]))
                else:
                    ttt_proj_pe(pe)
                    for step in range(TTT_STEPS):
                        grad_pe(pe, step)
                        ns_pe(pe, step)
                    apply_pe(pe)

        @block.scalar
        def _(act):
            load_act(act)
            for st in run:
                if st[:3] == "ffn":
                    f = int(st[3])
                    act.wait_ge(s("x_ready"), START + x_of(st))
                    act.wait_ge(s("pads_zero"), START + 3 * (f + 1))
                    ffn_act(act, f, 0)
                    ffn_act(act, f, 1)
                elif st == "attn":
                    attn_proj_act(act)
                    attn_act(act)
                elif st[:3] == "moe":
                    moe_act(act, int(st[3]))
                else:
                    ttt_proj_act(act)
                    for step in range(TTT_STEPS):
                        grad_act(act, step)
                        ns_act(act, step)
                    apply_act(act)

        @block.vector
        def _(v):
            load_dve(v)
            v.wait_ge(s("rot_scaled"), START + 8)
            for st in run:
                if st[:3] == "ffn":
                    f = int(st[3])
                    v.wait_ge(s("x_ready"), START + x_of(st))
                    v.wait_ge(s("mask_stored"), START + 32)
                    v.wait_ge(s("pads_zero"), START + 3 * (f + 1))
                    ffn_dve(v, f, 0)
                    ffn_dve(v, f, 1)
                elif st == "attn":
                    attn_proj_dve(v)
                    attn_dve(v)
                    attn_out_dve(v)
                elif st[:3] == "moe":
                    v.wait_ge(s("moe_loaded"), START + 64)
                    v.wait_ge(s("comb3_zero"), START + int(st[3]) + 1)
                    moe_dve(v, int(st[3]))
                else:
                    ttt_proj_dve(v)
                    for step in range(TTT_STEPS):
                        grad_dve(v, step)
                        ns_dve(v, step)
                    apply_dve(v)

        @block.gpsimd
        def _(g):
            for name in sorted(sems):
                g.sem_inc(sems[name], START)
            for st in run:
                g.wait_ge(s("x_ready"), START + x_of(st))
                if st[:3] == "ffn":
                    f = int(st[3])
                    ffn_zero_pads(g, f)
                    ffn_pool(g, f, 0)
                    ffn_pool(g, f, 1)
                elif st == "attn":
                    attn_pool(g)
                elif st[:3] == "moe":
                    moe_pool(g, int(st[3]))
                else:
                    for step in range(TTT_STEPS):
                        grad_pool(g, step)


def _layouts(i):
    f = lambda a: np.ascontiguousarray(np.asarray(a))
    cols = lambda *v: f(np.stack(v, -1))
    two = lambda a: np.concatenate([a, a], -1)
    swap = lambda a: np.concatenate([a[..., DH // 2:], a[..., :DH // 2]], -1)
    g = {k: np.asarray(v) for k, v in i.items()}
    wqkv = g["L0_ffn_wqkv"]
    qk = wqkv[:, :, :2 * INNER].reshape(DEPTH, D, 2 * HEADS, 2, DH // 2)[:, :, :, ::-1]
    w2 = np.zeros((3 * P,), wqkv.dtype)
    pad = lambda a, n: np.concatenate([a, np.zeros(a.shape[:-1] + (n - a.shape[-1],), a.dtype)], -1)
    b1 = g["L0_ffn_b1"]
    b1a, b1g = (pad(b, 3 * P).reshape(DEPTH, 3, P) for b in (b1[:, :HID], b1[:, HID:]))
    qs, ks = g["L0_ffn_q_scale"], g["L0_ffn_k_scale"]
    fc = np.zeros((P, DEPTH, 16), wqkv.dtype)
    vecs = [two(qs), two(swap(qs)), two(ks), two(swap(ks)), g["L0_ffn_ln_g"], g["L0_ffn_ln_b"], g["L0_ffn_b2"]]
    vecs += [b1a[:, c] for c in range(3)] + [b1g[:, c] for c in range(3)]
    for n, v in enumerate(vecs):
        fc[:, :, n] = v.T
    w2 = pad(g["L0_ffn_w2"].transpose(0, 2, 1), 3 * P).reshape(DEPTH, D, 3, P).transpose(3, 0, 2, 1)
    ac = np.zeros((P, 8), wqkv.dtype)
    for n, k in enumerate(("L0_attn_bq", "L0_attn_bk", "L0_attn_bo")):
        ac[:, n] = g[k]
    ac[:, 3] = g["L0_attn_temperature"]
    ph = np.zeros((NH, 8), wqkv.dtype)
    ph[:, 0:3] = g["L0_attn_phase"]
    ph[:, 3] = g["L0_attn_threshold"]
    tc = np.zeros((P, 8), wqkv.dtype)
    for n, v in enumerate([np.tile(g["L1_attn_" + k], NH) for k in ("qn_scale", "qn_bias", "kn_scale", "kn_bias")]
                          + list(g["L1_attn_qkv_b"].reshape(3, D)) + [g["L1_attn_proj_b"]]):
        tc[:, n] = v
    return {
        "xT": f(g["L0_attn_x"].transpose(2, 0, 1)),
        "con": shape_constants(), "rot": rotary_tables(), "pos": position_tables(), "phase": ph,
        "wqkv": f(wqkv.transpose(1, 0, 2)),
        "wswap": f(qk.transpose(1, 0, 2, 3, 4)),
        "wo": f(g["L0_ffn_wo"].reshape(DEPTH, NCH, P, D).transpose(2, 0, 1, 3)),
        "w1": f(g["L0_ffn_w1"].transpose(1, 0, 2)),
        "w2": f(w2), "fcol": fc,
        "aw": f(np.stack([g["L0_attn_W" + k] for k in "qkvo"], 1)),
        "acol": ac, "bv_row": f(np.tile(g["L0_attn_bv"][None], (P, 1))),
        "gu": f(g["L1_ffn_gate_up_w"].transpose(1, 0, 2)),
        "dn": f(g["L1_ffn_down_w"].reshape(E, FCH, P, D).transpose(2, 0, 1, 3)),
        "sgu": f(g["L1_ffn_shared_gate_up_w"]), "sdn": f(g["L1_ffn_shared_down_w"]), "rw": f(g["L1_ffn_router_w"]),
        "mcol": cols(g["L1_ffn_ln_gamma"], g["L1_ffn_ln_beta"]),
        "tqkv": f(g["L1_attn_qkv_w"]), "tcol": tc,
        "th_g": f(g["L1_attn_ttt_gate"]), "th_v": f(g["L1_attn_ttt_val"]), "th_pT": f(g["L1_attn_ttt_proj"].T),
        "th_p": f(g["L1_attn_ttt_proj"].reshape(4, P, D).transpose(1, 0, 2)),
        "tpw": f(g["L1_attn_proj_w"]),
    }


def kernel(**inputs):
    import concourse.bacc as bacc
    from concourse.bass_utils import run_bass_kernel_spmd

    nc = bacc.Bacc("TRN2", target_bir_lowering=False, num_devices=1)
    arrays = _layouts(inputs)
    aps = {k: nc.dram_tensor("in_" + k, a.shape, F32, kind="ExternalInput").ap() for k, a in arrays.items()}
    out = nc.dram_tensor("out_xT", (D, B, L), F32, kind="ExternalOutput").ap()
    build(nc, aps, out)
    r = run_bass_kernel_spmd(nc, [{"in_" + k: a for k, a in arrays.items()}], core_ids=[0])
    return np.ascontiguousarray(np.asarray(r.results[0]["out_xT"]).transpose(1, 2, 0))
```

```python
import numpy as np
import concourse.bass as bass
from concourse import mybir
from contextlib import ExitStack

F32 = mybir.dt.float32
BF16 = mybir.dt.bfloat16
U32 = mybir.dt.uint32
I32 = mybir.dt.int32
ALU = mybir.AluOpType
ACT = mybir.ActivationFunctionType
AX = mybir.AxisListType

B, L, D = 4, 512, 128
P = 128
TPB = L // P
LN_EPS = 1e-5

DEPTH, HEADS, DH, WINDOW = 2, 8, 64, 64
INNER = HEADS * DH
QK_SCALE = 8.0
HID = 341
HCH = [(0, 128), (128, 128), (256, HID - 256)]
NCH = INNER // P
UNITS = 2 * TPB

NH, HD = 16, 8
SPLIT_Q = (0, 0, 1, 1, 0, 2)
SPLIT_K = (0, 1, 0, 1, 2, 0)
KS = HD * len(SPLIT_Q)
A_SCALE = float(1.0 / np.sqrt(HD))
MASK_CLAMP = 40.0
MF = 6

E, F, FS = 8, 512, 128
FCH = F // P

TH = 4 * D
LR, NS_ITERS, TTT_STEPS = 0.1, 5, 2
NS_A, NS_B, NS_C = 3.4445, -4.775, 2.0315
GRAD_SCALE = 2.0 / (B * L * D)

LS = 36
LN2 = float(np.log(2.0))

C_ID, C_ONES, C_BLK64, C_BLK8, C_MASK, C_IOTA, C_SEL = 0, 128, 256, 384, 512, 768, 800
C_N = C_SEL + E * 128


def shape_constants():
    c = np.zeros((P, C_N), np.float32)
    r = np.arange(P)
    c[:, C_ID:C_ID + P] = np.eye(P)
    c[:, C_ONES:C_ONES + P] = 1.0
    c[:, C_BLK64:C_BLK64 + P] = (r[:, None] // DH == r[None] // DH)
    c[:, C_BLK8:C_BLK8 + P] = (r[:, None] // HD == r[None] // HD)
    i, j = r[:, None] % WINDOW, r[None]
    ok = (j >= i) & (j <= i + WINDOW)
    first = ok & ((r[:, None] >= WINDOW) | (j >= WINDOW))
    c[:, C_MASK:C_MASK + P] = np.where(first, 0.0, -1e30)
    c[:, C_MASK + P:C_MASK + 2 * P] = np.where(ok, 0.0, -1e30)
    c[:, C_IOTA:C_IOTA + TPB * E] = np.tile(np.arange(E), TPB)
    for e in range(E):
        c[[e, 32 + e, 64 + e], C_SEL + e * P:C_SEL + (e + 1) * P] = 1.0
    return c


def rotary_tables():
    half = np.arange(0, DH, 2, dtype=np.float32)
    inv = (np.float32(1.0) / np.float32(10000.0) ** (half / np.float32(DH))).astype(np.float32)
    t = np.arange(L, dtype=np.float32)
    fr = (t[:, None] * inv[None]).astype(np.float32).astype(np.float64)
    base = (half + np.float32(0.4 * DH)) / np.float32(1.4 * DH)
    power = (t - L // 2) / np.float32(WINDOW // 2)
    sc = base[None].astype(np.float64) ** power[:, None].astype(np.float64)
    two = lambda a: np.concatenate([a, a], 1).T
    cos, sin, sc = two(np.cos(fr)), two(np.sin(fr)), two(sc)
    sign = np.where(np.arange(DH) < DH // 2, -1.0, 1.0)[:, None]
    tabs = [cos * sc * QK_SCALE, sign * sin * sc * QK_SCALE, cos / sc, sign * sin / sc]
    return np.stack([np.tile(a, (2, 1)) for a in tabs], 1).astype(np.float32)


def position_tables():
    pos = (np.arange(L, dtype=np.float32) / np.float32(L) * np.float32(2 * np.pi)).astype(np.float64)
    t = np.stack([np.sin(pos), np.cos(pos), np.sin(pos / 2), np.cos(pos / 2)])
    return np.tile(t[None], (NH, 1, 1)).astype(np.float32)


START = 1


def at(n, per, k=0):
    return n * per + k


def reuse(n, per, k, depth):
    return at(n, per, k - depth + 1 if k >= depth else 0)


def build(nc, I, out, stop=None):
    ctx = ExitStack()
    with ctx:
        sems = {}

        def s(name):
            if name not in sems:
                sems[name] = ctx.enter_context(nc.semaphore(name))
            return sems[name]

        def sb(name, shape, dt=F32):
            return ctx.enter_context(nc.sbuf_tensor(name, shape, dt))

        PS = ctx.enter_context(nc.psum_tensor("PS", [P, 8, 512], F32))
        q_dram = nc.dram_tensor("q_split", (3, D, B, L), BF16).ap()
        k_dram = nc.dram_tensor("k_split", (3, D, B, L), BF16).ap()
        mq_dram = nc.dram_tensor("mask_q", (NH, MF, L), F32).ap()
        mk_dram = nc.dram_tensor("mask_k", (NH, MF, L), F32).ap()
        o_dram = nc.dram_tensor("heads_out", (2, D, B, L), F32).ap()

        xT = sb("xT", [P, B, L])
        con = sb("con", [P, C_N])
        ident, ones = con[:, C_ID:C_ID + P], con[:, C_ONES:C_ONES + P]
        blk64, blk8 = con[:, C_BLK64:C_BLK64 + P], con[:, C_BLK8:C_BLK8 + P]
        mean_w = sb("mean_w", [P, P])
        ident_b = sb("ident_b", [P, P], BF16)
        mask_b = sb("mask_b", [P, TPB, P], BF16)
        sel_b = sb("sel_b", [P, E, P], BF16)
        col = sb("col", [P, 8])
        c_eps, c_tiny, c_norm, c_1e6, c_one, c_zero, c_neg = (col[:, i:i + 1] for i in range(7))
        fcol = sb("fcol", [P, DEPTH, 16])
        aw = sb("aw", [P, 4, D])
        acol = sb("acol", [P, 8])
        bv_row = sb("bv_row", [P, D])
        sgu = sb("sgu", [P, 2 * FS])
        sdn = sb("sdn", [P, D])
        rw = sb("rw", [P, E])
        mcol = sb("mcol", [P, 2])
        tqkv = sb("tqkv", [P, 3 * D])
        tcol = sb("tcol", [P, 8])
        th_g = sb("th_g", [P, TH])
        th_v = sb("th_v", [P, TH])
        th_pT = sb("th_pT", [P, TH])
        th_p = sb("th_p", [P, 4, D])
        tpw = sb("tpw", [P, D])
        lnc, lnq, lnr, lnt = (sb(n, [P, L]) for n in ("ln_centered", "ln_square", "ln_rstd", "ln_scaled"))
        big = sb("big", [P, 12400])
        arena = sb("arena", [P, 29800])
        memory, taken = [big], [0]

        def stage_memory(m=arena):
            memory[0], taken[0] = m, 0

        def carve(shape, dt=F32):
            n = int(np.prod(shape))
            w = (n + 1) // 2 if dt == BF16 else n
            a = memory[0][:, taken[0]:taken[0] + w]
            taken[0] += w
            assert taken[0] <= memory[0].shape[1], taken
            if dt != F32:
                a = a.bitcast(dt)
            if len(shape) == 1:
                return a
            names = "abcd"[:len(shape)]
            return a.rearrange(f"p ({' '.join(names)}) -> p {' '.join(names)}", **dict(zip(names, shape)))

        stage_memory(big)
        rot = carve([DEPTH, 4, L])
        wqkv = carve([DEPTH, 3 * INNER])
        wswap = carve([DEPTH, 2 * HEADS, 2, DH // 2])
        wo = carve([DEPTH, NCH, D])
        w1 = carve([DEPTH, 2 * HID])
        w2 = carve([DEPTH, 3, D])
        stage_memory(big)
        gu = carve([E, 2 * F])
        dn = carve([E, FCH, D])

        STAGES = ["load", "ffn0", "attn", "ffn1", "moe0", "ttt", "moe1"]
        if stop:
            STAGES = STAGES[:STAGES.index(stop) + 1]
        first_ln = {"ffn0": 0, "attn": 12, "ffn1": 16, "moe0": 28, "ttt": 32, "moe1": 36}

        def x_of(name):
            return B * STAGES.index(name)

        def plain_wait(eng):
            eng.sem_inc(s("passed"), 1)

        def ln_mean(src, bank):
            nc.tensor.matmul(PS[:, bank, :], mean_w[:], src, start=True, stop=True).then_inc(s("ln_sums"), 1)

        def ln_variance(e, bank):
            pe = nc.tensor
            pe.wait_ge(s("ln_squared"), START + e + 1)
            pe.matmul(PS[:, bank, :], mean_w[:], lnq[:], start=True, stop=True).then_inc(s("ln_sums"), 1)

        def ln_pe(src, e, mean_bank, var_bank):
            ln_mean(src, mean_bank)
            ln_variance(e, var_bank)

        def ln_square(e):
            act = nc.scalar
            act.wait_ge(s("ln_centred"), START + e + 1)
            act.activation(lnq[:], lnc[:], ACT.Square).then_inc(s("ln_squared"), 1)

        def ln_rstd(e, var_bank):
            act = nc.scalar
            act.wait_ge(s("ln_sums"), START + at(e, 2, 2))
            act.activation(lnr[:], PS[:, var_bank, :], ACT.Ln, bias=c_eps).then_inc(s("ln_rstd_step"), 1)
            act.wait_ge(s("ln_rstd_step"), START + at(e, 2, 1))
            act.activation(lnr[:], lnr[:], ACT.Exp, scale=-0.5).then_inc(s("ln_rstd_step"), 1)

        def ln_act(e, var_bank):
            ln_square(e)
            ln_rstd(e, var_bank)

        def ln_centre(src, e, mean_bank):
            v = nc.vector
            v.wait_ge(s("ln_sums"), START + at(e, 2, 1))
            v.tensor_tensor(lnc[:], src, PS[:, mean_bank, :], ALU.subtract).then_inc(s("ln_centred"), 1)

        def ln_scale(e, gamma, beta, dst, free=()):
            v = nc.vector
            v.wait_ge(s("ln_rstd_step"), START + at(e, 2, 2))
            v.scalar_tensor_tensor(lnt[:], lnc[:], gamma, lnr[:], ALU.mult, ALU.mult).then_inc(s("ln_scaled_done"), 1)
            v.wait_ge(s("ln_scaled_done"), START + e + 1)
            for name, count in free:
                v.wait_ge(s(name), START + count)
            v.tensor_scalar(dst, lnt[:], beta, None, ALU.add).then_inc(s("ln_done"), 1)

        def ln_dve(src, e, mean_bank, gamma, beta, dst, free=()):
            ln_centre(src, e, mean_bank)
            ln_scale(e, gamma, beta, dst, free)

        stage_memory()
        y = carve([B, L])
        h_pad = carve([WINDOW + L])
        t_cos, t_sin, t_rot, t_rn, t_sq = (carve([2, L]) for _ in range(5))
        t_ln = carve([2, L])
        qs = carve([NCH, L])
        ks = carve([NCH, WINDOW + L])
        vs = carve([2, TPB, INNER])
        pr = carve([2, 4, P])
        pn = carve([2, 4, P])
        pT = carve([2, 4, P])
        nmax, psum_, pinv = (carve([2, 4]) for _ in range(3))
        oT = carve([NCH, L])
        h2 = carve([L])
        ln2 = carve([L])
        gl = carve([2, L])
        hid = carve([3, L])

        PIECES = 2 * NCH

        def ffn_walk(eng, f, enter, project, normalise, project_values, step, tail):
            first = B * DEPTH * f
            enter(first, 0, 0, None)
            for j in range(PIECES + 1):
                if j < PIECES:
                    project(first, 0, j)
                if j:
                    normalise(first, j - 1, f == 0)
            for i in range(2 * TPB):
                project_values(first, 0, i)

            def one(layer, b, nx):
                N = b + B * (DEPTH * f + layer)
                for u in range(UNITS + 3):
                    step(N, u, nx)
                tail(N, layer, b, nx)

            for layer in range(DEPTH):
                with eng.Fori(0, B - 1) as b:
                    one(layer, b, (b + 1 + B * (DEPTH * f + layer), layer, b + 1))
                one(layer, B - 1, (B * (DEPTH * f + layer + 1), layer + 1, 0) if layer + 1 < DEPTH else None)

        def e_input(f, b, prologue):
            return first_ln[f"ffn{f}"] + (0 if prologue else 2 * b - 1)

        def e_hidden(f, layer, b):
            if layer == 0:
                return first_ln[f"ffn{f}"] + (2 * b + 2 if type(b) is not int else 2 * B - 1)
            return b + (first_ln[f"ffn{f}"] + 2 * B)

        def ffn_pe(pe, f):
            def enter(N, layer, b, part):
                if layer == 0:
                    e = e_input(f, b, part is None)
                    if part in (0, None):
                        ln_mean(xT[:, b, :], 5)
                    if part in (1, None):
                        ln_variance(e, 6)

            def project(N, layer, j):
                J = at(N, PIECES, j)
                if j == 0:
                    pe.wait_ge(s("h_ready"), START + at(N, 2, 2))
                pe.wait_ge(s("rot_products"), START + J)
                pe.wait_ge(s("qk_squared"), START + J)
                c = j // 2 + (NCH if j % 2 else 0)
                pe.matmul(PS[:, 5, :], wqkv[:, layer, c * P:(c + 1) * P], h_pad[:, WINDOW:], start=True, stop=True).then_inc(s("proj"), 1)
                w = wswap[:, layer, 2 * c:2 * c + 2, :, :].rearrange("p a b c -> p (a b c)")
                pe.matmul(PS[:, 6, :], w, h_pad[:, WINDOW:], start=True, stop=True).then_inc(s("proj"), 1)

            def normalise(N, j, fresh):
                J = at(N, PIECES, j)
                pe.wait_ge(s("qk_squared"), START + J + 1)
                pe.wait_ge(s("qk_log"), START + J)
                pe.matmul(PS[:, 7, :], blk64, t_sq[:, j % 2, :], start=True, stop=True).then_inc(s("qk_sums"), 1)

            def project_values(N, layer, i):
                off = WINDOW + (i % TPB) * P if i < TPB else (i % TPB) * P
                if i == 0:
                    pe.wait_ge(s("p_exp"), START + at(N, TPB * UNITS))
                if i >= 2:
                    pe.wait_ge(s("v_act" if i % 2 == 0 else "v_dve"), START + at(N, TPB, i // 2))
                pe.matmul(PS[:, i % 2, :], h_pad[:, off:off + P], wqkv[:, layer, 2 * INNER:], start=True,
                          stop=True).then_inc(s("v_proj"), 1)

            def scores(N, u):
                c, par = u // 2, u % 2
                if u == 0:
                    pe.wait_ge(s("qk_scaled"), START + at(N, PIECES, PIECES))
                    pe.wait_ge(s("v_act"), START + at(N, TPB, TPB))
                    pe.wait_ge(s("v_dve"), START + at(N, TPB, TPB))
                    pe.wait_ge(s("hid_ready"), START + at(N, 3))
                if u >= 2:
                    pe.wait_ge(s("p_exp"), START + at(N, TPB * UNITS, TPB * (u - 1)))
                pe.matmul(PS[:, par, :], ident_b[:], mask_b[:].rearrange("p a b -> p (a b)"), start=True, stop=False,
                          skip_group_check=True)
                r = slice(DH * par, DH * par + DH)
                for t in range(TPB):
                    for w in range(2):
                        a = t * P + w * WINDOW
                        mm = pe.matmul(PS[w * WINDOW:(w + 1) * WINDOW, par, t * P:(t + 1) * P], qs[r, c, a:a + WINDOW],
                                       ks[r, c, a:a + 2 * WINDOW], start=False, stop=True, skip_group_check=True)
                mm.then_inc(s("scores_ready"), 1)

            def turned(N, u):
                pe.wait_ge(s("p_normed"), START + at(N, UNITS, u + 1))
                if u >= 2:
                    pe.wait_ge(s("pT_ready"), START + at(N, UNITS, u - 1))
                for t in range(TPB):
                    tr = pe.transpose(PS[:, 2 + u % 2, t * P:(t + 1) * P], pn[:, u % 2, t, :], ident)
                tr.then_inc(s("pT_done"), 1)

            def values(N, u):
                c, par = u // 2, u % 2
                pe.wait_ge(s("pT_ready"), START + at(N, UNITS, u + 1))
                if u == 0:
                    pe.wait_ge(s("y_added"), START + at(N, 1))
                elif par == 0:
                    pe.wait_ge(s("oT_ready"), START + at(N, NCH, c))
                for t in range(TPB):
                    for w in range(2):
                        mm = pe.matmul(PS[DH * par:DH * par + DH, 4, t * P + w * WINDOW:t * P + (w + 1) * WINDOW],
                                       vs[:, 1 - w, t, u * DH:(u + 1) * DH], pT[:, par, t, w * WINDOW:(w + 1) * WINDOW],
                                       start=True, stop=True)
                mm.then_inc(s("pv_done"), 1)

            def step(N, u, nx):
                if u < UNITS:
                    scores(N, u)
                if nx:
                    if u < 2:
                        enter(*nx, u)
                    if 2 <= u < PIECES + 2:
                        project(nx[0], nx[1], u - 2)
                    if 3 <= u < PIECES + 3:
                        normalise(nx[0], u - 3, False)
                if 1 <= u <= UNITS:
                    turned(N, u - 1)
                if 2 <= u <= UNITS + 1:
                    values(N, u - 2)

            def tail(N, layer, b, nx):
                e = e_hidden(f, layer, b)

                def fill(*pieces):
                    for i in pieces if nx else ():
                        project_values(nx[0], nx[1], i)

                pe.wait_ge(s("oT_ready"), START + at(N, NCH, NCH))
                for c in range(NCH):
                    mm = pe.matmul(PS[:, 2, :], wo[:, layer, c, :], oT[:, c, :], start=c == 0, stop=c == NCH - 1)
                mm.then_inc(s("wo_ready"), 1)
                fill(0, 1, 2)
                pe.wait_ge(s("h2_ready"), START + at(N, 2, 2))
                ln_mean(h2[:], 3)
                fill(3, 4)
                ln_variance(e, 4)
                fill(5, 6, 7)
                pe.wait_ge(s("ln_done"), START + e + 1)
                for c, (o, n) in enumerate(HCH):
                    if c >= 2:
                        pe.wait_ge(s("hid_ready"), START + at(N, 3, c - 1))
                    pe.matmul(PS[0:n, 2 + c % 2, :], w1[:, layer, o:o + n], ln2[:], start=True, stop=True).then_inc(s("ffn_proj"), 1)
                    pe.matmul(PS[0:n, 5 + c % 2, :], w1[:, layer, HID + o:HID + o + n], ln2[:], start=True,
                              stop=True).then_inc(s("ffn_proj"), 1)
                for c, (o, n) in enumerate(HCH):
                    pe.wait_ge(s("hid_ready"), START + at(N, 3, c + 1))
                    mm = pe.matmul(PS[:, 4, :], w2[0:n, layer, c, :], hid[0:n, c, :], start=c == 0, stop=c == 2)
                mm.then_inc(s("ffn_out"), 1)

            ffn_walk(pe, f, enter, project, normalise, project_values, step, tail)

        def ffn_act(act, f):
            def enter(N, layer, b, part):
                e = e_input(f, b, part is None)
                if layer == 0 and part in (0, None):
                    ln_square(e)
                if part == 0:
                    return
                if layer == 0:
                    ln_rstd(e, 6)
                    act.wait_ge(s("ln_done"), START + e + 1)
                else:
                    act.wait_ge(s("y_added"), START + at(N, 1, -3))
                act.wait_ge(s("v_proj"), START + at(N, 2 * TPB))
                plain_wait(act)
                act.activation(h_pad[64:128, WINDOW + 1:WINDOW + L], y[64:128, b, 0:L - 1], ACT.Copy).then_inc(s("h_ready"), 1)

            def project(N, layer, j):
                act.wait_ge(s("rot_cos"), START + at(N, PIECES, j + 1))
                act.wait_ge(s("qk_sums"), START + reuse(N, PIECES, j, 2))
                act.activation(t_sq[:, j % 2, :], PS[:, 5, :], ACT.Square).then_inc(s("qk_squared"), 1)

            def normalise(N, j, fresh):
                J = at(N, PIECES, j)
                act.wait_ge(s("qk_sums"), START + J + 1)
                act.wait_ge(s("qk_rnorm"), START + reuse(N, PIECES, j, 2))
                act.activation(t_ln[:, j % 2, :], PS[:, 7, :], ACT.Ln, bias=c_tiny, scale=2.0 ** LS).then_inc(s("qk_log"), 1)
                act.wait_ge(s("qk_log"), START + J + 1)
                act.wait_ge(s("qk_scaled"), START + reuse(N, PIECES, j, 2))
                act.activation(t_rn[:, j % 2, :], t_ln[:, j % 2, :], ACT.Exp, bias=c_norm, scale=-0.5).then_inc(s("qk_rnorm"), 1)

            def project_values(N, layer, i):
                if i % 2 == 0:
                    if i == 0:
                        act.wait_ge(s("pv_done"), START + at(N, UNITS))
                    act.wait_ge(s("v_proj"), START + at(N, 2 * TPB, i + 1))
                    act.activation(vs[:, i // TPB, i % TPB, :], PS[:, 0, :], ACT.Copy).then_inc(s("v_act"), 1)

            def step(N, u, nx):
                if u < UNITS:
                    act.wait_ge(s("nmax_ready"), START + at(N, UNITS, u + 1))
                    act.wait_ge(s("p_normed"), START + reuse(N, UNITS, u, 2))
                    for t in range(TPB):
                        act.activation(pr[:, u % 2, t, :], PS[:, u % 2, t * P:(t + 1) * P], ACT.Exp,
                                       bias=nmax[:, u % 2, t:t + 1],
                                       accum_out=psum_[:, u % 2, t:t + 1]).then_inc(s("p_exp"), 1)
                if nx:
                    if u < 2:
                        enter(*nx, u)
                    if 2 <= u < PIECES + 2:
                        project(nx[0], nx[1], u - 2)
                    if 3 <= u < PIECES + 3:
                        normalise(nx[0], u - 3, False)
                if u >= 3 and u % 2 and u <= UNITS + 1:
                    c = (u - 3) // 2
                    act.wait_ge(s("pv_done"), START + at(N, UNITS, 2 * c + 2))
                    if c == 0:
                        act.wait_ge(s("wo_ready"), START + at(N, 1))
                    act.activation(oT[:, c, :], PS[:, 4, :], ACT.Copy).then_inc(s("oT_ready"), 1)

            def tail(N, layer, b, nx):
                e = e_hidden(f, layer, b)

                def fill(i):
                    if nx:
                        project_values(nx[0], nx[1], i)

                fill(0)
                act.wait_ge(s("wo_added"), START + at(N, 1, 1))
                plain_wait(act)
                act.activation(h2[64:128, 1:L], y[64:128, b, 0:L - 1], ACT.Copy).then_inc(s("h2_ready"), 1)
                fill(2)
                ln_square(e)
                fill(4)
                ln_rstd(e, 4)
                fill(6)
                for c, (o, n) in enumerate(HCH):
                    act.wait_ge(s("ffn_proj"), START + at(N, 6, 2 * c + 2))
                    act.wait_ge(s("hid_ready"), START + reuse(N, 3, c, 2))
                    act.activation(gl[0:n, c % 2, :], PS[0:n, 5 + c % 2, :], ACT.Gelu,
                                   bias=fcol[0:n, layer, 10 + c:11 + c]).then_inc(s("gelu_ready"), 1)
                act.preload_act_table_set("natural_log_exp_and_others")

            act.preload_act_table_set("natural_log_exp_and_others")
            ffn_walk(act, f, enter, project, normalise, project_values, step, tail)

        def ffn_dve(v, f):
            def enter(N, layer, b, part):
                e = e_input(f, b, part is None)
                if layer == 0 and part in (0, None):
                    ln_centre(xT[:, b, :], e, 5)
                if part == 0:
                    return
                if layer == 0:
                    ln_scale(e, c_one, c_zero, y[:, b, :])
                    v.wait_ge(s("ln_done"), START + e + 1)
                else:
                    v.wait_ge(s("y_added"), START + at(N, 1, -3))
                v.wait_ge(s("v_proj"), START + at(N, 2 * TPB))
                plain_wait(v)
                v.tensor_copy(h_pad[0:64, WINDOW:], y[0:64, b, :]).then_inc(s("h_ready"), 1)

            def project(N, layer, j):
                tab = 2 * (j % 2)
                v.wait_ge(s("qk_rotated"), START + reuse(N, PIECES, j, 2))
                v.wait_ge(s("proj"), START + at(N, 2 * PIECES, 2 * j + 1))
                v.tensor_tensor(t_cos[:, j % 2, :], PS[:, 5, :], rot[:, layer, tab, :], ALU.mult).then_inc(s("rot_cos"), 1)
                v.wait_ge(s("proj"), START + at(N, 2 * PIECES, 2 * j + 2))
                v.tensor_tensor(t_sin[:, j % 2, :], PS[:, 6, :], rot[:, layer, tab + 1, :],
                                ALU.mult).then_inc(s("rot_products"), 1)

            def normalise(N, j, fresh):
                J, c = at(N, PIECES, j), j // 2
                v.wait_ge(s("qk_rotated"), START + J + 1)
                v.wait_ge(s("qk_rnorm"), START + J + 1)
                if not fresh:
                    v.wait_ge(s("scores_ready"), START + at(N, UNITS, 2 * c + 2 - UNITS))
                dst = qs[:, c, :] if j % 2 == 0 else ks[:, c, WINDOW:]
                v.scalar_tensor_tensor(dst, t_rn[:, j % 2, :], 1e12, t_rot[:, j % 2, :], ALU.min,
                                       ALU.mult).then_inc(s("qk_scaled"), 1)

            def project_values(N, layer, i):
                if i % 2:
                    if i == 1:
                        v.wait_ge(s("pv_done"), START + at(N, UNITS))
                    v.wait_ge(s("v_proj"), START + at(N, 2 * TPB, i + 1))
                    v.tensor_copy(vs[:, i // TPB, i % TPB, :], PS[:, 1, :]).then_inc(s("v_dve"), 1)

            def step(N, u, nx):
                if u < UNITS:
                    v.wait_ge(s("scores_ready"), START + at(N, UNITS, u + 1))
                    v.wait_ge(s("p_exp"), START + at(N, TPB * UNITS, TPB * (u - 1) if u >= 2 else 0))
                    v.tensor_reduce(nmax[:, u % 2, :], PS[:, u % 2, :].rearrange("p (a b) -> p a b", a=TPB), AX.X,
                                    ALU.max, negate=True).then_inc(s("nmax_ready"), 1)
                if nx:
                    if u == 0:
                        enter(*nx, u)
                    if 2 <= u < PIECES + 2:
                        project(nx[0], nx[1], u - 2)
                if u < UNITS:
                    v.wait_ge(s("p_exp"), START + at(N, TPB * UNITS, TPB * u + TPB))
                    v.wait_ge(s("p_normed"), START + reuse(N, UNITS, u, 2))
                    v.reciprocal(pinv[:, u % 2, :], psum_[:, u % 2, :]).then_inc(s("pinv_ready"), 1)
                if 1 <= u <= UNITS:
                    w = u - 1
                    v.wait_ge(s("pT_done"), START + at(N, UNITS, w + 1))
                    v.wait_ge(s("pv_done"), START + reuse(N, UNITS, w, 2))
                    v.tensor_copy(pT[:, w % 2, :, :].rearrange("p a b -> p (a b)"), PS[:, 2 + w % 2, :]).then_inc(s("pT_ready"), 1)
                if nx and u == 1:
                    enter(*nx, u)
                if nx and 3 <= u < PIECES + 3:
                    normalise(nx[0], u - 3, False)

            def tail(N, layer, b, nx):
                e = e_hidden(f, layer, b)

                def fill(i):
                    if nx:
                        project_values(nx[0], nx[1], i)

                v.wait_ge(s("wo_ready"), START + at(N, 1, 1))
                v.tensor_tensor(y[:, b, :], y[:, b, :], PS[:, 2, :], ALU.add).then_inc(s("wo_added"), 1)
                v.wait_ge(s("wo_added"), START + at(N, 1, 1))
                plain_wait(v)
                v.tensor_copy(h2[0:64], y[0:64, b, :]).then_inc(s("h2_ready"), 1)
                fill(1)
                v.wait_ge(s("h2_ready"), START + at(N, 2, 2))
                ln_centre(h2[:], e, 3)
                fill(3)
                fill(5)
                ln_scale(e, fcol[:, layer, 4:5], fcol[:, layer, 5:6], ln2)
                fill(7)
                for c, (o, n) in enumerate(HCH):
                    v.wait_ge(s("gelu_ready"), START + at(N, 3, c + 1))
                    v.scalar_tensor_tensor(hid[0:n, c, :], PS[0:n, 2 + c % 2, :], fcol[0:n, layer, 7 + c:8 + c],
                                           gl[0:n, c % 2, :], ALU.add, ALU.mult).then_inc(s("hid_ready"), 1)
                v.wait_ge(s("ffn_out"), START + at(N, 1, 1))
                v.scalar_tensor_tensor(y[:, b, :], PS[:, 4, :], fcol[:, layer, 6:7], y[:, b, :], ALU.add,
                                       ALU.add).then_inc(s("y_added"), 1)
                if layer == DEPTH - 1:
                    v.wait_ge(s("y_added"), START + at(N, 1, 1))
                    v.scalar_tensor_tensor(xT[:, b, :], y[:, b, :], 0.5, xT[:, b, :], ALU.mult, ALU.add).then_inc(s("x_ready"), 1)

            ffn_walk(v, f, enter, project, normalise, project_values, step, tail)

        def ffn_pool(g, f):
            def project(N, layer, j):
                g.wait_ge(s("rot_cos"), START + at(N, PIECES, j + 1))
                g.wait_ge(s("rot_products"), START + at(N, PIECES, j + 1))
                g.wait_ge(s("qk_scaled"), START + reuse(N, PIECES, j, 2))
                g.tensor_tensor(t_rot[:, j % 2, :], t_cos[:, j % 2, :], t_sin[:, j % 2, :], ALU.add).then_inc(s("qk_rotated"), 1)

            def step(N, u, nx):
                if nx and 2 <= u < PIECES + 2:
                    project(nx[0], nx[1], u - 2)
                if u < UNITS:
                    g.wait_ge(s("pinv_ready"), START + at(N, UNITS, u + 1))
                    g.wait_ge(s("pT_done"), START + reuse(N, UNITS, u, 2))
                    g.tensor_tensor(pn[:, u % 2, :, :], pr[:, u % 2, :, :],
                                    pinv[:, u % 2, :].unsqueeze(2).broadcast_to([P, TPB, P]), ALU.mult).then_inc(s("p_normed"), 1)

            def nothing(*_):
                pass

            ffn_walk(g, f, nothing, project, nothing, nothing, step, nothing)

        def ffn_zero_pads(g, f):
            g.wait_ge(s("x_ready"), START + x_of(f"ffn{f}"))
            if f == 0:
                g.wait_ge(s("mask_stored"), START + 32)
            g.memset(h_pad[:, 0:WINDOW + 1], 0.0).then_inc(s("pads_zero"), 1)
            g.memset(ks[:, :, 0:WINDOW], 0.0).then_inc(s("pads_zero"), 1)
            g.memset(h2[:, 0:1], 0.0).then_inc(s("pads_zero"), 1)

        stage_memory()
        pos = carve([4, L])
        m_q = carve([MF, L])
        m_k = carve([MF, L])
        m_t = carve([6, L])
        ang, turns, ang_f, sc = (carve([8]) for _ in range(4))
        turns_i = turns.bitcast(I32)
        phase = carve([8])

        def load_sync(sp):
            for name, dst in (("xT", xT[:]), ("con", con[:]), ("fcol", fcol[:]), ("wqkv", wqkv), ("wswap", wswap)):
                sp.dma_start(dst, I[name]).then_inc(s("first_loads"), 16)
            for layer in range(DEPTH):
                sp.dma_start(rot[:, layer, :, :], I["rot"]).then_inc(s("first_loads"), 16)
            sp.dma_start(phase[0:NH, :], I["phase"]).then_inc(s("phase_loaded"), 16)
            sp.dma_start(pos[0:NH, :, :], I["pos"]).then_inc(s("phase_loaded"), 16)
            sp.dma_start(wo, I["wo"]).then_inc(s("ffn_loaded"), 16)
            sp.dma_start(w1, I["w1"]).then_inc(s("ffn_loaded"), 16)
            sp.dma_start(w2, I["w2"]).then_inc(s("ffn_loaded"), 16)
            for name, dst in (("aw", aw), ("acol", acol), ("bv_row", bv_row)):
                sp.dma_start(dst[:], I[name]).then_inc(s("attn_loaded"), 16)
            sp.wait_ge(s("mask_rows"), START + 2)
            sp.dma_start(mq_dram.rearrange("h f n -> h (f n)"), m_q[0:NH].rearrange("p a b -> p (a b)")).then_inc(s("mask_stored"), 16)
            sp.dma_start(mk_dram.rearrange("h f n -> h (f n)"), m_k[0:NH].rearrange("p a b -> p (a b)")).then_inc(s("mask_stored"), 16)
            for name, dst in (("sgu", sgu), ("sdn", sdn), ("rw", rw), ("mcol", mcol)):
                sp.dma_start(dst[:], I[name]).then_inc(s("moe_loaded"), 16)
            for name, dst in (("tqkv", tqkv), ("tcol", tcol), ("th_g", th_g), ("th_v", th_v), ("th_pT", th_pT),
                              ("th_p", th_p), ("tpw", tpw)):
                sp.dma_start(dst[:], I[name]).then_inc(s("ttt_loaded"), 16)

        def load_experts(sp):
            sp.wait_ge(s("x_ready"), START + x_of("moe0"))
            for e in range(E):
                sp.dma_start(gu[:, e, :], I["gu"][:, e, :]).then_inc(s(f"experts{e // 2}_loaded"), 16)
                sp.dma_start(dn[:, e, :, :], I["dn"][:, e, :, :]).then_inc(s(f"experts{e // 2}_loaded"), 16)

        def load_dve(v):
            for i, val in enumerate((LN_EPS, 2.0 ** -60, 0.5 * LS * LN2, 1e-6, 1.0, 0.0, -0.5 * LS * LN2)):
                v.memset(col[:, i:i + 1], val).then_inc(s("columns"), 1)
            v.wait_ge(s("columns"), START + 7)
            v.wait_ge(s("first_loads"), START + 112)
            v.tensor_scalar(mean_w[:], ones, 1.0 / D, None, ALU.mult).then_inc(s("consts"), 1)
            v.tensor_copy(ident_b[:], ident).then_inc(s("consts"), 1)
            m = con[:, C_MASK:C_MASK + 2 * P].rearrange("p (a b) -> p a b", a=2)
            for t in range(TPB):
                v.tensor_copy(mask_b[:, t, :], m[:, 1 if t else 0, :]).then_inc(s("consts"), 1)
            v.tensor_copy(sel_b[:].rearrange("p a b -> p (a b)"), con[:, C_SEL:]).then_inc(s("consts"), 1)
            v.tensor_copy(col[:, 7:8], c_one).then_inc(s("x_ready"), B)
            for layer in range(DEPTH):
                for i in range(4):
                    v.tensor_scalar(rot[:, layer, i, :], rot[:, layer, i, :], fcol[:, layer, i:i + 1], None,
                                    ALU.mult).then_inc(s("rot_scaled"), 1)
            mask_factors(v)

        def mask_factors(v):
            steps = [0]

            def then(ins):
                steps[0] += 1
                ins.then_inc(s("mask_step"), 1)
                v.wait_ge(s("mask_step"), START + steps[0])

            h = slice(0, NH)
            pi = float(np.pi)
            two_pi_hi = float(np.float32(2 * np.pi))
            two_pi_lo = float(2 * np.pi - two_pi_hi)
            v.wait_ge(s("phase_loaded"), START + 32)
            then(v.tensor_copy(ang[h, 0:3], phase[h, 0:3]))
            then(v.tensor_scalar(ang[h, 3:6], phase[h, 0:3], pi / 2, None, ALU.add))
            then(v.tensor_scalar(ang_f[h, 0:6], ang[h, 0:6], 1.0 / (2 * pi), None, ALU.mult))
            then(v.tensor_copy(turns_i[h, 0:6], ang_f[h, 0:6]))
            then(v.tensor_copy(ang_f[h, 0:6], turns_i[h, 0:6]))
            for part in (two_pi_hi, two_pi_lo):
                then(v.scalar_tensor_tensor(ang[h, 0:6], ang_f[h, 0:6], -part, ang[h, 0:6], ALU.mult, ALU.add))
            for op, bound, turn in ((ALU.is_gt, pi, -two_pi_hi), (ALU.is_lt, -pi, two_pi_hi)):
                then(v.tensor_scalar(ang_f[h, 0:6], ang[h, 0:6], bound, turn, op, ALU.mult))
                then(v.tensor_tensor(ang[h, 0:6], ang[h, 0:6], ang_f[h, 0:6], ALU.add))
            then(v.tensor_scalar(ang[h, 0:6], ang[h, 0:6], 3.1415925, -3.1415925, ALU.min, ALU.max))
            v.tensor_copy(sc[h, 6:7], ang[h, 0:1]).then_inc(s("angles"), 1)
            v.wait_ge(s("sines"), START + 1)
            s0, s1, s2, c0, c1, c2 = (sc[h, i:i + 1] for i in range(6))
            sa, ca, sh, ch = (pos[h, i, :] for i in range(4))

            def angle_sum(dst, t, a, x, b, y, op):
                then(v.tensor_scalar(t, a, x, None, ALU.mult))
                then(v.scalar_tensor_tensor(dst, b, y, t, ALU.mult, op))

            t = m_t[h, 5, :]
            sin_q, cos_q, sin_z, cos_z, sin_k = m_q[h, 0, :], m_t[h, 1, :], m_t[h, 2, :], m_q[h, 1, :], m_t[h, 4, :]
            angle_sum(sin_q, t, ca, s0, sa, c0, ALU.add)
            angle_sum(cos_q, t, sa, s0, ca, c0, ALU.subtract)
            angle_sum(cos_z, t, sh, s2, ch, c2, ALU.subtract)
            angle_sum(sin_z, t, ch, s2, sh, c2, ALU.add)
            angle_sum(m_k[h, 0, :], t, sa, s1, ca, c1, ALU.subtract)
            angle_sum(sin_k, t, ca, s1, sa, c1, ALU.add)
            then(v.tensor_scalar(m_q[h, 2, :], sin_z, -1.0, None, ALU.mult))
            then(v.tensor_tensor(m_q[h, 3, :], cos_q, sin_z, ALU.mult))
            then(v.tensor_tensor(m_q[h, 4, :], cos_q, cos_z, ALU.mult))
            then(v.tensor_scalar(m_q[h, 5, :], sa, 0.0, phase[h, 3:4], ALU.mult, ALU.subtract))
            then(v.tensor_tensor(m_k[h, 1, :], sin_k, ch, ALU.mult))
            then(v.tensor_tensor(m_k[h, 2, :], sin_k, sh, ALU.mult))
            then(v.tensor_copy(m_k[h, 3, :], ch))
            then(v.tensor_copy(m_k[h, 4, :], sh))
            v.memset(m_k[h, 5, :], 1.0).then_inc(s("mask_rows"), 1)
            v.wait_ge(s("attn_loaded"), START + 48)
            then(v.tensor_scalar(acol[:, 4:5], acol[:, 3:4], 1e-6, -1.0, ALU.add, ALU.mult))
            then(v.tensor_scalar(acol[:, 6:7], acol[:, 0:1], A_SCALE, None, ALU.mult))
            v.reciprocal(acol[:, 5:6], acol[:, 4:5]).then_inc(s("mask_rows"), 1)

        def load_act(act):
            act.wait_ge(s("angles"), START + 1)
            act.activation(sc[0:NH, 0:6], ang[0:NH, 0:6], ACT.Sin).then_inc(s("sines"), 1)
            act.wait_ge(s("columns"), START + 7)
            act.wait_ge(s("consts"), START + 7)

        stage_memory()
        xn = carve([L])
        f_qk = carve([2, L])
        rest = carve([2, 2, L])
        parts = carve([2, 3, L], BF16)
        v_all = carve([B * TPB, D])
        v_head = carve([2, B * TPB, 2 * HD])
        q_st = [carve([B, L], BF16) for _ in range(2)]
        k_st = [carve([B, L], BF16) for _ in range(2)]
        mq_st = [carve([L]) for _ in range(2)]
        mk_st = [carve([L]) for _ in range(2)]
        mk = carve([2, TPB, L])
        pp = carve([2, TPB, L])
        ppT = carve([TPB, L])
        a_nmax = carve([2, TPB])
        o_sb = carve([2, B, P])
        o_all, s_all = pp[:, 0, :, :], pp[:, 1, :, :]
        att = f_qk
        inv = rest[:, 0, :, :]

        def attn_proj_pe(pe):
            pe.wait_ge(s("x_ready"), START + x_of("attn"))
            pe.wait_ge(s("attn_loaded"), START + 48)
            with pe.Fori(0, B) as b:
                e = b + first_ln["attn"]
                ln_pe(xT[:, b, :], e, 4, 5)
                pe.wait_ge(s("ln_done"), START + e + 1)
                pe.wait_ge(s("a_biased"), START + at(b, 2))
                for i in range(2):
                    pe.matmul(PS[:, i, :], aw[:, i, :], xn, start=True, stop=True).then_inc(s("a_proj"), 1)
                pe.wait_ge(s("a_values"), START + at(b, 1))
                for t in range(TPB):
                    mm = pe.matmul(PS[:, 2, t * P:(t + 1) * P], xn[:, t * P:(t + 1) * P], aw[:, 2, :], start=True, stop=True)
                mm.then_inc(s("a_vproj"), 1)

        def attn_proj_act(act):
            act.wait_ge(s("x_ready"), START + x_of("attn"))
            with act.Fori(0, B) as b:
                e = b + first_ln["attn"]
                ln_act(e, 5)
                for i in range(2):
                    act.wait_ge(s("a_proj"), START + at(b, 2, i + 1))
                    act.wait_ge(s("a_split"), START + at(b, 10))
                    act.activation(f_qk[:, i, :], PS[:, i, :], ACT.Identity, bias=acol[:, 6:7] if i == 0 else acol[:, 1:2],
                                   scale=A_SCALE if i == 0 else 1.0).then_inc(s("a_biased"), 1)

        def attn_proj_dve(v):
            v.wait_ge(s("x_ready"), START + x_of("attn"))
            with v.Fori(0, B) as b:
                e = b + first_ln["attn"]
                ln_dve(xT[:, b, :], e, 4, c_one, c_zero, xn, free=[("a_vproj", at(b, 1))])
                v.wait_ge(s("a_vproj"), START + at(b, 1, 1))
                v.tensor_tensor(v_all[:, bass.ds(b * TPB, TPB), :], PS[:, 2, :].rearrange("p (a b) -> p a b", a=TPB),
                                bv_row[:].unsqueeze(1).broadcast_to([P, TPB, P]), ALU.add).then_inc(s("a_values"), 1)
                v.wait_ge(s("parts_stored"), START + at(b, 96))
                for st in range(5):
                    for i in range(2):
                        if st == 0:
                            v.wait_ge(s("a_biased"), START + at(b, 2, i + 1))
                        else:
                            v.wait_ge(s("a_split"), START + at(b, 10, 2 * (st - 1) + i + 1))
                        src = f_qk[:, i, :] if st < 2 else rest[:, i, (st - 2) // 2, :]
                        if st % 2 == 0:
                            ins = v.tensor_copy(parts[:, i, st // 2, :], src)
                        else:
                            ins = v.tensor_tensor(rest[:, i, st // 2, :], src, parts[:, i, st // 2, :], ALU.subtract)
                        ins.then_inc(s("a_split"), 1)
            for hp in range(2):
                v.memset(v_head[:, hp, :, HD:], 1.0).then_inc(s("a_values"), 1)

        def attn_proj_sync(sp):
            with sp.Fori(0, B) as b:
                sp.wait_ge(s("a_split"), START + at(b, 10, 10))
                for i, dst in enumerate((q_dram, k_dram)):
                    for part in range(3):
                        sp.dma_start(dst[part, :, b, :], parts[:, i, part, :]).then_inc(s("parts_stored"), 16)

        HEADS_PER_PASS = 2
        STEPS = HEADS_PER_PASS * B
        PASSES = NH // HEADS_PER_PASS
        OUT_ROWS = 32
        STORES = 16 * 2 * TPB
        MASK_OPS = 5

        def attn_sync(sp):
            sp.wait_ge(s("parts_stored"), START + B * 96)
            sp.wait_ge(s("mask_stored"), START + 32)

            def load_head(i, hp, copied=None):
                h = i * HEADS_PER_PASS + hp
                if copied is not None:
                    sp.wait_ge(s("o_copied"), START + copied)
                for st, src, split in ((q_st[hp], q_dram, SPLIT_Q), (k_st[hp], k_dram, SPLIT_K)):
                    for g, part in enumerate(split):
                        sp.dma_start(st[g * HD:(g + 1) * HD], src[part, bass.ds(h * HD, HD), :, :]).then_inc(s(f"head{hp}_loaded"), 16)

            def load_mask_factors(i, hp, copied=None):
                h = i * HEADS_PER_PASS + hp
                if copied is not None:
                    sp.wait_ge(s("o_copied"), START + copied)
                sp.dma_start(mq_st[hp][0:MF], mq_dram[bass.ds(h, 1), :, :].rearrange("a f n -> (a f) n")).then_inc(s(f"factors{hp}_loaded"), 16)
                sp.dma_start(mk_st[hp][0:MF], mk_dram[bass.ds(h, 1), :, :].rearrange("a f n -> (a f) n")).then_inc(s(f"factors{hp}_loaded"), 16)

            def store(i, hp):
                h = i * HEADS_PER_PASS + hp
                sp.wait_ge(s("o_copied"), START + at(i, STEPS, B * (hp + 1)))
                for t in range(TPB):
                    for w in range(2):
                        r = OUT_ROWS * t + w * HD
                        sp.dma_start(o_dram[w, bass.ds(h * HD, HD), :, t * P:(t + 1) * P], o_sb[r:r + HD, hp, :, :]).then_inc(s("o_stored%d" % hp), 16)

            for hp in range(HEADS_PER_PASS):
                load_mask_factors(0, hp)
                load_head(0, hp)

            def one(i, last):
                for hp in range(HEADS_PER_PASS):
                    if not last:
                        load_mask_factors(i + 1, hp, at(i, STEPS, B * hp + 1))
                        load_head(i + 1, hp, at(i, STEPS, B * hp + 2))
                    store(i, hp)

            with sp.Fori(0, PASSES - 1) as i:
                one(i, False)
            one(PASSES - 1, True)
            sp.wait_ge(s("o_stored0"), START + STORES * PASSES)
            sp.wait_ge(s("o_stored1"), START + STORES * PASSES)
            sp.dma_start(o_all, o_dram[0]).then_inc(s("o_loaded"), 16)
            sp.dma_start(s_all, o_dram[1]).then_inc(s("o_loaded"), 16)

        def stepping(eng, scored, quarter, values, turned):
            for tile in range(TPB):
                quarter(0, tile)
            for st in range(2):
                scored(0, st)
                quarter(0, st + TPB)
            turned(0, 0)

            def one(i, last):
                def of(k):
                    return (i, k) if k < STEPS else (i + 1, k - STEPS)
                for st in range(STEPS):
                    if not (last and st + 2 >= STEPS):
                        scored(*of(st + 2))
                        if not (last and st + 2 + TPB >= STEPS):
                            quarter(*of(st + 2 + TPB))
                    values(i, st)
                    if not (last and st + 1 >= STEPS):
                        turned(*of(st + 1))

            with eng.Fori(0, PASSES - 1) as i:
                one(i, False)
            one(PASSES - 1, True)

        def nothing(i, st):
            pass

        def attn_pe(pe):
            pe.wait_ge(s("a_biased"), START + 2 * B)
            pe.wait_ge(s("a_values"), START + B + 2)

            def scored(i, st):
                hp, b = st // B, st % B
                if b == 0:
                    pe.wait_ge(s(f"head{hp}_loaded"), START + at(i, 12 * 16, 12 * 16))
                for t in range(TPB):
                    pe.wait_ge(s("a_exp"), START + at(i, TPB * STEPS, TPB * (st - 1) + t + 1) if st or type(i) is not int or i else START)
                    pe.matmul(PS[:, t, :], q_st[hp][0:KS, b, t * P:(t + 1) * P], k_st[hp][0:KS, b, :], start=True,
                              stop=True).then_inc(s("a_scores"), 1)

            def quarter(i, q):
                hp, tile = q // TPB, q % TPB
                if tile == 0:
                    pe.wait_ge(s(f"factors{hp}_loaded"), START + at(i, 32, 32))
                pe.wait_ge(s("mask_clamped"), START + at(i, STEPS, q))
                pe.matmul(PS[:, 7, :], mq_st[hp][0:MF, tile * P:(tile + 1) * P], mk_st[hp][0:MF, :], start=True,
                          stop=True).then_inc(s("mask_arg"), 1)

            def turned(i, st):
                for t in range(TPB):
                    if t % 2 == 0:
                        pe.wait_ge(s("a_masked"), START + at(i, 2 * STEPS, 2 * st + t // 2 + 1))
                    pe.wait_ge(s("ppT_ready"), START + at(i, TPB * STEPS, TPB * st + t - 1) if st or t or type(i) is not int else START)
                    for kt in range(TPB):
                        tr = pe.transpose(PS[:, 4 + t % 2, kt * P:(kt + 1) * P], pp[:, st % 2, t, kt * P:(kt + 1) * P], ident)
                    tr.then_inc(s("a_transposed"), 1)

            def values(i, st):
                hp, b = st // B, st % B
                pe.wait_ge(s("ppT_ready"), START + at(i, TPB * STEPS, TPB * st + TPB))
                pe.wait_ge(s("v_head_ready"), START + at(i, HEADS_PER_PASS, hp + 1))
                pe.wait_ge(s("o_copied"), START + at(i, STEPS, st))
                for kt in range(TPB):
                    for t in range(TPB):
                        mm = pe.matmul(PS[OUT_ROWS * t:OUT_ROWS * t + 2 * HD, 6, 0:P], v_head[:, hp, b * TPB + kt, :],
                                       ppT[:, kt, t * P:(t + 1) * P], start=kt == 0, stop=kt == TPB - 1)
                mm.then_inc(s("a_pv"), 1)

            stepping(pe, scored, quarter, values, turned)

        def attn_act(act):
            act.wait_ge(s("mask_rows"), START + 2)

            def scored(i, st):
                for t in range(TPB):
                    if t == 0:
                        act.wait_ge(s("a_nmax"), START + at(i, STEPS, st + 1))
                        if st >= 2 or type(i) is not int or i:
                            act.wait_ge(s("a_transposed"), START + at(i, TPB * STEPS, TPB * (st - 1)))
                    act.activation(pp[:, st % 2, t, :], PS[:, t, :], ACT.Exp, bias=a_nmax[:, st % 2, t:t + 1]).then_inc(s("a_exp"), 1)

            def quarter(i, q):
                hp, tile = q // TPB, q % TPB
                act.wait_ge(s("mask_clamped"), START + at(i, STEPS, q + 1))
                z = mk[:, hp, tile, :]
                for k, (func, bias, scale) in enumerate(((ACT.Exp, 0.0, 1.0), (ACT.Ln, 1.0, 1.0), (ACT.Exp, 0.0, -1.0),
                                                         (ACT.Ln, c_1e6, 1.0), (ACT.Exp, 0.0, 0.3))):
                    if k:
                        act.wait_ge(s("mask_stage"), START + at(i, MASK_OPS * STEPS, MASK_OPS * q + k))
                    act.activation(z, z, func, bias=bias, scale=scale).then_inc(s("mask_stage"), 1)

            def values(i, st):
                act.wait_ge(s("a_pv"), START + at(i, STEPS, st + 1))
                hp, b = st // B, st % B
                if b == 0:
                    act.wait_ge(s("o_stored%d" % hp), START + at(i, STORES))
                act.activation(o_sb[:, hp, b, :], PS[:, 6, 0:P], ACT.Copy).then_inc(s("o_copied"), 1)

            act.preload_act_table_set("natural_log_exp_and_others")
            stepping(act, scored, quarter, values, nothing)

        def attn_dve(v):
            v.wait_ge(s("a_values"), START + B + 2)
            v.wait_ge(s("mask_rows"), START + 2)

            def scored(i, st):
                v.wait_ge(s("a_scores"), START + at(i, TPB * STEPS, TPB * (st + 1)))
                v.wait_ge(s("a_exp"), START + at(i, TPB * STEPS, TPB * (st - 1)) if st or type(i) is not int or i else START)
                v.tensor_reduce(a_nmax[:, st % 2, :], PS[:, 0:TPB, :], AX.X, ALU.max, negate=True).then_inc(s("a_nmax"), 1)

            def quarter(i, q):
                hp, tile = q // TPB, q % TPB
                v.wait_ge(s("mask_arg"), START + at(i, STEPS, q + 1))
                if q >= 2 * B or type(i) is not int or i:
                    v.wait_ge(s("a_masked"), START + at(i, 2 * STEPS, 2 * B * (hp - 1)))
                v.tensor_scalar(mk[:, hp, tile, :], PS[:, 7, :], acol[:, 5:6], MASK_CLAMP, ALU.mult,
                                ALU.min).then_inc(s("mask_clamped"), 1)

            def turned(i, st):
                hp, b = st // B, st % B
                v.wait_ge(s("a_pv"), START + at(i, STEPS, st))
                if b == 0:
                    h = i * HEADS_PER_PASS + hp
                    plain_wait(v)
                    v.tensor_copy(v_head[:, hp, :, 0:HD], v_all[:, :, bass.ds(h * HD, HD)]).then_inc(s("v_head_ready"), 1)
                for t in range(TPB):
                    v.wait_ge(s("a_transposed"), START + at(i, TPB * STEPS, TPB * st + t + 1))
                    v.tensor_copy(ppT[:, :, t * P:(t + 1) * P],
                                  PS[:, 4 + t % 2, :].rearrange("p (a b) -> p a b", a=TPB)).then_inc(s("ppT_ready"), 1)

            stepping(v, scored, quarter, nothing, turned)

        def attn_pool(g):
            with g.Fori(0, PASSES) as i:
                for st in range(STEPS):
                    hp = st // B
                    if st % B == 0:
                        g.wait_ge(s("mask_stage"), START + at(i, MASK_OPS * STEPS, MASK_OPS * TPB * (hp + 1)))
                    for half in range(2):
                        g.wait_ge(s("a_exp"), START + at(i, TPB * STEPS, TPB * st + 2 * half + 2))
                        a = pp[:, st % 2, 2 * half:2 * half + 2, :]
                        g.tensor_tensor(a, a, mk[:, hp, 2 * half:2 * half + 2, :], ALU.mult).then_inc(s("a_masked"), 1)

        def attn_out_pe(pe):
            for b in range(B):
                pe.wait_ge(s("att_ready"), START + 2 * b + 2)
                pe.matmul(PS[:, b, :], aw[:, 3, :], att[:, b % 2, :], start=True, stop=True).then_inc(s("a_out"), 1)

        def attn_out_dve(v):
            v.wait_ge(s("o_loaded"), START + 32)

            def added(b):
                v.wait_ge(s("a_out"), START + b + 1)
                v.scalar_tensor_tensor(xT[:, b, :], PS[:, b, :], acol[:, 2:3], xT[:, b, :], ALU.add, ALU.add).then_inc(s("x_ready"), 1)

            for b in range(B):
                v.reciprocal(inv[:, b % 2, :], s_all[:, b, :]).then_inc(s("att_ready"), 1)
                v.wait_ge(s("att_ready"), START + 2 * b + 1)
                if b >= 2:
                    v.wait_ge(s("a_out"), START + b - 1)
                v.tensor_tensor(att[:, b % 2, :], o_all[:, b, :], inv[:, b % 2, :], ALU.mult).then_inc(s("att_ready"), 1)
                if b:
                    added(b - 1)
            added(B - 1)

        stage_memory()
        m_xn = carve([L])
        m_next = carve([L])
        lg = carve([3, TPB, E])
        tops = carve([TPB, E])
        top_i = carve([TPB, E])
        top_u = top_i.bitcast(U32)
        top_f = carve([TPB, E])
        e_small = carve([6, TPB])
        eq = carve([3, TPB, E])
        comb = carve([TPB, E])
        c_rest = carve([2, L])
        comb3 = carve([L], BF16)
        c_two = carve([L], BF16)
        cb = carve([2, L])
        gc, sl = carve([2, L]), carve([2, L])
        mh = carve([3, L])
        weighted = carve([2, L])
        acc = carve([L])
        MOE_CHUNKS = [(e, c) for e in range(E) for c in range(FCH)] + [(E, 0)]
        LAG = 2
        NMC = len(MOE_CHUNKS)

        def moe_weights(e, c):
            if e == E:
                return sgu[:, 0:FS], sgu[:, FS:2 * FS], sdn[:]
            return gu[:, e, c * P:(c + 1) * P], gu[:, e, F + c * P:F + (c + 1) * P], dn[:, e, c, :]

        def moe_pe(pe, m):
            pe.wait_ge(s("x_ready"), START + x_of(f"moe{m}"))
            pe.wait_ge(s("moe_loaded"), START + 64)

            def ahead(b, part):
                e = b + first_ln[f"moe{m}"]
                if part == 0:
                    ln_mean(xT[:, b, :], 7)
                if part == 1:
                    ln_variance(e, 7)
                if part == 2:
                    pe.wait_ge(s("ln_done"), START + e + 1)
                    for t in range(TPB):
                        mm = pe.matmul(PS[:, 7, t * E:(t + 1) * E], m_next[:, t * P:(t + 1) * P], rw[:], start=True, stop=True)
                    mm.then_inc(s("logits"), 1)

            def one(b, last):
                n = b + B * m
                pe.wait_ge(s("moe_input"), START + n + 1)

                def down(k):
                    e, c = MOE_CHUNKS[k]
                    pe.wait_ge(s("moe_hidden"), START + at(n, NMC, k + 1))
                    if c == 0:
                        pe.wait_ge(s("moe_weighted"), START + at(n, E + 1, max(e - 1, 0)))
                    last = c == FCH - 1 or e == E
                    mm = pe.matmul(PS[:, 4 + e % 2, :], moe_weights(e, c)[2], mh[:, k % 3, :], start=c == 0, stop=last)
                    mm.then_inc(s("moe_down"), 1)

                def comb_rows():
                    pe.wait_ge(s("comb_ready"), START + n + 1)
                    for t in range(TPB):
                        tr = pe.transpose(PS[0:E, 7, t * P:(t + 1) * P], comb[:, t, :], ident)
                    tr.then_inc(s("combT"), 1)

                def comb_bcast(e):
                    if e == 0:
                        pe.wait_ge(s("comb_split"), START + at(n, 6, 6))
                    pe.wait_ge(s("cb_ready"), START + at(n, E, e))
                    pe.matmul(PS[:, 6, :], sel_b[0:96, e, :], comb3[0:96, :], start=True, stop=True).then_inc(s("cb_done"), 1)

                for k in range(NMC + LAG):
                    if k < NMC:
                        e, c = MOE_CHUNKS[k]
                        wg, wu, _ = moe_weights(e, c)
                        if c == 0 and e < E:
                            pe.wait_ge(s(f"experts{e // 2}_loaded"), START + 64)
                        pe.wait_ge(s("moe_clipped"), START + reuse(n, NMC, k, 2))
                        pe.matmul(PS[:, k % 2, :], wg, m_xn, start=True, stop=True).then_inc(s("moe_proj"), 1)
                        pe.wait_ge(s("moe_hidden"), START + reuse(n, NMC, k, 2))
                        pe.matmul(PS[:, 2 + k % 2, :], wu, m_xn, start=True, stop=True).then_inc(s("moe_proj"), 1)
                    if k == 1:
                        comb_rows()
                    if not last and k - AHEAD in range(3):
                        if k == AHEAD:
                            pe.wait_ge(s("comb_split"), START + at(n, 6, 2))
                        ahead(b + 1, k - AHEAD)
                    if k >= LAG:
                        down(k - LAG)
                        e, c = MOE_CHUNKS[k - LAG]
                        if c == 1:
                            comb_bcast(e)

            for part in range(3):
                ahead(0, part)
            with pe.Fori(0, B - 1) as b:
                one(b, False)
            one(B - 1, True)

        def moe_act(act, m):
            act.wait_ge(s("x_ready"), START + x_of(f"moe{m}"))

            def ahead(b, part):
                e = b + first_ln[f"moe{m}"]
                if part == 0:
                    ln_square(e)
                if part == 1:
                    act.preload_act_table_set("natural_log_exp_and_others")
                    ln_rstd(e, 7)
                if part == 2:
                    act.wait_ge(s("logits_shifted"), START + b + B * m + 1)
                    act.activation(lg[:, 1, :, :], lg[:, 0, :, :], ACT.Exp).then_inc(s("logits_exp"), 1)

            def one(b, last):
                n = b + B * m
                act.wait_ge(s("moe_proj"), START + at(n, 2 * NMC))
                act.wait_ge(s("ln_done"), START + b + first_ln[f"moe{m}"] + 1)
                plain_wait(act)
                act.activation(m_xn, m_next, ACT.Copy).then_inc(s("moe_input"), 1)
                for k in range(NMC + 3):
                    if not last and k - AHEAD in range(3):
                        ahead(b + 1, k - AHEAD)
                    if k < NMC:
                        act.wait_ge(s("moe_clipped"), START + at(n, NMC, k + 1))
                        act.wait_ge(s("moe_hidden"), START + reuse(n, NMC, k, 2))
                        act.activation(sl[:, k % 2, :], gc[:, k % 2, :], ACT.Silu).then_inc(s("moe_silu"), 1)
                    if k >= 3 and MOE_CHUNKS[k - 3][1] == 1:
                        e = MOE_CHUNKS[k - 3][0]
                        act.wait_ge(s("cb_done"), START + at(n, E, e + 1))
                        act.wait_ge(s("moe_weighted"), START + at(n, E + 1, max(e - 1, 0)))
                        act.activation(cb[:, e % 2, :], PS[:, 6, :], ACT.Copy).then_inc(s("cb_ready"), 1)

            for part in range(3):
                ahead(0, part)
            with act.Fori(0, B - 1) as b:
                one(b, False)
            one(B - 1, True)

        def moe_dve(v, m):
            v.wait_ge(s("x_ready"), START + x_of(f"moe{m}"))

            def ahead(b, part):
                e, n = b + first_ln[f"moe{m}"], b + B * m
                chain = [0, 0, 0, 1, 4, 6, 8, 10, 12, 15, 18][part]

                def then(ins):
                    nonlocal chain
                    chain += 1
                    ins.then_inc(s("route_step"), 1)
                    v.wait_ge(s("route_step"), START + at(n, ROUTE_STEPS, chain))

                def bc(a):
                    return a.unsqueeze(2).broadcast_to([P, TPB, E])

                if part == 0:
                    ln_centre(xT[:, b, :], e, 7)
                elif part == 1:
                    ln_scale(e, mcol[:, 0:1], mcol[:, 1:2], m_next, free=[("moe_input", n)])
                elif part == 2:
                    v.wait_ge(s("logits"), START + n + 1)
                    logits = PS[:, 7, 0:TPB * E].rearrange("p (a b) -> p a b", a=TPB)
                    then(v.tensor_reduce(e_small[:, 0, :], logits, AX.X, ALU.max))
                    v.tensor_tensor(lg[:, 0, :, :], logits, bc(e_small[:, 0, :]), ALU.subtract).then_inc(s("logits_shifted"), 1)
                elif part == 3:
                    v.wait_ge(s("logits_exp"), START + n + 1)
                    then(v.tensor_reduce(e_small[:, 1, :], lg[:, 1, :, :], AX.X, ALU.add))
                    then(v.reciprocal(e_small[:, 2, :], e_small[:, 1, :]))
                    then(v.tensor_tensor(lg[:, 2, :, :], lg[:, 1, :, :], bc(e_small[:, 2, :]), ALU.mult))
                elif part < 8:
                    t = part - 4
                    plain_wait(v)
                    then(v.max(tops[:, t, :], lg[:, 2, t, :]))
                    plain_wait(v)
                    then(v.max_index(top_u[:, t, :], tops[:, t, :], lg[:, 2, t, :]))
                elif part == 8:
                    then(v.tensor_copy(top_f, top_u))
                    then(v.tensor_tensor(e_small[:, 3, :], tops[:, :, 0], tops[:, :, 1], ALU.add))
                    then(v.reciprocal(e_small[:, 4, :], e_small[:, 3, :]))
                else:
                    i = part - 9
                    iota = con[:, C_IOTA:C_IOTA + TPB * E].rearrange("p (a b) -> p a b", a=TPB)
                    then(v.tensor_tensor(e_small[:, 5, :], tops[:, :, i], e_small[:, 4, :], ALU.mult))
                    then(v.tensor_tensor(eq[:, i, :, :], iota, bc(top_f[:, :, i]), ALU.is_equal))
                    then(v.tensor_tensor(eq[:, i, :, :], eq[:, i, :, :], bc(e_small[:, 5, :]), ALU.mult))
                    if i:
                        v.tensor_tensor(comb, eq[:, 0, :, :], eq[:, 1, :, :], ALU.add).then_inc(s("comb_ready"), 1)
                        assert chain == ROUTE_STEPS, chain

            def one(b, last):
                n = b + B * m

                def comb_parts():
                    v.wait_ge(s("combT"), START + n + 1)
                    T, c1, c2 = PS[0:E, 7, :], comb3[0:E], c_two[0:E]
                    r1, r2 = c_rest[0:E, 0], c_rest[0:E, 1]
                    for st, (dst, a, part) in enumerate(((c1, T, None), (r1, T, c1), (c2, r1, None), (r2, r1, c2),
                                                         (comb3[32:32 + E], c2, None), (comb3[64:64 + E], r2, None))):
                        if st:
                            v.wait_ge(s("comb_split"), START + at(n, 6, st))
                        ins = v.tensor_copy(dst, a) if part is None else v.tensor_tensor(dst, a, part, ALU.subtract)
                        ins.then_inc(s("comb_split"), 1)

                def weigh(e):
                    last = at(n, NMC, min((e + 1) * FCH, NMC))
                    v.wait_ge(s("moe_down"), START + last)
                    v.wait_ge(s("moe_acc"), START + at(n, E, max(e - 1, 0) if e < E else E))
                    if e < E:
                        v.wait_ge(s("cb_ready"), START + at(n, E, e + 1))
                        v.tensor_tensor(weighted[:, e % 2, :], PS[:, 4 + e % 2, :], cb[:, e % 2, :], ALU.mult).then_inc(s("moe_weighted"), 1)
                    else:
                        v.tensor_tensor(weighted[:, 0, :], PS[:, 4, :], acc, ALU.add).then_inc(s("moe_weighted"), 1)

                for k in range(NMC + LAG + 1):
                    if k == 2:
                        comb_parts()
                    if not last and k - AHEAD in range(AHEAD_PARTS):
                        ahead(b + 1, k - AHEAD)
                    if k < NMC:
                        v.wait_ge(s("moe_proj"), START + at(n, 2 * NMC, 2 * k + 1))
                        v.wait_ge(s("moe_silu"), START + reuse(n, NMC, k, 2))
                        v.tensor_scalar(gc[:, k % 2, :], PS[:, k % 2, :], 10.0, -10.0, ALU.min, ALU.max).then_inc(s("moe_clipped"), 1)
                    if 1 <= k <= NMC:
                        j = k - 1
                        v.wait_ge(s("moe_silu"), START + at(n, NMC, j + 1))
                        v.wait_ge(s("moe_proj"), START + at(n, 2 * NMC, 2 * j + 2))
                        v.wait_ge(s("moe_down"), START + reuse(n, NMC, j, 3))
                        v.tensor_tensor(mh[:, j % 3, :], sl[:, j % 2, :], PS[:, 2 + j % 2, :], ALU.mult).then_inc(s("moe_hidden"), 1)
                    if k >= 3 and k - 3 < NMC and k - 3 >= 1 and MOE_CHUNKS[k - 3][1] == 0 and MOE_CHUNKS[k - 3][0] > 0:
                        weigh(MOE_CHUNKS[k - 3][0] - 1)
                weigh(E)
                v.wait_ge(s("moe_weighted"), START + at(n, E + 1, E + 1))
                v.scalar_tensor_tensor(xT[:, b, :], weighted[:, 0, :], 0.5, xT[:, b, :], ALU.mult, ALU.add).then_inc(s("x_ready"), 1)

            for part in range(AHEAD_PARTS):
                ahead(0, part)
            with v.Fori(0, B - 1) as b:
                one(b, False)
            one(B - 1, True)

        ROUTE_STEPS = 4 + 2 * TPB + 3 + 6
        AHEAD_PARTS = 3 + 1 + TPB + 1 + 2
        AHEAD = 8

        def moe_pool(g, m):
            g.memset(comb3[0:96, :].bitcast(F32), 0.0).then_inc(s("comb3_zero"), 1)
            with g.Fori(0, B) as b:
                n = b + B * m
                for e in range(E):
                    g.wait_ge(s("moe_weighted"), START + at(n, E + 1, e + 1))
                    g.wait_ge(s("moe_acc"), START + at(n, E, e))
                    if e == 0:
                        plain_wait(g)
                        g.tensor_copy(acc, weighted[:, 0, :]).then_inc(s("moe_acc"), 1)
                    else:
                        g.tensor_tensor(acc, acc, weighted[:, e % 2, :], ALU.add).then_inc(s("moe_acc"), 1)

        stage_memory()
        t_xn = carve([L])
        qT, kT, vT = (carve([B, L]) for _ in range(3))
        k_tok = carve([B * TPB, D])
        raw, rsq, rlog = carve([2, L]), carve([2, L]), carve([2, L])
        k_s = carve([L])
        kt_s = carve([TPB, D])
        sg, g_m, g_d = carve([2, TH]), carve([2, TH]), carve([2, TH])
        start = taken[0]
        th_h, th_s, th_w = (carve([TPB, TH]) for _ in range(3))
        end, taken[0] = taken[0], start
        X = [carve([TH]) for _ in range(3)]
        XT = [carve([4, D]) for _ in range(3)]
        A_s, A_b, B_s = ([carve([D]) for _ in range(3)] for _ in range(3))
        gsq = carve([TH])
        assert taken[0] <= end
        taken[0] = end
        hT = carve([4, L])
        dp = carve([L])
        dp_tok = carve([TPB, D])
        du, dg = carve([2, TH]), carve([2, TH])
        grad = carve([3, TH])
        nrm = carve([4, 4])
        a_ident = carve([D])
        v_bias = carve([1])

        def ttt_proj_pe(pe):
            pe.wait_ge(s("x_ready"), START + x_of("ttt"))
            pe.wait_ge(s("ttt_loaded"), START + 112)
            with pe.Fori(0, B) as b:
                e = b + first_ln["ttt"]
                ln_pe(xT[:, b, :], e, 6, 7)
                pe.wait_ge(s("ln_done"), START + e + 1)
                pe.wait_ge(s("t_biased"), START + at(b, 3))
                for i in range(3):
                    pe.matmul(PS[:, i, :], tqkv[:, i * D:(i + 1) * D], t_xn, start=True, stop=True).then_inc(s("t_proj"), 1)
                for i in range(2):
                    pe.wait_ge(s("t_squared"), START + at(b, 2, i + 1))
                    pe.matmul(PS[:, 3 + i, :], blk8, rsq[:, i, :], start=True, stop=True).then_inc(s("t_sums"), 1)
                pe.wait_ge(s("k_staged"), START + at(b, 1, 1))
                pe.wait_ge(s("k_tok_ready"), START + at(b, 1))
                for t in range(TPB):
                    tr = pe.transpose(PS[:, 5, t * P:(t + 1) * P], k_s[:, t * P:(t + 1) * P], ident)
                tr.then_inc(s("k_transposed"), 1)

        def ttt_proj_act(act):
            act.wait_ge(s("x_ready"), START + x_of("ttt"))
            act.wait_ge(s("ttt_consts"), START + 2)
            act.preload_act_table_set("natural_log_exp_and_others")
            with act.Fori(0, B) as b:
                e = b + first_ln["ttt"]
                ln_act(e, 7)
                for i in range(3):
                    act.wait_ge(s("t_proj"), START + at(b, 3, i + 1))
                    act.wait_ge(s("t_scaled"), START + at(b, 2))
                    dst = raw[:, i, :] if i < 2 else vT[:, b, :]
                    plain_wait(act)
                    act.activation(dst, PS[:, i, :], ACT.Identity, bias=tcol[:, 4 + i:5 + i] if i < 2 else v_bias,
                                   scale=1.0 if i < 2 else GRAD_SCALE).then_inc(s("t_biased"), 1)
                for i in range(2):
                    act.wait_ge(s("t_biased"), START + at(b, 3, i + 1))
                    act.activation(rsq[:, i, :], raw[:, i, :], ACT.Square).then_inc(s("t_squared"), 1)
                for i in range(2):
                    act.wait_ge(s("t_sums"), START + at(b, 2, i + 1))
                    c = at(b, 8, 4 * i)
                    act.activation(rlog[:, i, :], PS[:, 3 + i, :], ACT.Ln, bias=c_tiny, scale=2.0 ** LS).then_inc(s("t_norm_step"), 1)
                    act.wait_ge(s("t_norm_step"), START + c + 1)
                    act.activation(rlog[:, i, :], rlog[:, i, :], ACT.Exp, bias=c_neg, scale=0.5).then_inc(s("t_norm_step"), 1)
                    act.wait_ge(s("t_norm_step"), START + c + 2)
                    act.activation(rlog[:, i, :], rlog[:, i, :], ACT.Ln, bias=c_1e6).then_inc(s("t_norm_step"), 1)
                    act.wait_ge(s("t_norm_step"), START + c + 3)
                    act.activation(rlog[:, i, :], rlog[:, i, :], ACT.Exp, scale=-1.0).then_inc(s("t_norm_step"), 1)

        def ttt_proj_dve(v):
            v.wait_ge(s("x_ready"), START + x_of("ttt"))
            v.wait_ge(s("ttt_loaded"), START + 112)
            v.tensor_scalar(v_bias, tcol[:, 6:7], GRAD_SCALE, None, ALU.mult).then_inc(s("ttt_consts"), 1)
            v.tensor_scalar(a_ident, ident, NS_A, None, ALU.mult).then_inc(s("ttt_consts"), 1)
            with v.Fori(0, B) as b:
                e = b + first_ln["ttt"]
                ln_dve(xT[:, b, :], e, 6, c_one, c_zero, t_xn)
                for i, dst in enumerate((qT, kT)):
                    v.wait_ge(s("t_norm_step"), START + at(b, 8, 4 * i + 4))
                    v.scalar_tensor_tensor(raw[:, i, :], raw[:, i, :], tcol[:, 2 * i:2 * i + 1], rlog[:, i, :], ALU.mult,
                                           ALU.mult).then_inc(s("t_scaled"), 1)
                    v.wait_ge(s("t_scaled"), START + at(b, 2, i + 1))
                    v.tensor_scalar(dst[:, b, :], raw[:, i, :], tcol[:, 2 * i + 1:2 * i + 2], None, ALU.add)
                v.wait_ge(s("k_transposed"), START + at(b, 1))
                v.tensor_scalar(k_s, raw[:, 1, :], tcol[:, 3:4], None, ALU.add).then_inc(s("k_staged"), 1)
                v.wait_ge(s("k_transposed"), START + at(b, 1, 1))
                plain_wait(v)
                v.tensor_copy(k_tok[:, bass.ds(b * TPB, TPB), :], PS[:, 5, :].rearrange("p (a b) -> p a b", a=TPB)).then_inc(s("k_tok_ready"), 1)

        def grad_pe(pe, step):
            with pe.Fori(0, B) as b:
                n = b + B * step
                pe.wait_ge(s("staged"), START + at(n, 2, 2))
                pe.wait_ge(s("theta_ready"), START + 4 * step)

                def turn(t):
                    pe.wait_ge(s("g_h"), START + at(n, TPB, t + 1))
                    pe.wait_ge(s("hT_ready"), START + at(n, TPB, t))
                    for c in range(4):
                        tr = pe.transpose(PS[:, 4, c * P:(c + 1) * P], th_h[:, t, c * P:(c + 1) * P], ident)
                    tr.then_inc(s("h_turned"), 1)

                for t in range(TPB):
                    kt = k_s[:, t * P:(t + 1) * P]
                    pe.wait_ge(s("g_w"), START + at(n, TPB, max(t - 1, 0)))
                    if t < 2:
                        pe.wait_ge(s("g_dg"), START + at(n, TPB))
                    pe.matmul(PS[:, t % 2, :], kt, th_g[:], start=True, stop=True).then_inc(s("g_gate"), 1)
                    pe.matmul(PS[:, 2 + t % 2, :], kt, th_v[:], start=True, stop=True).then_inc(s("g_val"), 1)
                    if t >= 1:
                        turn(t - 1)
                turn(TPB - 1)
                pe.wait_ge(s("hT_ready"), START + at(n, TPB, TPB))
                pe.wait_ge(s("grad_added"), START + at(n, 3))
                for c in range(4):
                    mm = pe.matmul(PS[:, 5, :], th_p[:, c, :], hT[:, c, :], start=c == 0, stop=c == 3)
                mm.then_inc(s("predicted"), 1)
                pe.wait_ge(s("dp_ready"), START + at(n, 1, 1))
                for t in range(TPB):
                    tr = pe.transpose(PS[:, 4, t * P:(t + 1) * P], dp[:, t * P:(t + 1) * P], ident)
                tr.then_inc(s("dp_turned"), 1)

                def dh(t):
                    pe.wait_ge(s("g_w"), START + at(n, TPB, TPB))
                    pe.wait_ge(s("g_dg"), START + at(n, TPB, max(t - 1, 0)))
                    pe.matmul(PS[:, t % 2, :], dp[:, t * P:(t + 1) * P], th_pT[:], start=True, stop=True).then_inc(s("g_dh"), 1)

                dh(0)
                pe.wait_ge(s("dp_tok_ready"), START + at(n, 1, 1))
                for t in range(TPB):
                    if t < TPB - 1:
                        dh(t + 1)
                    st, sp_ = t == 0, t == TPB - 1
                    mm = pe.matmul(PS[:, 5, :], dp_tok[:, t, :], th_h[:, t, :], start=st, stop=sp_)
                    if sp_:
                        mm.then_inc(s("grads"), 1)
                    pe.wait_ge(s("g_du"), START + at(n, TPB, t + 1))
                    mm = pe.matmul(PS[:, 6, :], kt_s[:, t, :], du[:, t % 2, :], start=st, stop=sp_)
                    if sp_:
                        mm.then_inc(s("grads"), 1)
                    pe.wait_ge(s("g_dg"), START + at(n, TPB, t + 1))
                    pe.matmul(PS[:, 7, :], kt_s[:, t, :], dg[:, t % 2, :], start=st, stop=sp_).then_inc(s("g_used"), 1)

        def grad_act(act, step):
            with act.Fori(0, B) as b:
                n = b + B * step
                for t in range(TPB + 1):
                    if t < TPB:
                        act.wait_ge(s("g_gate"), START + at(n, TPB, t + 1))
                        act.wait_ge(s("g_w"), START + at(n, TPB, max(t - 1, 0)))
                        act.activation(sg[:, t % 2, :], PS[:, t % 2, :], ACT.Sigmoid).then_inc(s("g_sig"), 1)
                    if t >= 1:
                        act.wait_ge(s("h_turned"), START + at(n, TPB, t))
                        if t == 1:
                            act.wait_ge(s("predicted"), START + n)
                        act.activation(hT[:, :, (t - 1) * P:t * P], PS[:, 4, :].rearrange("p (a b) -> p a b", a=4),
                                       ACT.Copy).then_inc(s("hT_ready"), 1)
                act.wait_ge(s("dp_turned"), START + n + 1)
                act.wait_ge(s("grads"), START + at(n, 2))
                act.activation(dp_tok.rearrange("p a b -> p (a b)"), PS[:, 4, :], ACT.Copy).then_inc(s("dp_tok_ready"), 1)

        def grad_dve(v, step):
            if step == 0:
                v.memset(grad, 0.0).then_inc(s("grad_zero"), 1)
            else:
                v.wait_ge(s("theta_ready"), START + 4 * step)
                v.memset(grad, 0.0).then_inc(s("grad_zero"), 1)
            v.wait_ge(s("grad_zero"), START + step + 1)
            with v.Fori(0, B) as b:
                n = b + B * step
                for t in range(TPB):
                    j = t % 2
                    u = PS[:, 2 + j, :]
                    v.wait_ge(s("g_sig"), START + at(n, TPB, t + 1))
                    v.wait_ge(s("g_val"), START + at(n, TPB, t + 1))
                    if t == 0:
                        v.wait_ge(s("g_used"), START + at(n, TPB))
                    v.tensor_tensor(th_s[:, t, :], PS[:, j, :], sg[:, j, :], ALU.mult).then_inc(s("g_silu"), 1)
                    v.wait_ge(s("g_silu"), START + at(n, TPB, t + 1))
                    v.scalar_tensor_tensor(g_m[:, j, :], sg[:, j, :], 1.0, th_s[:, t, :], ALU.subtract, ALU.mult).then_inc(s("g_slope"), 1)
                    v.tensor_tensor(th_h[:, t, :], th_s[:, t, :], u, ALU.mult).then_inc(s("g_h"), 1)
                    v.wait_ge(s("g_slope"), START + at(n, 2 * TPB, 2 * t + 1))
                    v.tensor_tensor(g_d[:, j, :], sg[:, j, :], g_m[:, j, :], ALU.subtract).then_inc(s("g_slope"), 1)
                    v.wait_ge(s("g_slope"), START + at(n, 2 * TPB, 2 * t + 2))
                    v.tensor_tensor(th_w[:, t, :], g_d[:, j, :], u, ALU.mult).then_inc(s("g_w"), 1)
                v.wait_ge(s("predicted"), START + n + 1)
                v.wait_ge(s("grads"), START + at(n, 2))
                v.scalar_tensor_tensor(dp, PS[:, 5, :], GRAD_SCALE, vT[:, b, :], ALU.mult, ALU.subtract).then_inc(s("dp_ready"), 1)
                for t in range(TPB):
                    v.wait_ge(s("g_dh"), START + at(n, TPB, t + 1))
                    v.wait_ge(s("g_used"), START + at(n, TPB, max(t - 1, 0)))
                    v.tensor_tensor(du[:, t % 2, :], PS[:, t % 2, :], th_s[:, t, :], ALU.mult).then_inc(s("g_du"), 1)
                    v.tensor_tensor(dg[:, t % 2, :], PS[:, t % 2, :], th_w[:, t, :], ALU.mult).then_inc(s("g_dg"), 1)
                v.wait_ge(s("grads"), START + at(n, 2, 2))
                v.wait_ge(s("g_used"), START + at(n, TPB, TPB))
                v.wait_ge(s("grad_added"), START + at(n, 3))
                for i, bank in enumerate((7, 6, 5)):
                    v.tensor_tensor(grad[:, i, :], grad[:, i, :], PS[:, bank, :], ALU.add).then_inc(s("grad_added"), 1)

        def grad_pool(g, step):
            with g.Fori(0, B) as b:
                n = b + B * step
                g.wait_ge(s("k_tok_ready"), START + B)
                g.wait_ge(s("g_used"), START + at(n, TPB))
                plain_wait(g)
                g.tensor_copy(k_s, kT[:, b, :]).then_inc(s("staged"), 1)
                plain_wait(g)
                g.tensor_copy(kt_s, k_tok[:, bass.ds(b * TPB, TPB), :]).then_inc(s("staged"), 1)

        def ns_pe(pe, step):
            pe.wait_ge(s("ns_sumsq"), START + 3 * (step + 1))
            pe.matmul(PS[:, 0, 0:3], ones, nrm[:, 0, 0:3], start=True, stop=True).then_inc(s("ns_norm"), 1)
            for j in range(3):
                pe.wait_ge(s("ns_X0"), START + 3 * step + j + 1)
                for c in range(4):
                    tr = pe.transpose(PS[:, 3 + j, c * P:(c + 1) * P], X[j][:, c * P:(c + 1) * P], ident)
                tr.then_inc(s("ns_T0"), 1)
            with pe.Fori(0, NS_ITERS) as it:
                n = it + NS_ITERS * step
                for j in range(3):
                    if j == 0:
                        pe.wait_ge(s("ns_T0_copied"), START + 3 * (step + 1))
                    pe.wait_ge(s("ns_XT"), START + at(n, 3))
                    for c in range(4):
                        mm = pe.matmul(PS[:, j, 0:P], XT[j][:, c, :], XT[j][:, c, :], start=c == 0, stop=c == 3)
                    mm.then_inc(s("ns_A"), 1)
                for j in range(3):
                    pe.wait_ge(s("ns_A_copied"), START + at(n, 3, j + 1))
                    pe.wait_ge(s("ns_A_poly"), START + at(n, 3, j + 1))
                    pe.matmul(PS[:, j, P:2 * P], A_s[j], A_s[j], start=True, stop=True).then_inc(s("ns_A2"), 1)
                for j in range(3):
                    pe.wait_ge(s("ns_B"), START + at(n, 3, j + 1))
                    pe.wait_ge(s("ns_X"), START + at(n, 3))
                    pe.matmul(PS[:, 3 + j, :], B_s[j], X[j], start=True, stop=True).then_inc(s("ns_BX"), 1)
                    if j >= 1:
                        pe.wait_ge(s("ns_XT"), START + (at(n, 3, j - 1) if j >= 2 else at(n, 3)))
                    for c in range(4):
                        mm = pe.matmul(PS[:, 6 + j % 2, c * P:(c + 1) * P], X[j][:, c * P:(c + 1) * P], B_s[j], start=True, stop=True)
                    mm.then_inc(s("ns_XTB"), 1)

        def ns_act(act, step):
            v3 = 3 * step
            act.preload_act_table_set("natural_log_exp_and_others")
            act.wait_ge(s("grad_added"), START + 3 * B * (step + 1))
            for j in range(3):
                if j:
                    act.wait_ge(s("ns_sumsq"), START + v3 + j)
                act.activation(gsq, grad[:, j, :], ACT.Square, accum_out=nrm[:, 0, j:j + 1]).then_inc(s("ns_sumsq"), 1)
            act.wait_ge(s("ns_norm"), START + step + 1)
            act.activation(nrm[:, 1, 0:3], PS[:, 0, 0:3], ACT.Ln, bias=c_tiny, scale=2.0 ** LS).then_inc(s("ns_scale_step"), 1)
            act.wait_ge(s("ns_scale_step"), START + 4 * step + 1)
            act.activation(nrm[:, 2, 0:3], nrm[:, 1, 0:3], ACT.Exp, bias=c_neg, scale=0.5).then_inc(s("ns_scale_step"), 1)
            for j in range(3):
                act.wait_ge(s("ns_T0"), START + v3 + j + 1)
                act.activation(XT[j].rearrange("p a b -> p (a b)"), PS[:, 3 + j, :], ACT.Copy).then_inc(s("ns_T0_copied"), 1)
            with act.Fori(0, NS_ITERS) as it:
                n = it + NS_ITERS * step
                for j in range(3):
                    act.wait_ge(s("ns_A"), START + at(n, 3, j + 1))
                    act.activation(A_s[j], PS[:, j, 0:P], ACT.Copy).then_inc(s("ns_A_copied"), 1)
                for j in range(3):
                    act.wait_ge(s("ns_XTB"), START + at(n, 3, j + 1))
                    act.activation(XT[j].rearrange("p a b -> p (a b)"), PS[:, 6 + j % 2, :], ACT.Copy).then_inc(s("ns_XT"), 1)

        def ns_dve(v, step):
            v3 = 3 * step
            v.wait_ge(s("ns_scale_step"), START + 4 * step + 2)
            v.tensor_scalar(nrm[:, 3, 0:3], nrm[:, 2, 0:3], 1e-7, None, ALU.add).then_inc(s("ns_scale_step"), 1)
            v.wait_ge(s("ns_scale_step"), START + 4 * step + 3)
            v.reciprocal(nrm[:, 1, 0:3], nrm[:, 3, 0:3]).then_inc(s("ns_scale_step"), 1)
            v.wait_ge(s("ns_scale_step"), START + 4 * step + 4)
            for j in range(3):
                v.tensor_scalar(X[j], grad[:, j, :], nrm[:, 1, j:j + 1], None, ALU.mult).then_inc(s("ns_X0"), 1)
            with v.Fori(0, NS_ITERS) as it:
                n = it + NS_ITERS * step
                for j in range(3):
                    v.wait_ge(s("ns_A_copied"), START + at(n, 3, j + 1))
                    v.scalar_tensor_tensor(A_b[j], A_s[j], NS_B, a_ident, ALU.mult, ALU.add).then_inc(s("ns_A_poly"), 1)
                for j in range(3):
                    v.wait_ge(s("ns_A2"), START + at(n, 3, j + 1))
                    v.wait_ge(s("ns_A_poly"), START + at(n, 3, j + 1))
                    v.scalar_tensor_tensor(B_s[j], PS[:, j, P:2 * P], NS_C, A_b[j], ALU.mult, ALU.add).then_inc(s("ns_B"), 1)
                for j in range(3):
                    v.wait_ge(s("ns_XTB"), START + at(n, 3, j + 1))
                    v.tensor_copy(X[j], PS[:, 3 + j, :]).then_inc(s("ns_X"), 1)
            n = NS_ITERS * (step + 1)
            v.wait_ge(s("ns_X"), START + 3 * n)
            v.wait_ge(s("ns_XT"), START + 3 * n)
            flat = lambda a: a.rearrange("p a b -> p (a b)")
            for dst, src in ((th_g[:], X[0]), (th_v[:], X[1]), (th_pT[:], X[2]), (flat(th_p[:]), flat(XT[2]))):
                v.scalar_tensor_tensor(dst, src, -LR, dst, ALU.mult, ALU.add).then_inc(s("theta_ready"), 1)

        def apply_pe(pe):
            pe.wait_ge(s("theta_ready"), START + 8)
            with pe.Fori(0, B) as b:
                def down(c):
                    pe.wait_ge(s("q_hidden"), START + at(b, 4, c + 1))
                    if c == 0:
                        pe.wait_ge(s("q_down_copied"), START + b)
                    mm = pe.matmul(PS[:, 4, :], th_p[:, c, :], hT[:, c, :], start=c == 0, stop=c == 3)
                    if c == 3:
                        mm.then_inc(s("q_down"), 1)

                for c in range(4):
                    pe.wait_ge(s("q_hidden"), START + reuse(b, 4, c, 2))
                    pe.matmul(PS[:, c % 2, :], th_g[:, c * P:(c + 1) * P], qT[:, b, :], start=True, stop=True).then_inc(s("q_proj"), 1)
                    pe.matmul(PS[:, 2 + c % 2, :], th_v[:, c * P:(c + 1) * P], qT[:, b, :], start=True, stop=True).then_inc(s("q_proj"), 1)
                    if c >= 1:
                        down(c - 1)
                down(3)
                pe.wait_ge(s("q_down_copied"), START + b + 1)
                pe.wait_ge(s("x_ready"), START + x_of("ttt") + b)
                pe.matmul(PS[:, 5, :], tpw[:], dp, start=True, stop=True).then_inc(s("q_out"), 1)

        def apply_act(act):
            with act.Fori(0, B) as b:
                for c in range(4):
                    act.wait_ge(s("q_proj"), START + at(b, 8, 2 * c + 1))
                    act.wait_ge(s("q_hidden"), START + reuse(b, 4, c, 2))
                    act.activation(sg[:, c % 2, :], PS[:, c % 2, :], ACT.Silu).then_inc(s("q_silu"), 1)
                act.wait_ge(s("q_down"), START + b + 1)
                act.wait_ge(s("q_out"), START + b)
                act.activation(dp, PS[:, 4, :], ACT.Copy).then_inc(s("q_down_copied"), 1)

        def apply_dve(v):
            with v.Fori(0, B) as b:
                for c in range(4):
                    v.wait_ge(s("q_silu"), START + at(b, 4, c + 1))
                    v.wait_ge(s("q_proj"), START + at(b, 8, 2 * c + 2))
                    if c == 0:
                        v.wait_ge(s("q_down"), START + b)
                    v.tensor_tensor(hT[:, c, :], sg[:, c % 2, :], PS[:, 2 + c % 2, :], ALU.mult).then_inc(s("q_hidden"), 1)
                v.wait_ge(s("q_out"), START + b + 1)
                v.scalar_tensor_tensor(xT[:, b, :], PS[:, 5, :], tcol[:, 7:8], xT[:, b, :], ALU.add, ALU.add).then_inc(s("x_ready"), 1)

        block = ctx.enter_context(nc.Block())
        run = STAGES[1:]

        @block.sync
        def _(sp):
            load_sync(sp)
            if "attn" in run:
                attn_proj_sync(sp)
                attn_sync(sp)
            if "moe0" in run:
                load_experts(sp)
            sp.wait_ge(s("x_ready"), START + B * len(STAGES))
            sp.dma_start(out, xT[:]).then_inc(s("out_stored"), 16)
            sp.wait_ge(s("out_stored"), START + 16)
            sp.wait_ge(s("mask_stored"), START + 32)

        @block.tensor
        def _(pe):
            pe.wait_ge(s("consts"), START + 7)
            for st in run:
                if st[:3] == "ffn":
                    f = int(st[3])
                    pe.wait_ge(s("x_ready"), START + x_of(st))
                    pe.wait_ge(s("ffn_loaded"), START + 48)
                    pe.wait_ge(s("pads_zero"), START + 3 * (f + 1))
                    ffn_pe(pe, f)
                elif st == "attn":
                    attn_proj_pe(pe)
                    attn_pe(pe)
                    attn_out_pe(pe)
                elif st[:3] == "moe":
                    pe.wait_ge(s("comb3_zero"), START + int(st[3]) + 1)
                    moe_pe(pe, int(st[3]))
                else:
                    ttt_proj_pe(pe)
                    for step in range(TTT_STEPS):
                        grad_pe(pe, step)
                        ns_pe(pe, step)
                    apply_pe(pe)

        @block.scalar
        def _(act):
            load_act(act)
            for st in run:
                if st[:3] == "ffn":
                    f = int(st[3])
                    act.wait_ge(s("x_ready"), START + x_of(st))
                    act.wait_ge(s("pads_zero"), START + 3 * (f + 1))
                    ffn_act(act, f)
                elif st == "attn":
                    attn_proj_act(act)
                    attn_act(act)
                elif st[:3] == "moe":
                    moe_act(act, int(st[3]))
                else:
                    ttt_proj_act(act)
                    for step in range(TTT_STEPS):
                        grad_act(act, step)
                        ns_act(act, step)
                    apply_act(act)

        @block.vector
        def _(v):
            load_dve(v)
            v.wait_ge(s("rot_scaled"), START + 8)
            for st in run:
                if st[:3] == "ffn":
                    f = int(st[3])
                    v.wait_ge(s("x_ready"), START + x_of(st))
                    v.wait_ge(s("mask_stored"), START + 32)
                    v.wait_ge(s("pads_zero"), START + 3 * (f + 1))
                    ffn_dve(v, f)
                elif st == "attn":
                    attn_proj_dve(v)
                    attn_dve(v)
                    attn_out_dve(v)
                elif st[:3] == "moe":
                    v.wait_ge(s("moe_loaded"), START + 64)
                    v.wait_ge(s("comb3_zero"), START + int(st[3]) + 1)
                    moe_dve(v, int(st[3]))
                else:
                    ttt_proj_dve(v)
                    for step in range(TTT_STEPS):
                        grad_dve(v, step)
                        ns_dve(v, step)
                    apply_dve(v)

        @block.gpsimd
        def _(g):
            for name in sorted(sems):
                g.sem_inc(sems[name], START)
            for st in run:
                g.wait_ge(s("x_ready"), START + x_of(st))
                if st[:3] == "ffn":
                    f = int(st[3])
                    ffn_zero_pads(g, f)
                    ffn_pool(g, f)
                elif st == "attn":
                    attn_pool(g)
                elif st[:3] == "moe":
                    moe_pool(g, int(st[3]))
                else:
                    for step in range(TTT_STEPS):
                        grad_pool(g, step)


def _layouts(i):
    f = lambda a: np.ascontiguousarray(np.asarray(a))
    cols = lambda *v: f(np.stack(v, -1))
    two = lambda a: np.concatenate([a, a], -1)
    swap = lambda a: np.concatenate([a[..., DH // 2:], a[..., :DH // 2]], -1)
    g = {k: np.asarray(v) for k, v in i.items()}
    wqkv = g["L0_ffn_wqkv"]
    qk = wqkv[:, :, :2 * INNER].reshape(DEPTH, D, 2 * HEADS, 2, DH // 2)[:, :, :, ::-1]
    w2 = np.zeros((3 * P,), wqkv.dtype)
    pad = lambda a, n: np.concatenate([a, np.zeros(a.shape[:-1] + (n - a.shape[-1],), a.dtype)], -1)
    b1 = g["L0_ffn_b1"]
    b1a, b1g = (pad(b, 3 * P).reshape(DEPTH, 3, P) for b in (b1[:, :HID], b1[:, HID:]))
    qs, ks = g["L0_ffn_q_scale"], g["L0_ffn_k_scale"]
    fc = np.zeros((P, DEPTH, 16), wqkv.dtype)
    vecs = [two(qs), two(swap(qs)), two(ks), two(swap(ks)), g["L0_ffn_ln_g"], g["L0_ffn_ln_b"], g["L0_ffn_b2"]]
    vecs += [b1a[:, c] for c in range(3)] + [b1g[:, c] for c in range(3)]
    for n, v in enumerate(vecs):
        fc[:, :, n] = v.T
    w2 = pad(g["L0_ffn_w2"].transpose(0, 2, 1), 3 * P).reshape(DEPTH, D, 3, P).transpose(3, 0, 2, 1)
    ac = np.zeros((P, 8), wqkv.dtype)
    for n, k in enumerate(("L0_attn_bq", "L0_attn_bk", "L0_attn_bo")):
        ac[:, n] = g[k]
    ac[:, 3] = g["L0_attn_temperature"]
    ph = np.zeros((NH, 8), wqkv.dtype)
    ph[:, 0:3] = g["L0_attn_phase"]
    ph[:, 3] = g["L0_attn_threshold"]
    tc = np.zeros((P, 8), wqkv.dtype)
    for n, v in enumerate([np.tile(g["L1_attn_" + k], NH) for k in ("qn_scale", "qn_bias", "kn_scale", "kn_bias")]
                          + list(g["L1_attn_qkv_b"].reshape(3, D)) + [g["L1_attn_proj_b"]]):
        tc[:, n] = v
    return {
        "xT": f(g["L0_attn_x"].transpose(2, 0, 1)),
        "con": shape_constants(), "rot": rotary_tables(), "pos": position_tables(), "phase": ph,
        "wqkv": f(wqkv.transpose(1, 0, 2)),
        "wswap": f(qk.transpose(1, 0, 2, 3, 4)),
        "wo": f(g["L0_ffn_wo"].reshape(DEPTH, NCH, P, D).transpose(2, 0, 1, 3)),
        "w1": f(g["L0_ffn_w1"].transpose(1, 0, 2)),
        "w2": f(w2), "fcol": fc,
        "aw": f(np.stack([g["L0_attn_W" + k] for k in "qkvo"], 1)),
        "acol": ac, "bv_row": f(np.tile(g["L0_attn_bv"][None], (P, 1))),
        "gu": f(g["L1_ffn_gate_up_w"].transpose(1, 0, 2)),
        "dn": f(g["L1_ffn_down_w"].reshape(E, FCH, P, D).transpose(2, 0, 1, 3)),
        "sgu": f(g["L1_ffn_shared_gate_up_w"]), "sdn": f(g["L1_ffn_shared_down_w"]), "rw": f(g["L1_ffn_router_w"]),
        "mcol": cols(g["L1_ffn_ln_gamma"], g["L1_ffn_ln_beta"]),
        "tqkv": f(g["L1_attn_qkv_w"]), "tcol": tc,
        "th_g": f(g["L1_attn_ttt_gate"]), "th_v": f(g["L1_attn_ttt_val"]), "th_pT": f(g["L1_attn_ttt_proj"].T),
        "th_p": f(g["L1_attn_ttt_proj"].reshape(4, P, D).transpose(1, 0, 2)),
        "tpw": f(g["L1_attn_proj_w"]),
    }


def kernel(**inputs):
    import concourse.bacc as bacc
    from concourse.bass_utils import run_bass_kernel_spmd

    nc = bacc.Bacc("TRN2", target_bir_lowering=False, num_devices=1)
    arrays = _layouts(inputs)
    aps = {k: nc.dram_tensor("in_" + k, a.shape, F32, kind="ExternalInput").ap() for k, a in arrays.items()}
    out = nc.dram_tensor("out_xT", (D, B, L), F32, kind="ExternalOutput").ap()
    build(nc, aps, out)
    r = run_bass_kernel_spmd(nc, [{"in_" + k: a for k, a in arrays.items()}], core_ids=[0])
    return np.ascontiguousarray(np.asarray(r.results[0]["out_xT"]).transpose(1, 2, 0))
```

```python
import numpy as np
import concourse.bass as bass
from concourse import mybir
from contextlib import ExitStack

F32 = mybir.dt.float32
BF16 = mybir.dt.bfloat16
F32R = mybir.dt.float32r
U32 = mybir.dt.uint32
I32 = mybir.dt.int32
ALU = mybir.AluOpType
ACT = mybir.ActivationFunctionType
AX = mybir.AxisListType

B, L, D = 4, 512, 128
P = 128
TPB = L // P
LN_EPS = 1e-5

DEPTH, HEADS, DH, WINDOW = 2, 8, 64, 64
INNER = HEADS * DH
QK_SCALE = 8.0
HID = 341
HCH = [(0, 128), (128, 128), (256, HID - 256)]
NCH = INNER // P
UNITS = 2 * TPB

NH, HD = 16, 8
SPLIT_Q = (0, 0, 1, 1, 0, 2)
SPLIT_K = (0, 1, 0, 1, 2, 0)
KS = HD * len(SPLIT_Q)
A_SCALE = float(1.0 / np.sqrt(HD))
MASK_CLAMP = 40.0
MF = 6

E, F, FS = 8, 512, 128
FCH = F // P

TH = 4 * D
LR, NS_ITERS, TTT_STEPS = 0.1, 5, 2
NS_A, NS_B, NS_C = 3.4445, -4.775, 2.0315
GRAD_SCALE = 2.0 / (B * L * D)

LS = 36
LN2 = float(np.log(2.0))

C_ID, C_ONES, C_BLK64, C_BLK8, C_MASK, C_IOTA, C_SEL = 0, 128, 256, 384, 512, 768, 800
C_N = C_SEL + E * 128


def shape_constants():
    c = np.zeros((P, C_N), np.float32)
    r = np.arange(P)
    c[:, C_ID:C_ID + P] = np.eye(P)
    c[:, C_ONES:C_ONES + P] = 1.0
    c[:, C_BLK64:C_BLK64 + P] = (r[:, None] // DH == r[None] // DH)
    c[:, C_BLK8:C_BLK8 + P] = (r[:, None] // HD == r[None] // HD)
    i, j = r[:, None] % WINDOW, r[None]
    ok = (j >= i) & (j <= i + WINDOW)
    first = ok & ((r[:, None] >= WINDOW) | (j >= WINDOW))
    c[:, C_MASK:C_MASK + P] = np.where(first, 0.0, -1e30)
    c[:, C_MASK + P:C_MASK + 2 * P] = np.where(ok, 0.0, -1e30)
    c[:, C_IOTA:C_IOTA + TPB * E] = np.tile(np.arange(E), TPB)
    for e in range(E):
        c[[e, 32 + e, 64 + e], C_SEL + e * P:C_SEL + (e + 1) * P] = 1.0
    return c


def rotary_tables():
    half = np.arange(0, DH, 2, dtype=np.float32)
    inv = (np.float32(1.0) / np.float32(10000.0) ** (half / np.float32(DH))).astype(np.float32)
    t = np.arange(L, dtype=np.float32)
    fr = (t[:, None] * inv[None]).astype(np.float32).astype(np.float64)
    base = (half + np.float32(0.4 * DH)) / np.float32(1.4 * DH)
    power = (t - L // 2) / np.float32(WINDOW // 2)
    sc = base[None].astype(np.float64) ** power[:, None].astype(np.float64)
    two = lambda a: np.concatenate([a, a], 1).T
    cos, sin, sc = two(np.cos(fr)), two(np.sin(fr)), two(sc)
    sign = np.where(np.arange(DH) < DH // 2, -1.0, 1.0)[:, None]
    tabs = [cos * sc * QK_SCALE, sign * sin * sc * QK_SCALE, cos / sc, sign * sin / sc]
    return np.stack([np.tile(a, (2, 1)) for a in tabs], 1).astype(np.float32)


def position_tables():
    pos = (np.arange(L, dtype=np.float32) / np.float32(L) * np.float32(2 * np.pi)).astype(np.float64)
    t = np.stack([np.sin(pos), np.cos(pos), np.sin(pos / 2), np.cos(pos / 2)])
    return np.tile(t[None], (NH, 1, 1)).astype(np.float32)


START = 1


def at(n, per, k=0):
    return n * per + k


def reuse(n, per, k, depth):
    return at(n, per, k - depth + 1 if k >= depth else 0)


def build(nc, I, out, stop=None):
    ctx = ExitStack()
    with ctx:
        sems = {}

        def s(name):
            if name not in sems:
                sems[name] = ctx.enter_context(nc.semaphore(name))
            return sems[name]

        def sb(name, shape, dt=F32):
            return ctx.enter_context(nc.sbuf_tensor(name, shape, dt))

        PS = ctx.enter_context(nc.psum_tensor("PS", [P, 8, 512], F32))
        q_dram = nc.dram_tensor("q_split", (3, D, B, L), BF16).ap()
        k_dram = nc.dram_tensor("k_split", (3, D, B, L), BF16).ap()
        mq_dram = nc.dram_tensor("mask_q", (NH, MF, L), F32).ap()
        mk_dram = nc.dram_tensor("mask_k", (NH, MF, L), F32).ap()
        o_dram = nc.dram_tensor("heads_out", (2, D, B, L), F32).ap()

        xT = sb("xT", [P, B, L])
        con = sb("con", [P, C_N])
        ident, ones = con[:, C_ID:C_ID + P], con[:, C_ONES:C_ONES + P]
        blk64, blk8 = con[:, C_BLK64:C_BLK64 + P], con[:, C_BLK8:C_BLK8 + P]
        mean_w = sb("mean_w", [P, P])
        ident_b = sb("ident_b", [P, P], BF16)
        mask_b = sb("mask_b", [P, TPB, P], BF16)
        sel_b = sb("sel_b", [P, E, P], BF16)
        col = sb("col", [P, 8])
        c_eps, c_tiny, c_norm, c_1e6, c_one, c_zero, c_neg = (col[:, i:i + 1] for i in range(7))
        fcol = sb("fcol", [P, DEPTH, 16])
        aw = sb("aw", [P, 4, D])
        acol = sb("acol", [P, 8])
        bv_row = sb("bv_row", [P, D])
        sgu = sb("sgu", [P, 2 * FS])
        sdn = sb("sdn", [P, D])
        rw = sb("rw", [P, E])
        mcol = sb("mcol", [P, 2])
        tqkv = sb("tqkv", [P, 3 * D])
        tcol = sb("tcol", [P, 8])
        th_g = sb("th_g", [P, TH])
        th_v = sb("th_v", [P, TH])
        th_pT = sb("th_pT", [P, TH])
        th_p = sb("th_p", [P, 4, D])
        tpw = sb("tpw", [P, D])
        lnc, lnq, lnr, lnt = (sb(n, [P, L]) for n in ("ln_centered", "ln_square", "ln_rstd", "ln_scaled"))
        BIG, ARENA, ARENA_R = 12400, 29800, 18432
        with ExitStack() as plain:
            big = plain.enter_context(nc.sbuf_tensor("big", [P, BIG], F32))
            arena = plain.enter_context(nc.sbuf_tensor("arena", [P, ARENA], F32))
        big_r, arena_r = sb("big_r", [P, BIG], F32R), sb("arena_r", [P, ARENA_R], F32R)
        memory, taken = [big], [0]

        def stage_memory(m=arena):
            memory[0], taken[0] = m, 0

        def carve(shape, dt=F32):
            n = int(np.prod(shape))
            w = (n + 1) // 2 if dt == BF16 else n
            a = memory[0][:, taken[0]:taken[0] + w]
            taken[0] += w
            assert taken[0] <= memory[0].shape[1], taken
            if dt not in (F32, F32R):
                a = a.bitcast(dt)
            if len(shape) == 1:
                return a
            names = "abcd"[:len(shape)]
            return a.rearrange(f"p ({' '.join(names)}) -> p {' '.join(names)}", **dict(zip(names, shape)))

        stage_memory(big)
        rot = carve([DEPTH, 4, L])
        wqkv = carve([DEPTH, 3 * INNER])
        wswap = carve([DEPTH, 2 * HEADS, 2, DH // 2])
        wo = carve([DEPTH, NCH, D])
        w1 = carve([DEPTH, 2 * HID])
        w2 = carve([DEPTH, 3, D])
        stage_memory(big)
        gu = carve([E, 2 * F])
        dn = carve([E, FCH, D])
        stage_memory(big_r)
        carve([DEPTH, 4, L], F32R)
        wqkv_lo = carve([DEPTH, 3 * INNER], F32R)
        wswap_lo = carve([DEPTH, 2 * HEADS, 2, DH // 2], F32R)
        stage_memory(big_r)
        gu_lo = carve([E, 2 * F], F32R)
        dn_lo = carve([E, FCH, D], F32R)

        STAGES = ["load", "ffn0", "attn", "ffn1", "moe0", "ttt", "moe1"]
        if stop:
            STAGES = STAGES[:STAGES.index(stop) + 1]
        first_ln = {"ffn0": 0, "attn": 12, "ffn1": 16, "moe0": 28, "ttt": 32, "moe1": 36}

        def x_of(name):
            return B * STAGES.index(name)

        def plain_wait(eng):
            eng.sem_inc(s("passed"), 1)

        def ln_mean(src, bank):
            nc.tensor.matmul(PS[:, bank, :], mean_w[:], src, start=True, stop=True).then_inc(s("ln_sums"), 1)

        def ln_variance(e, bank):
            pe = nc.tensor
            pe.wait_ge(s("ln_squared"), START + e + 1)
            pe.matmul(PS[:, bank, :], mean_w[:], lnq[:], start=True, stop=True).then_inc(s("ln_sums"), 1)

        def ln_pe(src, e, mean_bank, var_bank):
            ln_mean(src, mean_bank)
            ln_variance(e, var_bank)

        def ln_square(e):
            act = nc.scalar
            act.wait_ge(s("ln_centred"), START + e + 1)
            act.activation(lnq[:], lnc[:], ACT.Square).then_inc(s("ln_squared"), 1)

        def ln_rstd(e, var_bank):
            act = nc.scalar
            act.wait_ge(s("ln_sums"), START + at(e, 2, 2))
            act.activation(lnr[:], PS[:, var_bank, :], ACT.Ln, bias=c_eps).then_inc(s("ln_rstd_step"), 1)
            act.wait_ge(s("ln_rstd_step"), START + at(e, 2, 1))
            act.activation(lnr[:], lnr[:], ACT.Exp, scale=-0.5).then_inc(s("ln_rstd_step"), 1)

        def ln_act(e, var_bank):
            ln_square(e)
            ln_rstd(e, var_bank)

        def ln_centre(src, e, mean_bank):
            v = nc.vector
            v.wait_ge(s("ln_sums"), START + at(e, 2, 1))
            v.tensor_tensor(lnc[:], src, PS[:, mean_bank, :], ALU.subtract).then_inc(s("ln_centred"), 1)

        def ln_scale(e, gamma, beta, dst, free=()):
            v = nc.vector
            v.wait_ge(s("ln_rstd_step"), START + at(e, 2, 2))
            v.scalar_tensor_tensor(lnt[:], lnc[:], gamma, lnr[:], ALU.mult, ALU.mult).then_inc(s("ln_scaled_done"), 1)
            v.wait_ge(s("ln_scaled_done"), START + e + 1)
            for name, count in free:
                v.wait_ge(s(name), START + count)
            v.tensor_scalar(dst, lnt[:], beta, None, ALU.add).then_inc(s("ln_done"), 1)

        def ln_dve(src, e, mean_bank, gamma, beta, dst, free=()):
            ln_centre(src, e, mean_bank)
            ln_scale(e, gamma, beta, dst, free)

        def product(pe, bank, weights, hi, lo, first=True, last=True):
            w_hi, w_lo = weights
            pe.matmul(bank, w_hi, hi, start=first, stop=False)
            pe.matmul(bank, w_hi, lo, start=False, stop=False)
            return pe.matmul(bank, w_lo, hi, start=False, stop=last)

        stage_memory(arena_r)
        h_hi, h_lo = carve([WINDOW + L], F32R), carve([WINDOW + L], F32R)
        wqkv_hi = carve([DEPTH, 3 * INNER], F32R)
        wswap_hi = carve([DEPTH, 2 * HEADS, 2, DH // 2], F32R)
        memory[0] = arena
        y = carve([B, L])
        t_sq = carve([2, L])
        start = taken[0]
        t_cos, t_sin, t_rot, t_rn = (carve([2, L]) for _ in range(4))
        end, taken[0] = taken[0], start
        gl = carve([2, L])
        hid = carve([3, L])
        assert taken[0] <= end
        taken[0] = end
        qs = carve([NCH, L])
        ks = carve([NCH, WINDOW + L])
        vs = carve([2, TPB, INNER])
        pr = carve([2, 4, P])
        pn = carve([2, 4, P])
        pT = carve([2, 4, P])
        nmax, psum_, pinv = (carve([2, 4]) for _ in range(3))
        oT = carve([NCH, L])
        h2 = carve([L])
        ln2 = carve([L])

        PIECES = 2 * NCH
        FIRST = 3

        def ffn_walk(eng, f, enter, project, normalise, project_values, step, tail):
            first = B * DEPTH * f
            enter(first, 0, 0, None)
            for j in range(PIECES + 1):
                if j < PIECES:
                    project(first, 0, j)
                if j:
                    normalise(first, j - 1, f == 0)
            for i in range(2 * TPB):
                project_values(first, 0, i)

            def one(layer, b, nx):
                N = b + B * (DEPTH * f + layer)
                for u in range(PIECES + FIRST + 1):
                    step(N, u, nx)
                tail(N, layer, b, nx)

            for layer in range(DEPTH):
                with eng.Fori(0, B - 1) as b:
                    one(layer, b, (b + 1 + B * (DEPTH * f + layer), layer, b + 1))
                one(layer, B - 1, (B * (DEPTH * f + layer + 1), layer + 1, 0) if layer + 1 < DEPTH else None)

        def e_input(f, b, prologue):
            return first_ln[f"ffn{f}"] + (0 if prologue else 2 * b - 1)

        def e_hidden(f, layer, b):
            if layer == 0:
                return first_ln[f"ffn{f}"] + (2 * b + 2 if type(b) is not int else 2 * B - 1)
            return b + (first_ln[f"ffn{f}"] + 2 * B)

        def ffn_weights():
            return [(w[:, layer], hi[:, layer], lo[:, layer]) for layer in range(DEPTH)
                    for w, hi, lo in ((wqkv, wqkv_hi, wqkv_lo), (wswap, wswap_hi, wswap_lo))]

        FFN_SPLITS = 2 * DEPTH

        def ffn_pe(pe, f):
            pe.wait_ge(s("low_by_dve"), START + FFN_SPLITS * (f + 1))

            def enter(N, layer, b, part):
                if layer == 0:
                    e = e_input(f, b, part is None)
                    if part in (0, None):
                        ln_mean(xT[:, b, :], 5)
                    if part in (1, None):
                        ln_variance(e, 6)

            def project(N, layer, j):
                J = at(N, PIECES, j)
                if j == 0:
                    pe.wait_ge(s("h_ready"), START + at(N, 4, 4))
                pe.wait_ge(s("rot_products"), START + J)
                pe.wait_ge(s("qk_squared"), START + J)
                c = j // 2 + (NCH if j % 2 else 0)
                h = (h_hi[:, WINDOW:], h_lo[:, WINDOW:])
                w = tuple(a[:, layer, c * P:(c + 1) * P] for a in (wqkv_hi, wqkv_lo))
                product(pe, PS[:, 5, :], w, *h).then_inc(s("proj"), 1)
                w = tuple(a[:, layer, 2 * c:2 * c + 2, :, :].rearrange("p a b c -> p (a b c)") for a in (wswap_hi, wswap_lo))
                product(pe, PS[:, 6, :], w, *h).then_inc(s("proj"), 1)

            def normalise(N, j, _):
                J = at(N, PIECES, j)
                pe.wait_ge(s("qk_squared"), START + J + 1)
                pe.wait_ge(s("qk_log"), START + J)
                pe.matmul(PS[:, 7, :], blk64, t_sq[:, j % 2, :], start=True, stop=True).then_inc(s("qk_sums"), 1)

            def project_values(N, layer, i):
                off = WINDOW + (i % TPB) * P if i < TPB else (i % TPB) * P
                if i == 0:
                    pe.wait_ge(s("p_exp"), START + at(N, TPB * UNITS))
                if i >= 2:
                    pe.wait_ge(s("v_act" if i % 2 == 0 else "v_dve"), START + at(N, TPB, i // 2))
                product(pe, PS[:, i % 2, :], (h_hi[:, off:off + P], h_lo[:, off:off + P]), wqkv_hi[:, layer, 2 * INNER:],
                        wqkv_lo[:, layer, 2 * INNER:]).then_inc(s("v_proj"), 1)

            def scores(N, u):
                c, par = u // 2, u % 2
                if u == 0:
                    pe.wait_ge(s("qk_scaled"), START + at(N, PIECES, PIECES))
                    pe.wait_ge(s("v_act"), START + at(N, TPB, TPB))
                    pe.wait_ge(s("v_dve"), START + at(N, TPB, TPB))
                    pe.wait_ge(s("hid_ready"), START + at(N, 3))
                if u >= 2:
                    pe.wait_ge(s("p_exp"), START + at(N, TPB * UNITS, TPB * (u - 1)))
                pe.matmul(PS[:, par, :], ident_b[:], mask_b[:].rearrange("p a b -> p (a b)"), start=True, stop=False,
                          skip_group_check=True)
                r = slice(DH * par, DH * par + DH)
                for t in range(TPB):
                    for w in range(2):
                        a = t * P + w * WINDOW
                        mm = pe.matmul(PS[w * WINDOW:(w + 1) * WINDOW, par, t * P:(t + 1) * P], qs[r, c, a:a + WINDOW],
                                       ks[r, c, a:a + 2 * WINDOW], start=False, stop=True, skip_group_check=True)
                mm.then_inc(s("scores_ready"), 1)

            def turned(N, u):
                pe.wait_ge(s("p_normed"), START + at(N, UNITS, u + 1))
                if u >= 2:
                    pe.wait_ge(s("pT_ready"), START + at(N, UNITS, u - 1))
                for t in range(TPB):
                    tr = pe.transpose(PS[:, 2 + u % 2, t * P:(t + 1) * P], pn[:, u % 2, t, :], ident)
                tr.then_inc(s("pT_done"), 1)

            def values(N, u):
                c, par = u // 2, u % 2
                pe.wait_ge(s("pT_ready"), START + at(N, UNITS, u + 1))
                if u == 0:
                    pe.wait_ge(s("y_added"), START + at(N, 1))
                elif par == 0:
                    pe.wait_ge(s("oT_ready"), START + at(N, NCH, c))
                for t in range(TPB):
                    for w in range(2):
                        mm = pe.matmul(PS[DH * par:DH * par + DH, 4, t * P + w * WINDOW:t * P + (w + 1) * WINDOW],
                                       vs[:, 1 - w, t, u * DH:(u + 1) * DH], pT[:, par, t, w * WINDOW:(w + 1) * WINDOW],
                                       start=True, stop=True)
                mm.then_inc(s("pv_done"), 1)

            def step(N, u, nx):
                if nx and u == 0:
                    enter(*nx, 0)
                if u < UNITS:
                    scores(N, u)
                if nx:
                    if u == 0:
                        enter(*nx, 1)
                    if FIRST <= u < PIECES + FIRST:
                        project(nx[0], nx[1], u - FIRST)
                    if FIRST < u <= PIECES + FIRST:
                        normalise(nx[0], u - FIRST - 1, False)
                if 1 <= u <= UNITS:
                    turned(N, u - 1)
                if 2 <= u <= UNITS + 1:
                    values(N, u - 2)

            def tail(N, layer, b, nx):
                e = e_hidden(f, layer, b)

                def fill(*pieces):
                    for i in pieces if nx else ():
                        project_values(nx[0], nx[1], i)

                pe.wait_ge(s("oT_ready"), START + at(N, NCH, NCH))
                for c in range(NCH):
                    mm = pe.matmul(PS[:, 2, :], wo[:, layer, c, :], oT[:, c, :], start=c == 0, stop=c == NCH - 1)
                mm.then_inc(s("wo_ready"), 1)
                fill(0, 1, 2)
                pe.wait_ge(s("h2_ready"), START + at(N, 2, 2))
                ln_mean(h2[:], 3)
                fill(3, 4)
                ln_variance(e, 4)
                fill(5, 6, 7)
                pe.wait_ge(s("ln_done"), START + e + 1)
                for c, (o, n) in enumerate(HCH):
                    if c >= 2:
                        pe.wait_ge(s("hid_ready"), START + at(N, 3, c - 1))
                    pe.matmul(PS[0:n, 2 + c % 2, :], w1[:, layer, o:o + n], ln2[:], start=True, stop=True).then_inc(s("ffn_proj"), 1)
                    pe.matmul(PS[0:n, 5 + c % 2, :], w1[:, layer, HID + o:HID + o + n], ln2[:], start=True,
                              stop=True).then_inc(s("ffn_proj"), 1)
                for c, (o, n) in enumerate(HCH):
                    pe.wait_ge(s("hid_ready"), START + at(N, 3, c + 1))
                    mm = pe.matmul(PS[:, 4, :], w2[0:n, layer, c, :], hid[0:n, c, :], start=c == 0, stop=c == 2)
                mm.then_inc(s("ffn_out"), 1)

            ffn_walk(pe, f, enter, project, normalise, project_values, step, tail)

        def ffn_act(act, f):
            def enter(N, layer, b, part):
                e = e_input(f, b, part is None)
                if layer == 0 and part in (0, None):
                    ln_square(e)
                if layer == 0 and part in (1, None):
                    ln_rstd(e, 6)
                if part in (0, 1):
                    return
                if layer == 0:
                    act.wait_ge(s("ln_done"), START + e + 1)
                else:
                    act.wait_ge(s("y_added"), START + at(N, 1, -3))
                act.wait_ge(s("v_proj"), START + at(N, 2 * TPB))
                plain_wait(act)
                act.activation(h_hi[64:128, WINDOW + 1:WINDOW + L], y[64:128, b, 0:L - 1], ACT.Copy).then_inc(s("h_ready"), 1)

            def project(N, layer, j):
                act.wait_ge(s("rot_cos"), START + at(N, PIECES, j + 1))
                act.wait_ge(s("qk_sums"), START + reuse(N, PIECES, j, 2))
                act.activation(t_sq[:, j % 2, :], PS[:, 5, :], ACT.Square).then_inc(s("qk_squared"), 1)

            def normalise(N, j, _):
                J = at(N, PIECES, j)
                act.wait_ge(s("qk_sums"), START + J + 1)
                act.wait_ge(s("qk_rnorm"), START + reuse(N, PIECES, j, 2))
                act.wait_ge(s("qk_scaled"), START + reuse(N, PIECES, j, 2))
                act.activation(t_rn[:, j % 2, :], PS[:, 7, :], ACT.Ln, bias=c_tiny, scale=2.0 ** LS).then_inc(s("qk_log"), 1)
                act.wait_ge(s("qk_log"), START + J + 1)
                act.activation(t_rn[:, j % 2, :], t_rn[:, j % 2, :], ACT.Exp, bias=c_norm, scale=-0.5).then_inc(s("qk_rnorm"), 1)

            def project_values(N, layer, i):
                if i % 2 == 0:
                    if i == 0:
                        act.wait_ge(s("pv_done"), START + at(N, UNITS))
                    act.wait_ge(s("v_proj"), START + at(N, 2 * TPB, i + 1))
                    act.activation(vs[:, i // TPB, i % TPB, :], PS[:, 0, :], ACT.Copy).then_inc(s("v_act"), 1)

            def step(N, u, nx):
                if nx and u == 0:
                    enter(*nx, 0)
                if u < UNITS:
                    act.wait_ge(s("nmax_ready"), START + at(N, UNITS, u + 1))
                    act.wait_ge(s("p_normed"), START + reuse(N, UNITS, u, 2))
                    for t in range(TPB):
                        act.activation(pr[:, u % 2, t, :], PS[:, u % 2, t * P:(t + 1) * P], ACT.Exp,
                                       bias=nmax[:, u % 2, t:t + 1],
                                       accum_out=psum_[:, u % 2, t:t + 1]).then_inc(s("p_exp"), 1)
                if nx:
                    if u < 2:
                        enter(*nx, u + 1)
                    if FIRST <= u < PIECES + FIRST:
                        project(nx[0], nx[1], u - FIRST)
                    if FIRST < u <= PIECES + FIRST:
                        normalise(nx[0], u - FIRST - 1, False)
                if u >= 3 and u % 2 and u <= UNITS + 1:
                    c = (u - 3) // 2
                    act.wait_ge(s("pv_done"), START + at(N, UNITS, 2 * c + 2))
                    if c == 0:
                        act.wait_ge(s("wo_ready"), START + at(N, 1))
                    act.activation(oT[:, c, :], PS[:, 4, :], ACT.Copy).then_inc(s("oT_ready"), 1)

            def tail(N, layer, b, nx):
                e = e_hidden(f, layer, b)

                def fill(i):
                    if nx:
                        project_values(nx[0], nx[1], i)

                fill(0)
                act.wait_ge(s("wo_added"), START + at(N, 1, 1))
                plain_wait(act)
                act.activation(h2[64:128, 1:L], y[64:128, b, 0:L - 1], ACT.Copy).then_inc(s("h2_ready"), 1)
                fill(2)
                ln_square(e)
                fill(4)
                ln_rstd(e, 4)
                fill(6)
                for c, (o, n) in enumerate(HCH):
                    act.wait_ge(s("ffn_proj"), START + at(N, 6, 2 * c + 2))
                    act.wait_ge(s("hid_ready"), START + reuse(N, 3, c, 2))
                    act.activation(gl[0:n, c % 2, :], PS[0:n, 5 + c % 2, :], ACT.Gelu,
                                   bias=fcol[0:n, layer, 10 + c:11 + c]).then_inc(s("gelu_ready"), 1)
                act.preload_act_table_set("natural_log_exp_and_others")

            act.preload_act_table_set("natural_log_exp_and_others")
            if f:
                act.wait_ge(s("ffn_loaded"), START + 80)
            for w, hi, _ in ffn_weights():
                act.activation(hi, w, ACT.Copy).then_inc(s("weights_high"), 1)
            ffn_walk(act, f, enter, project, normalise, project_values, step, tail)

        def ffn_dve(v, f):
            def enter(N, layer, b, part):
                e = e_input(f, b, part is None)
                if layer == 0 and part in (0, None):
                    ln_centre(xT[:, b, :], e, 5)
                if part in (0, 1):
                    return
                if layer == 0:
                    ln_scale(e, c_one, c_zero, y[:, b, :])
                    v.wait_ge(s("ln_done"), START + e + 1)
                else:
                    v.wait_ge(s("y_added"), START + at(N, 1, -3))
                v.wait_ge(s("v_proj"), START + at(N, 2 * TPB))
                plain_wait(v)
                v.tensor_copy(h_hi[0:64, WINDOW:], y[0:64, b, :]).then_inc(s("h_ready"), 1)
                v.wait_ge(s("h_ready"), START + at(N, 4, 2))
                v.tensor_tensor(h_lo[0:64, WINDOW:], y[0:64, b, :], h_hi[0:64, WINDOW:].bitcast(F32),
                                ALU.subtract).then_inc(s("h_ready"), 1)
                v.tensor_tensor(h_lo[64:128, WINDOW + 1:WINDOW + L], y[64:128, b, 0:L - 1],
                                h_hi[64:128, WINDOW + 1:WINDOW + L].bitcast(F32), ALU.subtract).then_inc(s("h_ready"), 1)

            def project(N, layer, j):
                tab = 2 * (j % 2)
                v.wait_ge(s("qk_rotated"), START + reuse(N, PIECES, j, 2))
                v.wait_ge(s("proj"), START + at(N, 2 * PIECES, 2 * j + 1))
                v.tensor_tensor(t_cos[:, j % 2, :], PS[:, 5, :], rot[:, layer, tab, :], ALU.mult).then_inc(s("rot_cos"), 1)
                v.wait_ge(s("proj"), START + at(N, 2 * PIECES, 2 * j + 2))
                v.tensor_tensor(t_sin[:, j % 2, :], PS[:, 6, :], rot[:, layer, tab + 1, :],
                                ALU.mult).then_inc(s("rot_products"), 1)

            def normalise(N, j, fresh):
                J, c = at(N, PIECES, j), j // 2
                v.wait_ge(s("qk_rotated"), START + J + 1)
                v.wait_ge(s("qk_rnorm"), START + J + 1)
                if not fresh:
                    v.wait_ge(s("scores_ready"), START + at(N, UNITS, 2 * c + 2 - UNITS))
                dst = qs[:, c, :] if j % 2 == 0 else ks[:, c, WINDOW:]
                v.scalar_tensor_tensor(dst, t_rn[:, j % 2, :], 1e12, t_rot[:, j % 2, :], ALU.min,
                                       ALU.mult).then_inc(s("qk_scaled"), 1)

            def project_values(N, layer, i):
                if i % 2:
                    if i == 1:
                        v.wait_ge(s("pv_done"), START + at(N, UNITS))
                    v.wait_ge(s("v_proj"), START + at(N, 2 * TPB, i + 1))
                    v.tensor_copy(vs[:, i // TPB, i % TPB, :], PS[:, 1, :]).then_inc(s("v_dve"), 1)

            def step(N, u, nx):
                if nx and u == 0:
                    enter(*nx, 0)
                if u < UNITS:
                    v.wait_ge(s("scores_ready"), START + at(N, UNITS, u + 1))
                    v.wait_ge(s("p_exp"), START + at(N, TPB * UNITS, TPB * (u - 1) if u >= 2 else 0))
                    v.tensor_reduce(nmax[:, u % 2, :], PS[:, u % 2, :].rearrange("p (a b) -> p a b", a=TPB), AX.X,
                                    ALU.max, negate=True).then_inc(s("nmax_ready"), 1)
                if nx:
                    if FIRST <= u < PIECES + FIRST:
                        project(nx[0], nx[1], u - FIRST)
                if u < UNITS:
                    v.wait_ge(s("p_exp"), START + at(N, TPB * UNITS, TPB * u + TPB))
                    v.wait_ge(s("p_normed"), START + reuse(N, UNITS, u, 2))
                    v.reciprocal(pinv[:, u % 2, :], psum_[:, u % 2, :]).then_inc(s("pinv_ready"), 1)
                if 1 <= u <= UNITS:
                    w = u - 1
                    v.wait_ge(s("pT_done"), START + at(N, UNITS, w + 1))
                    v.wait_ge(s("pv_done"), START + reuse(N, UNITS, w, 2))
                    v.tensor_copy(pT[:, w % 2, :, :].rearrange("p a b -> p (a b)"), PS[:, 2 + w % 2, :]).then_inc(s("pT_ready"), 1)
                if nx and u == 1:
                    enter(*nx, 2)
                if nx and FIRST < u <= PIECES + FIRST:
                    normalise(nx[0], u - FIRST - 1, False)

            def tail(N, layer, b, nx):
                e = e_hidden(f, layer, b)

                def fill(i):
                    if nx:
                        project_values(nx[0], nx[1], i)

                v.wait_ge(s("wo_ready"), START + at(N, 1, 1))
                v.tensor_tensor(y[:, b, :], y[:, b, :], PS[:, 2, :], ALU.add).then_inc(s("wo_added"), 1)
                v.wait_ge(s("wo_added"), START + at(N, 1, 1))
                plain_wait(v)
                v.tensor_copy(h2[0:64], y[0:64, b, :]).then_inc(s("h2_ready"), 1)
                fill(1)
                v.wait_ge(s("h2_ready"), START + at(N, 2, 2))
                ln_centre(h2[:], e, 3)
                fill(3)
                fill(5)
                ln_scale(e, fcol[:, layer, 4:5], fcol[:, layer, 5:6], ln2)
                fill(7)
                for c, (o, n) in enumerate(HCH):
                    v.wait_ge(s("gelu_ready"), START + at(N, 3, c + 1))
                    v.scalar_tensor_tensor(hid[0:n, c, :], PS[0:n, 2 + c % 2, :], fcol[0:n, layer, 7 + c:8 + c],
                                           gl[0:n, c % 2, :], ALU.add, ALU.mult).then_inc(s("hid_ready"), 1)
                v.wait_ge(s("ffn_out"), START + at(N, 1, 1))
                v.scalar_tensor_tensor(y[:, b, :], PS[:, 4, :], fcol[:, layer, 6:7], y[:, b, :], ALU.add,
                                       ALU.add).then_inc(s("y_added"), 1)
                if layer == DEPTH - 1:
                    v.wait_ge(s("y_added"), START + at(N, 1, 1))
                    v.scalar_tensor_tensor(xT[:, b, :], y[:, b, :], 0.5, xT[:, b, :], ALU.mult, ALU.add).then_inc(s("x_ready"), 1)

            if f:
                v.wait_ge(s("ffn_loaded"), START + 80)
            for k, (w, hi, lo) in enumerate(ffn_weights()):
                v.wait_ge(s("weights_high"), START + FFN_SPLITS * f + k + 1)
                v.tensor_tensor(lo, w, hi.bitcast(F32), ALU.subtract).then_inc(s("low_by_dve"), 1)
            ffn_walk(v, f, enter, project, normalise, project_values, step, tail)

        def ffn_pool(g, f):
            def project(N, layer, j):
                g.wait_ge(s("rot_cos"), START + at(N, PIECES, j + 1))
                g.wait_ge(s("rot_products"), START + at(N, PIECES, j + 1))
                g.wait_ge(s("qk_scaled"), START + reuse(N, PIECES, j, 2))
                g.tensor_tensor(t_rot[:, j % 2, :], t_cos[:, j % 2, :], t_sin[:, j % 2, :], ALU.add).then_inc(s("qk_rotated"), 1)

            def step(N, u, nx):
                if nx and FIRST <= u < PIECES + FIRST:
                    project(nx[0], nx[1], u - FIRST)
                if u < UNITS:
                    g.wait_ge(s("pinv_ready"), START + at(N, UNITS, u + 1))
                    g.wait_ge(s("pT_done"), START + reuse(N, UNITS, u, 2))
                    g.tensor_tensor(pn[:, u % 2, :, :], pr[:, u % 2, :, :],
                                    pinv[:, u % 2, :].unsqueeze(2).broadcast_to([P, TPB, P]), ALU.mult).then_inc(s("p_normed"), 1)

            def nothing(*_):
                pass

            ffn_walk(g, f, nothing, project, nothing, nothing, step, nothing)

        def ffn_zero_pads(g, f):
            g.wait_ge(s("x_ready"), START + x_of(f"ffn{f}"))
            if f == 0:
                g.wait_ge(s("mask_stored"), START + 32)
            zeros = t_sq[:, 0, 0:WINDOW + 1]
            g.memset(zeros, 0.0).then_inc(s("pads_zero"), 1)
            g.wait_ge(s("pads_zero"), START + 5 * f + 1)
            for h in (h_hi, h_lo):
                g.tensor_copy(h[:, 0:WINDOW + 1], zeros).then_inc(s("pads_zero"), 1)
            g.memset(ks[:, :, 0:WINDOW], 0.0).then_inc(s("pads_zero"), 1)
            g.memset(h2[:, 0:1], 0.0).then_inc(s("pads_zero"), 1)

        stage_memory()
        pos = carve([4, L])
        m_q = carve([MF, L])
        m_k = carve([MF, L])
        m_t = carve([6, L])
        ang, turns, ang_f, sc = (carve([8]) for _ in range(4))
        turns_i = turns.bitcast(I32)
        phase = carve([8])

        def load_sync(sp):
            sp.dma_start(phase[0:NH, :], I["phase"]).then_inc(s("phase_loaded"), 16)
            sp.dma_start(pos[0:NH, :, :], I["pos"]).then_inc(s("phase_loaded"), 16)
            for name, dst in (("acol", acol), ("aw", aw), ("bv_row", bv_row)):
                sp.dma_start(dst[:], I[name]).then_inc(s("attn_loaded"), 16)
            for name, dst in (("xT", xT[:]), ("con", con[:]), ("fcol", fcol[:]), ("wqkv", wqkv), ("wswap", wswap)):
                sp.dma_start(dst, I[name]).then_inc(s("first_loads"), 16)
            for layer in range(DEPTH):
                sp.dma_start(rot[:, layer, :, :], I["rot"]).then_inc(s("first_loads"), 16)
            sp.dma_start(wo, I["wo"]).then_inc(s("ffn_loaded"), 16)
            sp.dma_start(w1, I["w1"]).then_inc(s("ffn_loaded"), 16)
            sp.dma_start(w2, I["w2"]).then_inc(s("ffn_loaded"), 16)
            sp.wait_ge(s("mask_rows"), START + 2)
            sp.dma_start(mq_dram.rearrange("h f n -> h (f n)"), m_q[0:NH].rearrange("p a b -> p (a b)")).then_inc(s("mask_stored"), 16)
            sp.dma_start(mk_dram.rearrange("h f n -> h (f n)"), m_k[0:NH].rearrange("p a b -> p (a b)")).then_inc(s("mask_stored"), 16)
            for name, dst in (("sgu", sgu), ("sdn", sdn), ("rw", rw), ("mcol", mcol)):
                sp.dma_start(dst[:], I[name]).then_inc(s("late_loads"), 16)
            for name, dst in (("tqkv", tqkv), ("tcol", tcol), ("th_g", th_g), ("th_v", th_v), ("th_pT", th_pT),
                              ("th_p", th_p), ("tpw", tpw)):
                sp.dma_start(dst[:], I[name]).then_inc(s("late_loads"), 16)

        def load_experts(sp, m):
            sp.wait_ge(s("x_ready"), START + x_of("ttt" if m else "moe0"))
            for e in range(E):
                sp.dma_start(gu[:, e, :], I["gu"][:, e, :]).then_inc(s(f"experts{e // 4}_loaded"), 16)
                sp.dma_start(dn[:, e, :, :], I["dn"][:, e, :, :]).then_inc(s(f"experts{e // 4}_loaded"), 16)

        def load_dve(v):
            for i, val in enumerate((LN_EPS, 2.0 ** -60, 0.5 * LS * LN2, 1e-6, 1.0, 0.0, -0.5 * LS * LN2)):
                v.memset(col[:, i:i + 1], val).then_inc(s("columns"), 1)
            mask_factors(v)
            v.wait_ge(s("columns"), START + 7)
            v.wait_ge(s("first_loads"), START + 112)
            v.tensor_scalar(mean_w[:], ones, 1.0 / D, None, ALU.mult).then_inc(s("consts"), 1)
            v.tensor_copy(ident_b[:], ident).then_inc(s("consts"), 1)
            m = con[:, C_MASK:C_MASK + 2 * P].rearrange("p (a b) -> p a b", a=2)
            for t in range(TPB):
                v.tensor_copy(mask_b[:, t, :], m[:, 1 if t else 0, :]).then_inc(s("consts"), 1)
            v.tensor_copy(sel_b[:].rearrange("p a b -> p (a b)"), con[:, C_SEL:]).then_inc(s("consts"), 1)
            v.tensor_copy(col[:, 7:8], c_one).then_inc(s("x_ready"), B)
            for layer in range(DEPTH):
                for i in range(4):
                    v.tensor_scalar(rot[:, layer, i, :], rot[:, layer, i, :], fcol[:, layer, i:i + 1], None,
                                    ALU.mult).then_inc(s("rot_scaled"), 1)

        def mask_factors(v):
            steps = [0]

            def then(ins):
                steps[0] += 1
                ins.then_inc(s("mask_step"), 1)
                v.wait_ge(s("mask_step"), START + steps[0])

            h = slice(0, NH)
            pi = float(np.pi)
            two_pi_hi = float(np.float32(2 * np.pi))
            two_pi_lo = float(2 * np.pi - two_pi_hi)
            v.wait_ge(s("phase_loaded"), START + 32)
            then(v.tensor_copy(ang[h, 0:3], phase[h, 0:3]))
            then(v.tensor_scalar(ang[h, 3:6], phase[h, 0:3], pi / 2, None, ALU.add))
            then(v.tensor_scalar(ang_f[h, 0:6], ang[h, 0:6], 1.0 / (2 * pi), None, ALU.mult))
            then(v.tensor_copy(turns_i[h, 0:6], ang_f[h, 0:6]))
            then(v.tensor_copy(ang_f[h, 0:6], turns_i[h, 0:6]))
            for part in (two_pi_hi, two_pi_lo):
                then(v.scalar_tensor_tensor(ang[h, 0:6], ang_f[h, 0:6], -part, ang[h, 0:6], ALU.mult, ALU.add))
            for op, bound, turn in ((ALU.is_gt, pi, -two_pi_hi), (ALU.is_lt, -pi, two_pi_hi)):
                then(v.tensor_scalar(ang_f[h, 0:6], ang[h, 0:6], bound, turn, op, ALU.mult))
                then(v.tensor_tensor(ang[h, 0:6], ang[h, 0:6], ang_f[h, 0:6], ALU.add))
            then(v.tensor_scalar(ang[h, 0:6], ang[h, 0:6], 3.1415925, -3.1415925, ALU.min, ALU.max))
            v.tensor_copy(sc[h, 6:7], ang[h, 0:1]).then_inc(s("angles"), 1)
            v.wait_ge(s("sines"), START + 1)
            s0, s1, s2, c0, c1, c2 = (sc[h, i:i + 1] for i in range(6))
            sa, ca, sh, ch = (pos[h, i, :] for i in range(4))

            def angle_sum(dst, t, a, x, b, y, op):
                then(v.tensor_scalar(t, a, x, None, ALU.mult))
                then(v.scalar_tensor_tensor(dst, b, y, t, ALU.mult, op))

            t = m_t[h, 5, :]
            sin_q, cos_q, sin_z, cos_z, sin_k = m_q[h, 0, :], m_t[h, 1, :], m_t[h, 2, :], m_q[h, 1, :], m_t[h, 4, :]
            angle_sum(sin_q, t, ca, s0, sa, c0, ALU.add)
            angle_sum(cos_q, t, sa, s0, ca, c0, ALU.subtract)
            angle_sum(cos_z, t, sh, s2, ch, c2, ALU.subtract)
            angle_sum(sin_z, t, ch, s2, sh, c2, ALU.add)
            angle_sum(m_k[h, 0, :], t, sa, s1, ca, c1, ALU.subtract)
            angle_sum(sin_k, t, ca, s1, sa, c1, ALU.add)
            then(v.tensor_scalar(m_q[h, 2, :], sin_z, -1.0, None, ALU.mult))
            then(v.tensor_tensor(m_q[h, 3, :], cos_q, sin_z, ALU.mult))
            then(v.tensor_tensor(m_q[h, 4, :], cos_q, cos_z, ALU.mult))
            then(v.tensor_scalar(m_q[h, 5, :], sa, 0.0, phase[h, 3:4], ALU.mult, ALU.subtract))
            then(v.tensor_tensor(m_k[h, 1, :], sin_k, ch, ALU.mult))
            then(v.tensor_tensor(m_k[h, 2, :], sin_k, sh, ALU.mult))
            then(v.tensor_copy(m_k[h, 3, :], ch))
            then(v.tensor_copy(m_k[h, 4, :], sh))
            v.memset(m_k[h, 5, :], 1.0).then_inc(s("mask_rows"), 1)
            v.wait_ge(s("attn_loaded"), START + 48)
            then(v.tensor_scalar(acol[:, 4:5], acol[:, 3:4], 1e-6, -1.0, ALU.add, ALU.mult))
            then(v.tensor_scalar(acol[:, 6:7], acol[:, 0:1], A_SCALE, None, ALU.mult))
            v.reciprocal(acol[:, 5:6], acol[:, 4:5]).then_inc(s("mask_rows"), 1)

        def load_act(act):
            act.wait_ge(s("angles"), START + 1)
            act.activation(sc[0:NH, 0:6], ang[0:NH, 0:6], ACT.Sin).then_inc(s("sines"), 1)
            act.wait_ge(s("columns"), START + 7)
            act.wait_ge(s("consts"), START + 7)

        stage_memory()
        xn = carve([L])
        f_qk = carve([2, L])
        rest = carve([2, 2, L])
        parts = carve([2, 3, L], BF16)
        v_all = carve([B * TPB, D])
        v_head = carve([2, B * TPB, 2 * HD])
        q_st = [carve([B, L], BF16) for _ in range(2)]
        k_st = [carve([B, L], BF16) for _ in range(2)]
        mq_st = [carve([L]) for _ in range(2)]
        mk_st = [carve([L]) for _ in range(2)]
        mk = carve([2, TPB, L])
        pp = carve([2, TPB, L])
        ppT = carve([TPB, L])
        a_nmax = carve([2, TPB])
        o_sb = carve([2, B, P])
        o_all, s_all = pp[:, 0, :, :], pp[:, 1, :, :]
        att = f_qk
        inv = rest[:, 0, :, :]

        def attn_proj_pe(pe):
            pe.wait_ge(s("x_ready"), START + x_of("attn"))
            pe.wait_ge(s("attn_loaded"), START + 48)
            with pe.Fori(0, B) as b:
                e = b + first_ln["attn"]
                ln_pe(xT[:, b, :], e, 4, 5)
                pe.wait_ge(s("ln_done"), START + e + 1)
                pe.wait_ge(s("a_biased"), START + at(b, 2))
                for i in range(2):
                    pe.matmul(PS[:, i, :], aw[:, i, :], xn, start=True, stop=True).then_inc(s("a_proj"), 1)
                pe.wait_ge(s("a_values"), START + at(b, 1))
                for t in range(TPB):
                    mm = pe.matmul(PS[:, 2, t * P:(t + 1) * P], xn[:, t * P:(t + 1) * P], aw[:, 2, :], start=True, stop=True)
                mm.then_inc(s("a_proj"), 1)

        def attn_proj_act(act):
            act.wait_ge(s("x_ready"), START + x_of("attn"))
            with act.Fori(0, B) as b:
                e = b + first_ln["attn"]
                ln_act(e, 5)
                for i in range(2):
                    act.wait_ge(s("a_proj"), START + at(b, 3, i + 1))
                    act.wait_ge(s("a_split"), START + at(b, 10))
                    act.activation(f_qk[:, i, :], PS[:, i, :], ACT.Identity, bias=acol[:, 6:7] if i == 0 else acol[:, 1:2],
                                   scale=A_SCALE if i == 0 else 1.0).then_inc(s("a_biased"), 1)

        def attn_proj_dve(v):
            v.wait_ge(s("x_ready"), START + x_of("attn"))
            with v.Fori(0, B) as b:
                e = b + first_ln["attn"]
                ln_dve(xT[:, b, :], e, 4, c_one, c_zero, xn, free=[("a_proj", at(b, 3))])
                v.wait_ge(s("a_proj"), START + at(b, 3, 3))
                v.tensor_tensor(v_all[:, bass.ds(b * TPB, TPB), :], PS[:, 2, :].rearrange("p (a b) -> p a b", a=TPB),
                                bv_row[:].unsqueeze(1).broadcast_to([P, TPB, P]), ALU.add).then_inc(s("a_values"), 1)
                v.wait_ge(s("parts_stored"), START + at(b, 96))
                for st in range(5):
                    for i in range(2):
                        if st == 0:
                            v.wait_ge(s("a_biased"), START + at(b, 2, i + 1))
                        else:
                            v.wait_ge(s("a_split"), START + at(b, 10, 2 * (st - 1) + i + 1))
                        src = f_qk[:, i, :] if st < 2 else rest[:, i, (st - 2) // 2, :]
                        if st % 2 == 0:
                            ins = v.tensor_copy(parts[:, i, st // 2, :], src)
                        else:
                            ins = v.tensor_tensor(rest[:, i, st // 2, :], src, parts[:, i, st // 2, :], ALU.subtract)
                        ins.then_inc(s("a_split"), 1)
            for hp in range(2):
                v.memset(v_head[:, hp, :, HD:], 1.0).then_inc(s("a_values"), 1)

        def attn_proj_sync(sp):
            with sp.Fori(0, B) as b:
                sp.wait_ge(s("a_split"), START + at(b, 10, 10))
                for i, dst in enumerate((q_dram, k_dram)):
                    for part in range(3):
                        sp.dma_start(dst[part, :, b, :], parts[:, i, part, :]).then_inc(s("parts_stored"), 16)

        HEADS_PER_PASS = 2
        STEPS = HEADS_PER_PASS * B
        PASSES = NH // HEADS_PER_PASS
        OUT_ROWS = 32
        STORES = 16 * 2 * TPB
        MASK_OPS = 5

        def attn_sync(sp):
            sp.wait_ge(s("parts_stored"), START + B * 96)
            sp.wait_ge(s("mask_stored"), START + 32)

            def load_head(i, hp, copied=None):
                h = i * HEADS_PER_PASS + hp
                if copied is not None:
                    sp.wait_ge(s("o_copied"), START + copied)
                for st, src, split in ((q_st[hp], q_dram, SPLIT_Q), (k_st[hp], k_dram, SPLIT_K)):
                    for g, part in enumerate(split):
                        sp.dma_start(st[g * HD:(g + 1) * HD], src[part, bass.ds(h * HD, HD), :, :]).then_inc(s(f"head{hp}_loaded"), 16)

            def load_mask_factors(i, hp, copied=None):
                h = i * HEADS_PER_PASS + hp
                if copied is not None:
                    sp.wait_ge(s("o_copied"), START + copied)
                sp.dma_start(mq_st[hp][0:MF], mq_dram[bass.ds(h, 1), :, :].rearrange("a f n -> (a f) n")).then_inc(s(f"factors{hp}_loaded"), 16)
                sp.dma_start(mk_st[hp][0:MF], mk_dram[bass.ds(h, 1), :, :].rearrange("a f n -> (a f) n")).then_inc(s(f"factors{hp}_loaded"), 16)

            def store(i, hp):
                h = i * HEADS_PER_PASS + hp
                sp.wait_ge(s("o_copied"), START + at(i, STEPS, B * (hp + 1)))
                for t in range(TPB):
                    for w in range(2):
                        r = OUT_ROWS * t + w * HD
                        sp.dma_start(o_dram[w, bass.ds(h * HD, HD), :, t * P:(t + 1) * P], o_sb[r:r + HD, hp, :, :]).then_inc(s("o_stored%d" % hp), 16)

            for hp in range(HEADS_PER_PASS):
                load_mask_factors(0, hp)
                load_head(0, hp)

            def one(i, last):
                for hp in range(HEADS_PER_PASS):
                    if not last:
                        load_mask_factors(i + 1, hp, at(i, STEPS, B * hp + 1))
                        load_head(i + 1, hp, at(i, STEPS, B * hp + 2))
                    store(i, hp)

            with sp.Fori(0, PASSES - 1) as i:
                one(i, False)
            one(PASSES - 1, True)
            sp.wait_ge(s("o_stored0"), START + STORES * PASSES)
            sp.wait_ge(s("o_stored1"), START + STORES * PASSES)
            sp.dma_start(o_all, o_dram[0]).then_inc(s("o_loaded"), 16)
            sp.dma_start(s_all, o_dram[1]).then_inc(s("o_loaded"), 16)

        def stepping(eng, scored, quarter, values, turned):
            for tile in range(TPB):
                quarter(0, tile)
            for st in range(2):
                scored(0, st)
                quarter(0, st + TPB)
            turned(0, 0)

            def one(i, last):
                def of(k):
                    return (i, k) if k < STEPS else (i + 1, k - STEPS)
                for st in range(STEPS):
                    if not (last and st + 2 >= STEPS):
                        scored(*of(st + 2))
                    values(i, st)
                    if not (last and st + 2 + TPB >= STEPS):
                        quarter(*of(st + 2 + TPB))
                    if not (last and st + 1 >= STEPS):
                        turned(*of(st + 1))

            with eng.Fori(0, PASSES - 1) as i:
                one(i, False)
            one(PASSES - 1, True)

        def nothing(i, st):
            pass

        def attn_pe(pe):
            pe.wait_ge(s("a_biased"), START + 2 * B)
            pe.wait_ge(s("a_values"), START + B + 2)

            def scored(i, st):
                hp, b = st // B, st % B
                if b == 0:
                    pe.wait_ge(s(f"head{hp}_loaded"), START + at(i, 12 * 16, 12 * 16))
                for t in range(TPB):
                    pe.wait_ge(s("a_exp"), START + at(i, TPB * STEPS, TPB * (st - 1) + t + 1) if st or type(i) is not int or i else START)
                    pe.matmul(PS[:, t, :], q_st[hp][0:KS, b, t * P:(t + 1) * P], k_st[hp][0:KS, b, :], start=True,
                              stop=True).then_inc(s("a_scores"), 1)

            def quarter(i, q):
                hp, tile = q // TPB, q % TPB
                if tile == 0:
                    pe.wait_ge(s(f"factors{hp}_loaded"), START + at(i, 32, 32))
                pe.wait_ge(s("mask_clamped"), START + at(i, STEPS, q))
                pe.matmul(PS[:, 7, :], mq_st[hp][0:MF, tile * P:(tile + 1) * P], mk_st[hp][0:MF, :], start=True,
                          stop=True).then_inc(s("mask_arg"), 1)

            def turned(i, st):
                for t in range(TPB):
                    if t % 2 == 0:
                        pe.wait_ge(s("a_masked"), START + at(i, 2 * STEPS, 2 * st + t // 2 + 1))
                    pe.wait_ge(s("ppT_ready"), START + at(i, TPB * STEPS, TPB * st + t - 1) if st or t or type(i) is not int else START)
                    for kt in range(TPB):
                        tr = pe.transpose(PS[:, 4 + t % 2, kt * P:(kt + 1) * P], pp[:, st % 2, t, kt * P:(kt + 1) * P], ident)
                    tr.then_inc(s("a_transposed"), 1)

            def values(i, st):
                hp, b = st // B, st % B
                pe.wait_ge(s("ppT_ready"), START + at(i, TPB * STEPS, TPB * st + TPB))
                pe.wait_ge(s("v_head_ready"), START + at(i, HEADS_PER_PASS, hp + 1))
                pe.wait_ge(s("o_copied"), START + at(i, STEPS, st))
                for kt in range(TPB):
                    for t in range(TPB):
                        mm = pe.matmul(PS[OUT_ROWS * t:OUT_ROWS * t + 2 * HD, 6, 0:P], v_head[:, hp, b * TPB + kt, :],
                                       ppT[:, kt, t * P:(t + 1) * P], start=kt == 0, stop=kt == TPB - 1)
                mm.then_inc(s("a_pv"), 1)

            stepping(pe, scored, quarter, values, turned)

        def attn_act(act):
            act.wait_ge(s("mask_rows"), START + 2)

            def scored(i, st):
                for t in range(TPB):
                    if t == 0:
                        act.wait_ge(s("a_nmax"), START + at(i, STEPS, st + 1))
                        if st >= 2 or type(i) is not int or i:
                            act.wait_ge(s("a_transposed"), START + at(i, TPB * STEPS, TPB * (st - 1)))
                    act.activation(pp[:, st % 2, t, :], PS[:, t, :], ACT.Exp, bias=a_nmax[:, st % 2, t:t + 1]).then_inc(s("a_exp"), 1)

            def quarter(i, q):
                hp, tile = q // TPB, q % TPB
                act.wait_ge(s("mask_clamped"), START + at(i, STEPS, q + 1))
                z = mk[:, hp, tile, :]
                for k, (func, bias, scale) in enumerate(((ACT.Exp, 0.0, 1.0), (ACT.Ln, 1.0, 1.0), (ACT.Exp, 0.0, -1.0),
                                                         (ACT.Ln, c_1e6, 1.0), (ACT.Exp, 0.0, 0.3))):
                    if k:
                        act.wait_ge(s("mask_stage"), START + at(i, MASK_OPS * STEPS, MASK_OPS * q + k))
                    act.activation(z, z, func, bias=bias, scale=scale).then_inc(s("mask_stage"), 1)

            def values(i, st):
                act.wait_ge(s("a_pv"), START + at(i, STEPS, st + 1))
                hp, b = st // B, st % B
                if b == 0:
                    act.wait_ge(s("o_stored%d" % hp), START + at(i, STORES))
                act.activation(o_sb[:, hp, b, :], PS[:, 6, 0:P], ACT.Copy).then_inc(s("o_copied"), 1)

            act.preload_act_table_set("natural_log_exp_and_others")
            stepping(act, scored, quarter, values, nothing)

        def attn_dve(v):
            v.wait_ge(s("a_values"), START + B + 2)
            v.wait_ge(s("mask_rows"), START + 2)

            def scored(i, st):
                v.wait_ge(s("a_scores"), START + at(i, TPB * STEPS, TPB * (st + 1)))
                v.wait_ge(s("a_exp"), START + at(i, TPB * STEPS, TPB * (st - 1)) if st or type(i) is not int or i else START)
                v.tensor_reduce(a_nmax[:, st % 2, :], PS[:, 0:TPB, :], AX.X, ALU.max, negate=True).then_inc(s("a_nmax"), 1)

            def quarter(i, q):
                hp, tile = q // TPB, q % TPB
                v.wait_ge(s("mask_arg"), START + at(i, STEPS, q + 1))
                if q >= 2 * B or type(i) is not int or i:
                    v.wait_ge(s("a_masked"), START + at(i, 2 * STEPS, 2 * B * (hp - 1)))
                v.tensor_scalar(mk[:, hp, tile, :], PS[:, 7, :], acol[:, 5:6], MASK_CLAMP, ALU.mult,
                                ALU.min).then_inc(s("mask_clamped"), 1)

            def turned(i, st):
                hp, b = st // B, st % B
                v.wait_ge(s("a_pv"), START + at(i, STEPS, st))
                if b == 0:
                    h = i * HEADS_PER_PASS + hp
                    plain_wait(v)
                    v.tensor_copy(v_head[:, hp, :, 0:HD], v_all[:, :, bass.ds(h * HD, HD)]).then_inc(s("v_head_ready"), 1)
                for t in range(TPB):
                    v.wait_ge(s("a_transposed"), START + at(i, TPB * STEPS, TPB * st + t + 1))
                    v.tensor_copy(ppT[:, :, t * P:(t + 1) * P],
                                  PS[:, 4 + t % 2, :].rearrange("p (a b) -> p a b", a=TPB)).then_inc(s("ppT_ready"), 1)

            stepping(v, scored, quarter, nothing, turned)

        def attn_pool(g):
            with g.Fori(0, PASSES) as i:
                for st in range(STEPS):
                    hp = st // B
                    if st % B == 0:
                        g.wait_ge(s("mask_stage"), START + at(i, MASK_OPS * STEPS, MASK_OPS * TPB * (hp + 1)))
                    for half in range(2):
                        g.wait_ge(s("a_exp"), START + at(i, TPB * STEPS, TPB * st + 2 * half + 2))
                        a = pp[:, st % 2, 2 * half:2 * half + 2, :]
                        g.tensor_tensor(a, a, mk[:, hp, 2 * half:2 * half + 2, :], ALU.mult).then_inc(s("a_masked"), 1)

        def attn_out_pe(pe):
            for b in range(B):
                pe.wait_ge(s("att_ready"), START + 2 * b + 2)
                pe.matmul(PS[:, b, :], aw[:, 3, :], att[:, b % 2, :], start=True, stop=True).then_inc(s("a_out"), 1)

        def attn_out_dve(v):
            v.wait_ge(s("o_loaded"), START + 32)

            def added(b):
                v.wait_ge(s("a_out"), START + b + 1)
                v.scalar_tensor_tensor(xT[:, b, :], PS[:, b, :], acol[:, 2:3], xT[:, b, :], ALU.add, ALU.add).then_inc(s("x_ready"), 1)

            for b in range(B):
                v.reciprocal(inv[:, b % 2, :], s_all[:, b, :]).then_inc(s("att_ready"), 1)
                v.wait_ge(s("att_ready"), START + 2 * b + 1)
                if b >= 2:
                    v.wait_ge(s("a_out"), START + b - 1)
                v.tensor_tensor(att[:, b % 2, :], o_all[:, b, :], inv[:, b % 2, :], ALU.mult).then_inc(s("att_ready"), 1)
                if b:
                    added(b - 1)
            added(B - 1)

        stage_memory(arena_r)
        m_hi = carve([L], F32R)
        m_lo = carve([L], F32R)
        gu_hi = carve([E, 2 * F], F32R)
        dn_hi = carve([E, FCH, D], F32R)
        sgu_hi, sgu_lo = carve([2 * FS], F32R), carve([2 * FS], F32R)
        sdn_hi, sdn_lo = carve([D], F32R), carve([D], F32R)
        mh_hi, mh_lo = carve([4, L], F32R), carve([4, L], F32R)
        memory[0] = arena
        m_next = carve([L])
        lg = carve([3, TPB, E])
        tops = carve([TPB, E])
        top_i = carve([TPB, E])
        top_u = top_i.bitcast(U32)
        top_f = carve([TPB, E])
        e_small = carve([6, TPB])
        eq = carve([3, TPB, E])
        comb = carve([TPB, E])
        c_rest = carve([2, L])
        comb3 = carve([L], BF16)
        c_two = carve([L], BF16)
        cb = carve([2, L])
        gc, sl = carve([2, L]), carve([2, L])
        mh = carve([3, L])
        weighted = carve([2, L])
        acc = carve([L])
        MOE_CHUNKS = [(e, c) for e in range(E) for c in range(FCH)] + [(E, 0)]
        LAG = 4
        NMC = len(MOE_CHUNKS)

        HIDDEN = 4
        SPLITS = 2 * (E + 1)
        POOL_EXPERTS = 3

        def moe_weights(e, c):
            if e == E:
                return ((sgu_hi[:, 0:FS], sgu_lo[:, 0:FS]), (sgu_hi[:, FS:2 * FS], sgu_lo[:, FS:2 * FS]), (sdn_hi, sdn_lo))
            g, u = slice(c * P, (c + 1) * P), slice(F + c * P, F + (c + 1) * P)
            return ((gu_hi[:, e, g], gu_lo[:, e, g]), (gu_hi[:, e, u], gu_lo[:, e, u]),
                    (dn_hi[:, e, c, :], dn_lo[:, e, c, :]))

        def split_weights(e):
            if e == E:
                return (sgu[:], sgu_hi, sgu_lo), (sdn[:], sdn_hi, sdn_lo)
            return (gu[:, e, :], gu_hi[:, e, :], gu_lo[:, e, :]), (dn[:, e, :, :], dn_hi[:, e, :, :], dn_lo[:, e, :, :])

        SPLIT_ORDER = list(range(E - POOL_EXPERTS)) + [E] + list(range(E - POOL_EXPERTS, E))

        def split_high(act, m):
            for e in SPLIT_ORDER:
                if e < E and e % 4 == 0:
                    act.wait_ge(s(f"experts{e // 4}_loaded"), START + 128 * (m + 1))
                for w, hi, _ in split_weights(e):
                    act.activation(hi, w, ACT.Copy).then_inc(s("weights_high"), 1)

        def split_low(eng, name, experts, m):
            for e in experts:
                k = SPLIT_ORDER.index(e)
                for i, (w, hi, lo) in enumerate(split_weights(e)):
                    eng.wait_ge(s("weights_high"), START + 2 * FFN_SPLITS + SPLITS * m + 2 * k + i + 1)
                    eng.tensor_tensor(lo, w, hi.bitcast(F32), ALU.subtract).then_inc(s(name), 1)

        DVE_EXPERTS = SPLIT_ORDER[:-POOL_EXPERTS]

        def moe_pe(pe, m):
            pe.wait_ge(s("x_ready"), START + x_of(f"moe{m}"))
            pe.wait_ge(s("late_loads"), START + 176)

            def ahead(b, part):
                e = b + first_ln[f"moe{m}"]
                if part == 0:
                    ln_mean(xT[:, b, :], 7)
                if part == 1:
                    ln_variance(e, 7)
                if part == 2:
                    pe.wait_ge(s("ln_done"), START + e + 1)
                    for t in range(TPB):
                        mm = pe.matmul(PS[:, 7, t * E:(t + 1) * E], m_next[:, t * P:(t + 1) * P], rw[:], start=True, stop=True)
                    mm.then_inc(s("logits"), 1)

            def one(b, last):
                n = b + B * m
                pe.wait_ge(s("moe_input"), START + at(n, 2, 2))

                def down(k):
                    e, c = MOE_CHUNKS[k]
                    pe.wait_ge(s("hidden_low"), START + at(n, NMC, k + 1))
                    if c == 0:
                        pe.wait_ge(s("moe_weighted"), START + at(n, E + 1, max(e - 1, 0)))
                    last = c == FCH - 1 or e == E
                    mm = product(pe, PS[:, 4 + e % 2, :], moe_weights(e, c)[2], mh_hi[:, k % HIDDEN, :], mh_lo[:, k % HIDDEN, :],
                                 c == 0, last)
                    mm.then_inc(s("moe_down"), 1)

                def comb_rows():
                    pe.wait_ge(s("comb_ready"), START + n + 1)
                    for t in range(TPB):
                        tr = pe.transpose(PS[0:E, 7, t * P:(t + 1) * P], comb[:, t, :], ident)
                    tr.then_inc(s("combT"), 1)

                def comb_bcast(e):
                    if e == 0:
                        pe.wait_ge(s("comb_split"), START + at(n, 6, 6))
                    pe.wait_ge(s("cb_ready"), START + at(n, E, e))
                    pe.matmul(PS[:, 6, :], sel_b[0:96, e, :], comb3[0:96, :], start=True, stop=True).then_inc(s("cb_done"), 1)

                for k in range(NMC + LAG):
                    if k < NMC:
                        e, c = MOE_CHUNKS[k]
                        wg, wu, _ = moe_weights(e, c)
                        if c == 0 and e in DVE_EXPERTS:
                            pe.wait_ge(s("low_by_dve"), START + 2 * FFN_SPLITS + 2 * len(DVE_EXPERTS) * m
                                       + 2 * DVE_EXPERTS.index(e) + 2)
                        elif c == 0:
                            pe.wait_ge(s("low_by_pool"), START + 2 * POOL_EXPERTS * m + 2 * (e - E + POOL_EXPERTS) + 2)
                        pe.wait_ge(s("moe_clipped"), START + reuse(n, NMC, k, 2))
                        product(pe, PS[:, k % 2, :], wg, m_hi, m_lo).then_inc(s("moe_proj"), 1)
                        pe.wait_ge(s("moe_hidden"), START + reuse(n, NMC, k, 2))
                        product(pe, PS[:, 2 + k % 2, :], wu, m_hi, m_lo).then_inc(s("moe_proj"), 1)
                    if k == 1:
                        comb_rows()
                    if not last and k in AHEAD_PE:
                        if k == AHEAD_PE[0]:
                            pe.wait_ge(s("comb_split"), START + at(n, 6, 2))
                        ahead(b + 1, AHEAD_PE.index(k))
                    if k >= LAG:
                        down(k - LAG)
                        e, c = MOE_CHUNKS[k - LAG]
                        if c == 1:
                            comb_bcast(e)

            for part in range(3):
                ahead(0, part)
            with pe.Fori(0, B - 1) as b:
                one(b, False)
            one(B - 1, True)

        def moe_act(act, m):
            act.wait_ge(s("x_ready"), START + x_of(f"moe{m}"))

            def ahead(b, part):
                e = b + first_ln[f"moe{m}"]
                if part == 0:
                    ln_square(e)
                if part == 1:
                    act.preload_act_table_set("natural_log_exp_and_others")
                    ln_rstd(e, 7)
                if part == 2:
                    act.wait_ge(s("logits_shifted"), START + b + B * m + 1)
                    act.activation(lg[:, 1, :, :], lg[:, 0, :, :], ACT.Exp).then_inc(s("logits_exp"), 1)

            def take_input(b):
                act.wait_ge(s("moe_proj"), START + at(b + B * m, 2 * NMC))
                act.wait_ge(s("ln_done"), START + b + first_ln[f"moe{m}"] + 1)
                plain_wait(act)
                act.activation(m_hi, m_next, ACT.Copy).then_inc(s("moe_input"), 1)

            def one(b, last):
                n = b + B * m
                for k in range(NMC + LAG + 1):
                    if not last and k in AHEAD_ACT:
                        ahead(b + 1, AHEAD_ACT.index(k))
                    if k < NMC:
                        act.wait_ge(s("moe_clipped"), START + at(n, NMC, k + 1))
                        act.wait_ge(s("moe_hidden"), START + reuse(n, NMC, k, 2))
                        act.activation(sl[:, k % 2, :], gc[:, k % 2, :], ACT.Silu).then_inc(s("moe_silu"), 1)
                    if 1 <= k <= NMC:
                        j = k - 1
                        act.wait_ge(s("moe_hidden"), START + at(n, NMC, j + 1))
                        act.wait_ge(s("moe_down"), START + reuse(n, NMC, j, HIDDEN))
                        act.activation(mh_hi[:, j % HIDDEN, :], mh[:, j % 3, :], ACT.Copy).then_inc(s("hidden_high"), 1)
                    if k == NMC + 1 and not last:
                        take_input(b + 1)
                    if k > LAG and MOE_CHUNKS[k - LAG - 1][1] == 1:
                        e = MOE_CHUNKS[k - LAG - 1][0]
                        act.wait_ge(s("cb_done"), START + at(n, E, e + 1))
                        act.wait_ge(s("moe_weighted"), START + at(n, E + 1, max(e - 1, 0)))
                        act.activation(cb[:, e % 2, :], PS[:, 6, :], ACT.Copy).then_inc(s("cb_ready"), 1)

            ahead(0, 0)
            ahead(0, 1)
            take_input(0)
            split_high(act, m)
            ahead(0, 2)
            with act.Fori(0, B - 1) as b:
                one(b, False)
            one(B - 1, True)

        def moe_dve(v, m):
            v.wait_ge(s("x_ready"), START + x_of(f"moe{m}"))

            def ahead(b, part):
                e, n = b + first_ln[f"moe{m}"], b + B * m
                chain = [0, 0, 0, 1, 4, 6, 8, 10, 12, 15, 18][part]

                def then(ins):
                    nonlocal chain
                    chain += 1
                    ins.then_inc(s("route_step"), 1)
                    v.wait_ge(s("route_step"), START + at(n, ROUTE_STEPS, chain))

                def bc(a):
                    return a.unsqueeze(2).broadcast_to([P, TPB, E])

                if part == 0:
                    ln_centre(xT[:, b, :], e, 7)
                elif part == 1:
                    ln_scale(e, mcol[:, 0:1], mcol[:, 1:2], m_next, free=[("moe_input", at(n, 2))])
                elif part == 2:
                    v.wait_ge(s("logits"), START + n + 1)
                    logits = PS[:, 7, 0:TPB * E].rearrange("p (a b) -> p a b", a=TPB)
                    then(v.tensor_reduce(e_small[:, 0, :], logits, AX.X, ALU.max))
                    v.tensor_tensor(lg[:, 0, :, :], logits, bc(e_small[:, 0, :]), ALU.subtract).then_inc(s("logits_shifted"), 1)
                elif part == 3:
                    v.wait_ge(s("logits_exp"), START + n + 1)
                    then(v.tensor_reduce(e_small[:, 1, :], lg[:, 1, :, :], AX.X, ALU.add))
                    then(v.reciprocal(e_small[:, 2, :], e_small[:, 1, :]))
                    then(v.tensor_tensor(lg[:, 2, :, :], lg[:, 1, :, :], bc(e_small[:, 2, :]), ALU.mult))
                elif part < 8:
                    t = part - 4
                    plain_wait(v)
                    then(v.max(tops[:, t, :], lg[:, 2, t, :]))
                    plain_wait(v)
                    then(v.max_index(top_u[:, t, :], tops[:, t, :], lg[:, 2, t, :]))
                elif part == 8:
                    then(v.tensor_copy(top_f, top_u))
                    then(v.tensor_tensor(e_small[:, 3, :], tops[:, :, 0], tops[:, :, 1], ALU.add))
                    then(v.reciprocal(e_small[:, 4, :], e_small[:, 3, :]))
                else:
                    i = part - 9
                    iota = con[:, C_IOTA:C_IOTA + TPB * E].rearrange("p (a b) -> p a b", a=TPB)
                    then(v.tensor_tensor(e_small[:, 5, :], tops[:, :, i], e_small[:, 4, :], ALU.mult))
                    then(v.tensor_tensor(eq[:, i, :, :], iota, bc(top_f[:, :, i]), ALU.is_equal))
                    then(v.tensor_tensor(eq[:, i, :, :], eq[:, i, :, :], bc(e_small[:, 5, :]), ALU.mult))
                    if i:
                        v.tensor_tensor(comb, eq[:, 0, :, :], eq[:, 1, :, :], ALU.add).then_inc(s("comb_ready"), 1)
                        assert chain == ROUTE_STEPS, chain

            def take_input(b):
                n = b + B * m
                v.wait_ge(s("moe_proj"), START + at(n, 2 * NMC))
                v.wait_ge(s("moe_input"), START + at(n, 2, 1))
                v.tensor_tensor(m_lo, m_next, m_hi.bitcast(F32), ALU.subtract).then_inc(s("moe_input"), 1)

            def one(b, last):
                n = b + B * m

                def comb_parts():
                    v.wait_ge(s("combT"), START + n + 1)
                    T, c1, c2 = PS[0:E, 7, :], comb3[0:E], c_two[0:E]
                    r1, r2 = c_rest[0:E, 0], c_rest[0:E, 1]
                    for st, (dst, a, part) in enumerate(((c1, T, None), (r1, T, c1), (c2, r1, None), (r2, r1, c2),
                                                         (comb3[32:32 + E], c2, None), (comb3[64:64 + E], r2, None))):
                        if st:
                            v.wait_ge(s("comb_split"), START + at(n, 6, st))
                        ins = v.tensor_copy(dst, a) if part is None else v.tensor_tensor(dst, a, part, ALU.subtract)
                        ins.then_inc(s("comb_split"), 1)

                def weigh(e):
                    last = at(n, NMC, min((e + 1) * FCH, NMC))
                    v.wait_ge(s("moe_down"), START + last)
                    v.wait_ge(s("moe_acc"), START + at(n, E, max(e - 1, 0) if e < E else E))
                    if e < E:
                        v.wait_ge(s("cb_ready"), START + at(n, E, e + 1))
                        v.tensor_tensor(weighted[:, e % 2, :], PS[:, 4 + e % 2, :], cb[:, e % 2, :], ALU.mult).then_inc(s("moe_weighted"), 1)
                    else:
                        v.tensor_tensor(weighted[:, 0, :], PS[:, 4, :], acc, ALU.add).then_inc(s("moe_weighted"), 1)

                for k in range(NMC + LAG + 1):
                    if k == 2:
                        comb_parts()
                    if not last and k in AHEAD_DVE:
                        ahead(b + 1, AHEAD_DVE.index(k))
                    if k < NMC:
                        v.wait_ge(s("moe_proj"), START + at(n, 2 * NMC, 2 * k + 1))
                        v.wait_ge(s("moe_silu"), START + reuse(n, NMC, k, 2))
                        v.tensor_scalar(gc[:, k % 2, :], PS[:, k % 2, :], 10.0, -10.0, ALU.min, ALU.max).then_inc(s("moe_clipped"), 1)
                    if 1 <= k <= NMC:
                        j = k - 1
                        v.wait_ge(s("moe_silu"), START + at(n, NMC, j + 1))
                        v.wait_ge(s("moe_proj"), START + at(n, 2 * NMC, 2 * j + 2))
                        v.wait_ge(s("hidden_low"), START + reuse(n, NMC, j, 3))
                        v.tensor_tensor(mh[:, j % 3, :], sl[:, j % 2, :], PS[:, 2 + j % 2, :], ALU.mult).then_inc(s("moe_hidden"), 1)
                    if k == NMC + 1 and not last:
                        take_input(b + 1)
                    if k > LAG + 1 and MOE_CHUNKS[k - LAG - 1][1] == 0:
                        weigh(MOE_CHUNKS[k - LAG - 1][0] - 1)
                weigh(E)
                v.wait_ge(s("moe_weighted"), START + at(n, E + 1, E + 1))
                v.scalar_tensor_tensor(xT[:, b, :], weighted[:, 0, :], 0.5, xT[:, b, :], ALU.mult, ALU.add).then_inc(s("x_ready"), 1)

            ahead(0, 0)
            ahead(0, 1)
            take_input(0)
            split_low(v, "low_by_dve", DVE_EXPERTS, m)
            for part in range(2, AHEAD_PARTS):
                ahead(0, part)
            with v.Fori(0, B - 1) as b:
                one(b, False)
            one(B - 1, True)

        ROUTE_STEPS = 4 + 2 * TPB + 3 + 6
        AHEAD_PARTS = 3 + 1 + TPB + 1 + 2
        AHEAD_PE, AHEAD_ACT = (6, 8, 12), (7, 8, 14)
        AHEAD_DVE = (6, 10, 13) + tuple(range(16, 16 + AHEAD_PARTS - 3))

        def moe_pool(g, m):
            g.memset(comb3[0:96, :].bitcast(F32), 0.0).then_inc(s("comb3_zero"), 1)
            split_low(g, "low_by_pool", SPLIT_ORDER[-POOL_EXPERTS:], m)
            with g.Fori(0, B) as b:
                n = b + B * m
                for k in range(NMC + LAG + 1):
                    if k < NMC:
                        g.wait_ge(s("hidden_high"), START + at(n, NMC, k + 1))
                        g.wait_ge(s("moe_down"), START + reuse(n, NMC, k, HIDDEN))
                        g.tensor_tensor(mh_lo[:, k % HIDDEN, :], mh[:, k % 3, :], mh_hi[:, k % HIDDEN, :].bitcast(F32),
                                        ALU.subtract).then_inc(s("hidden_low"), 1)
                    e = (k - LAG - 1 - FCH) // FCH
                    if (k - LAG - 1) % FCH == 0 and 0 <= e < E:
                        g.wait_ge(s("moe_weighted"), START + at(n, E + 1, e + 1))
                        g.wait_ge(s("moe_acc"), START + at(n, E, e))
                        if e == 0:
                            plain_wait(g)
                            g.tensor_copy(acc, weighted[:, 0, :]).then_inc(s("moe_acc"), 1)
                        else:
                            g.tensor_tensor(acc, acc, weighted[:, e % 2, :], ALU.add).then_inc(s("moe_acc"), 1)

        stage_memory()
        t_xn = carve([L])
        qT, kT, vT = (carve([B, L]) for _ in range(3))
        k_tok = carve([B * TPB, D])
        raw, rsq, rlog = carve([2, L]), carve([2, L]), carve([2, L])
        k_s = carve([L])
        kt_s = carve([TPB, D])
        sg, g_m, g_d = carve([2, TH]), carve([2, TH]), carve([2, TH])
        start = taken[0]
        th_h, th_s, th_w = (carve([TPB, TH]) for _ in range(3))
        end, taken[0] = taken[0], start
        X = [carve([TH]) for _ in range(3)]
        XT = [carve([4, D]) for _ in range(3)]
        A_s, A_b, B_s = ([carve([D]) for _ in range(3)] for _ in range(3))
        gsq = carve([TH])
        assert taken[0] <= end
        taken[0] = end
        hT = carve([4, L])
        dp = carve([L])
        dp_tok = carve([TPB, D])
        du, dg = carve([2, TH]), carve([2, TH])
        grad = carve([3, TH])
        nrm = carve([4, 4])
        a_ident = carve([D])
        v_bias = carve([1])

        def over_batches(eng, one):
            with eng.Fori(0, B - 1) as b:
                one(b, False)
            one(B - 1, True)

        def ttt_proj_pe(pe):
            pe.wait_ge(s("x_ready"), START + x_of("ttt"))
            pe.wait_ge(s("late_loads"), START + 176)
            ln_pe(xT[:, 0, :], first_ln["ttt"], 6, 7)

            def one(b, last):
                e = b + first_ln["ttt"]
                pe.wait_ge(s("ln_done"), START + e + 1)
                pe.wait_ge(s("t_biased"), START + at(b, 3))
                for i in range(3):
                    pe.matmul(PS[:, i, :], tqkv[:, i * D:(i + 1) * D], t_xn, start=True, stop=True).then_inc(s("t_proj"), 1)
                pe.wait_ge(s("t_squared"), START + b + 1)
                for i in range(2):
                    mm = pe.matmul(PS[:, 3 + i, :], blk8, rsq[:, i, :], start=True, stop=True)
                mm.then_inc(s("t_proj"), 1)
                if not last:
                    ln_pe(xT[:, b + 1, :], e + 1, 6, 7)
                pe.wait_ge(s("k_staged"), START + at(b, 1, 1))
                pe.wait_ge(s("k_tok_ready"), START + at(b, 1))
                for t in range(TPB):
                    tr = pe.transpose(PS[:, 5, t * P:(t + 1) * P], k_s[:, t * P:(t + 1) * P], ident)
                tr.then_inc(s("k_transposed"), 1)

            over_batches(pe, one)

        def ttt_proj_act(act):
            act.wait_ge(s("x_ready"), START + x_of("ttt"))
            act.wait_ge(s("ttt_consts"), START + 2)
            act.preload_act_table_set("natural_log_exp_and_others")
            ln_act(first_ln["ttt"], 7)

            def one(b, last):
                e = b + first_ln["ttt"]
                for i in range(3):
                    act.wait_ge(s("t_proj"), START + at(b, 4, i + 1))
                    act.wait_ge(s("t_scaled"), START + at(b, 2))
                    dst = raw[:, i, :] if i < 2 else vT[:, b, :]
                    plain_wait(act)
                    act.activation(dst, PS[:, i, :], ACT.Identity, bias=tcol[:, 4 + i:5 + i] if i < 2 else v_bias,
                                   scale=1.0 if i < 2 else GRAD_SCALE).then_inc(s("t_biased"), 1)
                    if i == 1:
                        act.wait_ge(s("t_biased"), START + at(b, 3, 2))
                        act.activation(rsq, raw, ACT.Square).then_inc(s("t_squared"), 1)
                act.wait_ge(s("t_proj"), START + at(b, 4, 4))
                c = at(b, 4)
                act.activation(rlog, PS[:, 3:5, :], ACT.Ln, bias=c_tiny, scale=2.0 ** LS).then_inc(s("t_norm_step"), 1)
                act.wait_ge(s("t_norm_step"), START + c + 1)
                act.activation(rlog, rlog, ACT.Exp, bias=c_neg, scale=0.5).then_inc(s("t_norm_step"), 1)
                if not last:
                    ln_square(e + 1)
                act.wait_ge(s("t_norm_step"), START + c + 2)
                act.activation(rlog, rlog, ACT.Ln, bias=c_1e6).then_inc(s("t_norm_step"), 1)
                act.wait_ge(s("t_norm_step"), START + c + 3)
                act.activation(rlog, rlog, ACT.Exp, scale=-1.0).then_inc(s("t_norm_step"), 1)
                if not last:
                    ln_rstd(e + 1, 7)

            over_batches(act, one)

        def ttt_proj_dve(v):
            v.wait_ge(s("x_ready"), START + x_of("ttt"))
            v.wait_ge(s("late_loads"), START + 176)
            v.tensor_scalar(v_bias, tcol[:, 6:7], GRAD_SCALE, None, ALU.mult).then_inc(s("ttt_consts"), 1)
            v.tensor_scalar(a_ident, ident, NS_A, None, ALU.mult).then_inc(s("ttt_consts"), 1)
            ln_dve(xT[:, 0, :], first_ln["ttt"], 6, c_one, c_zero, t_xn)

            def one(b, last):
                e = b + first_ln["ttt"]
                if not last:
                    ln_centre(xT[:, b + 1, :], e + 1, 6)
                for i in range(2):
                    v.wait_ge(s("t_norm_step"), START + at(b, 4, 4))
                    v.scalar_tensor_tensor(raw[:, i, :], raw[:, i, :], tcol[:, 2 * i:2 * i + 1], rlog[:, i, :], ALU.mult,
                                           ALU.mult).then_inc(s("t_scaled"), 1)
                v.wait_ge(s("t_scaled"), START + at(b, 2, 2))
                v.wait_ge(s("k_transposed"), START + at(b, 1))
                v.tensor_scalar(k_s, raw[:, 1, :], tcol[:, 3:4], None, ALU.add).then_inc(s("k_staged"), 1)
                for i, dst in enumerate((qT, kT)):
                    v.tensor_scalar(dst[:, b, :], raw[:, i, :], tcol[:, 2 * i + 1:2 * i + 2], None, ALU.add)
                if not last:
                    ln_scale(e + 1, c_one, c_zero, t_xn, free=[("t_proj", at(b, 4, 3))])
                v.wait_ge(s("k_transposed"), START + at(b, 1, 1))
                plain_wait(v)
                v.tensor_copy(k_tok[:, bass.ds(b * TPB, TPB), :], PS[:, 5, :].rearrange("p (a b) -> p a b", a=TPB)).then_inc(s("k_tok_ready"), 1)

            over_batches(v, one)

        def grad_pe(pe, step):
            with pe.Fori(0, B) as b:
                n = b + B * step
                pe.wait_ge(s("staged"), START + at(n, 2, 1))
                pe.wait_ge(s("theta_ready"), START + 4 * step)

                def turn(t):
                    pe.wait_ge(s("g_h"), START + at(n, TPB, t + 1))
                    pe.wait_ge(s("hT_ready"), START + at(n, TPB, t))
                    for c in range(4):
                        tr = pe.transpose(PS[:, 4, c * P:(c + 1) * P], th_h[:, t, c * P:(c + 1) * P], ident)
                    tr.then_inc(s("h_turned"), 1)

                def predict(t):
                    pe.wait_ge(s("hT_ready"), START + at(n, TPB, t + 1))
                    if t == 0:
                        pe.wait_ge(s("grad_added"), START + at(n, 3))
                    for c in range(4):
                        mm = pe.matmul(PS[:, 5, t * P:(t + 1) * P], th_p[:, c, :], hT[:, c, t * P:(t + 1) * P], start=c == 0,
                                       stop=c == 3)
                    if t == TPB - 1:
                        mm.then_inc(s("predicted"), 1)

                for t in range(TPB):
                    kt = k_s[:, t * P:(t + 1) * P]
                    pe.wait_ge(s("g_w"), START + at(n, TPB, max(t - 1, 0)))
                    if t < 2:
                        pe.wait_ge(s("g_dg"), START + at(n, TPB))
                    pe.matmul(PS[:, t % 2, :], kt, th_g[:], start=True, stop=True).then_inc(s("g_gate"), 1)
                    pe.matmul(PS[:, 2 + t % 2, :], kt, th_v[:], start=True, stop=True).then_inc(s("g_val"), 1)
                    if t >= 2:
                        predict(t - 2)
                    if t >= 1:
                        turn(t - 1)
                predict(TPB - 2)
                turn(TPB - 1)
                predict(TPB - 1)
                pe.wait_ge(s("dp_ready"), START + at(n, 1, 1))
                for t in range(TPB):
                    tr = pe.transpose(PS[:, 4, t * P:(t + 1) * P], dp[:, t * P:(t + 1) * P], ident)
                tr.then_inc(s("dp_turned"), 1)

                def dh(t):
                    pe.wait_ge(s("g_w"), START + at(n, TPB, TPB))
                    pe.wait_ge(s("g_dg"), START + at(n, TPB, max(t - 1, 0)))
                    pe.matmul(PS[:, t % 2, :], dp[:, t * P:(t + 1) * P], th_pT[:], start=True, stop=True).then_inc(s("g_dh"), 1)

                dh(0)
                pe.wait_ge(s("dp_tok_ready"), START + at(n, 1, 1))
                pe.wait_ge(s("staged"), START + at(n, 2, 2))
                for t in range(TPB):
                    if t < TPB - 1:
                        dh(t + 1)
                    st, sp_ = t == 0, t == TPB - 1
                    mm = pe.matmul(PS[:, 5, :], dp_tok[:, t, :], th_h[:, t, :], start=st, stop=sp_)
                    if sp_:
                        mm.then_inc(s("grads"), 1)
                    pe.wait_ge(s("g_du"), START + at(n, TPB, t + 1))
                    mm = pe.matmul(PS[:, 6, :], kt_s[:, t, :], du[:, t % 2, :], start=st, stop=sp_)
                    if sp_:
                        mm.then_inc(s("grads"), 1)
                    pe.wait_ge(s("g_dg"), START + at(n, TPB, t + 1))
                    pe.matmul(PS[:, 7, :], kt_s[:, t, :], dg[:, t % 2, :], start=st, stop=sp_).then_inc(s("g_used"), 1)

        def grad_act(act, step):
            with act.Fori(0, B) as b:
                n = b + B * step
                for t in range(TPB + 1):
                    if t < TPB:
                        act.wait_ge(s("g_gate"), START + at(n, TPB, t + 1))
                        act.wait_ge(s("g_w"), START + at(n, TPB, max(t - 1, 0)))
                        act.activation(sg[:, t % 2, :], PS[:, t % 2, :], ACT.Sigmoid).then_inc(s("g_sig"), 1)
                        act.activation(g_m[:, t % 2, :], PS[:, t % 2, :], ACT.Sigmoid, scale=-1.0).then_inc(s("g_sig"), 1)
                    if t >= 1:
                        act.wait_ge(s("h_turned"), START + at(n, TPB, t))
                        if t == 1:
                            act.wait_ge(s("predicted"), START + n)
                        act.activation(hT[:, :, (t - 1) * P:t * P], PS[:, 4, :].rearrange("p (a b) -> p a b", a=4),
                                       ACT.Copy).then_inc(s("hT_ready"), 1)
                act.wait_ge(s("dp_turned"), START + n + 1)
                act.wait_ge(s("grads"), START + at(n, 2))
                act.activation(dp_tok.rearrange("p a b -> p (a b)"), PS[:, 4, :], ACT.Copy).then_inc(s("dp_tok_ready"), 1)

        def grad_dve(v, step):
            if step == 0:
                v.memset(grad, 0.0).then_inc(s("grad_zero"), 1)
            else:
                v.wait_ge(s("theta_ready"), START + 4 * step)
                v.memset(grad, 0.0).then_inc(s("grad_zero"), 1)
            v.wait_ge(s("grad_zero"), START + step + 1)
            with v.Fori(0, B) as b:
                n = b + B * step
                for t in range(TPB + 1):
                    if t < TPB:
                        v.wait_ge(s("g_sig"), START + at(n, 2 * TPB, 2 * t + 2))
                        if t == 0:
                            v.wait_ge(s("g_used"), START + at(n, TPB))
                        v.tensor_tensor(th_s[:, t, :], PS[:, t % 2, :], sg[:, t % 2, :], ALU.mult).then_inc(s("g_silu"), 1)
                        v.wait_ge(s("g_silu"), START + at(n, TPB, t + 1))
                        v.wait_ge(s("g_val"), START + at(n, TPB, t + 1))
                        v.tensor_tensor(th_h[:, t, :], th_s[:, t, :], PS[:, 2 + t % 2, :], ALU.mult).then_inc(s("g_h"), 1)
                    if t:
                        v.wait_ge(s("g_slope"), START + at(n, 2 * TPB, 2 * t))
                        v.tensor_tensor(th_w[:, t - 1, :], g_d[:, (t - 1) % 2, :], PS[:, 2 + (t - 1) % 2, :], ALU.mult).then_inc(s("g_w"), 1)
                v.wait_ge(s("predicted"), START + n + 1)
                v.wait_ge(s("grads"), START + at(n, 2))
                v.scalar_tensor_tensor(dp, PS[:, 5, :], GRAD_SCALE, vT[:, b, :], ALU.mult, ALU.subtract).then_inc(s("dp_ready"), 1)
                for t in range(TPB):
                    v.wait_ge(s("g_dh"), START + at(n, TPB, t + 1))
                    v.wait_ge(s("g_used"), START + at(n, TPB, max(t - 1, 0)))
                    v.tensor_tensor(du[:, t % 2, :], PS[:, t % 2, :], th_s[:, t, :], ALU.mult).then_inc(s("g_du"), 1)
                    v.tensor_tensor(dg[:, t % 2, :], PS[:, t % 2, :], th_w[:, t, :], ALU.mult).then_inc(s("g_dg"), 1)
                v.wait_ge(s("grads"), START + at(n, 2, 2))
                v.wait_ge(s("g_used"), START + at(n, TPB, TPB))
                v.wait_ge(s("grad_added"), START + at(n, 3))
                for i, bank in enumerate((7, 6, 5)):
                    v.tensor_tensor(grad[:, i, :], grad[:, i, :], PS[:, bank, :], ALU.add).then_inc(s("grad_added"), 1)

        def grad_pool(g, step):
            with g.Fori(0, B) as b:
                n = b + B * step
                g.wait_ge(s("k_tok_ready"), START + B)
                g.wait_ge(s("g_val"), START + at(n, TPB))
                plain_wait(g)
                g.tensor_copy(k_s, kT[:, b, :]).then_inc(s("staged"), 1)
                for t in range(TPB):
                    j = t % 2
                    g.wait_ge(s("g_silu"), START + at(n, TPB, t + 1))
                    g.wait_ge(s("g_w"), START + at(n, TPB, max(t - 1, 0)))
                    g.tensor_tensor(g_d[:, j, :], th_s[:, t, :], g_m[:, j, :], ALU.mult).then_inc(s("g_slope"), 1)
                    g.wait_ge(s("g_slope"), START + at(n, 2 * TPB, 2 * t + 1))
                    g.tensor_tensor(g_d[:, j, :], g_d[:, j, :], sg[:, j, :], ALU.add).then_inc(s("g_slope"), 1)
                g.wait_ge(s("g_used"), START + at(n, TPB))
                plain_wait(g)
                g.tensor_copy(kt_s, k_tok[:, bass.ds(b * TPB, TPB), :]).then_inc(s("staged"), 1)

        def ns_pe(pe, step):
            pe.wait_ge(s("ns_sumsq"), START + 3 * (step + 1))
            pe.matmul(PS[:, 0, 0:3], ones, nrm[:, 0, 0:3], start=True, stop=True).then_inc(s("ns_norm"), 1)
            for j in range(3):
                pe.wait_ge(s("ns_X0"), START + 3 * step + j + 1)
                for c in range(4):
                    tr = pe.transpose(PS[:, 3 + j, c * P:(c + 1) * P], X[j][:, c * P:(c + 1) * P], ident)
                tr.then_inc(s("ns_T0"), 1)
            with pe.Fori(0, NS_ITERS) as it:
                n = it + NS_ITERS * step
                for j in range(3):
                    if j == 0:
                        pe.wait_ge(s("ns_T0_copied"), START + 3 * (step + 1))
                    pe.wait_ge(s("ns_XT"), START + at(n, 3))
                    for c in range(4):
                        mm = pe.matmul(PS[:, j, 0:P], XT[j][:, c, :], XT[j][:, c, :], start=c == 0, stop=c == 3)
                    mm.then_inc(s("ns_A"), 1)
                for j in range(3):
                    pe.wait_ge(s("ns_A_copied"), START + at(n, 3, j + 1))
                    pe.wait_ge(s("ns_A_poly"), START + at(n, 3, j + 1))
                    pe.matmul(PS[:, j, P:2 * P], A_s[j], A_s[j], start=True, stop=True).then_inc(s("ns_A2"), 1)
                for j in range(3):
                    pe.wait_ge(s("ns_B"), START + at(n, 3, j + 1))
                    pe.wait_ge(s("ns_X"), START + at(n, 3))
                    pe.matmul(PS[:, 3 + j, :], B_s[j], X[j], start=True, stop=True)
                    if j >= 1:
                        pe.wait_ge(s("ns_XT"), START + (at(n, 3, j - 1) if j >= 2 else at(n, 3)))
                    for c in range(4):
                        mm = pe.matmul(PS[:, 6 + j % 2, c * P:(c + 1) * P], X[j][:, c * P:(c + 1) * P], B_s[j], start=True, stop=True)
                    mm.then_inc(s("ns_XTB"), 1)

        def ns_act(act, step):
            v3 = 3 * step
            act.preload_act_table_set("natural_log_exp_and_others")
            act.wait_ge(s("grad_added"), START + 3 * B * (step + 1))
            for j in range(3):
                if j:
                    act.wait_ge(s("ns_sumsq"), START + v3 + j)
                act.activation(gsq, grad[:, j, :], ACT.Square, accum_out=nrm[:, 0, j:j + 1]).then_inc(s("ns_sumsq"), 1)
            act.wait_ge(s("ns_norm"), START + step + 1)
            act.activation(nrm[:, 1, 0:3], PS[:, 0, 0:3], ACT.Ln, bias=c_tiny, scale=2.0 ** LS).then_inc(s("ns_scale_step"), 1)
            act.wait_ge(s("ns_scale_step"), START + 4 * step + 1)
            act.activation(nrm[:, 2, 0:3], nrm[:, 1, 0:3], ACT.Exp, bias=c_neg, scale=0.5).then_inc(s("ns_scale_step"), 1)
            for j in range(3):
                act.wait_ge(s("ns_T0"), START + v3 + j + 1)
                act.activation(XT[j].rearrange("p a b -> p (a b)"), PS[:, 3 + j, :], ACT.Copy).then_inc(s("ns_T0_copied"), 1)
            with act.Fori(0, NS_ITERS) as it:
                n = it + NS_ITERS * step
                for j in range(3):
                    act.wait_ge(s("ns_A"), START + at(n, 3, j + 1))
                    act.activation(A_s[j], PS[:, j, 0:P], ACT.Copy).then_inc(s("ns_A_copied"), 1)
                for j in range(3):
                    act.wait_ge(s("ns_XTB"), START + at(n, 3, j + 1))
                    act.activation(XT[j].rearrange("p a b -> p (a b)"), PS[:, 6 + j % 2, :], ACT.Copy).then_inc(s("ns_XT"), 1)

        def ns_dve(v, step):
            v3 = 3 * step
            v.wait_ge(s("ns_scale_step"), START + 4 * step + 2)
            v.tensor_scalar(nrm[:, 3, 0:3], nrm[:, 2, 0:3], 1e-7, None, ALU.add).then_inc(s("ns_scale_step"), 1)
            v.wait_ge(s("ns_scale_step"), START + 4 * step + 3)
            v.reciprocal(nrm[:, 1, 0:3], nrm[:, 3, 0:3]).then_inc(s("ns_scale_step"), 1)
            v.wait_ge(s("ns_scale_step"), START + 4 * step + 4)
            for j in range(3):
                v.tensor_scalar(X[j], grad[:, j, :], nrm[:, 1, j:j + 1], None, ALU.mult).then_inc(s("ns_X0"), 1)
            with v.Fori(0, NS_ITERS) as it:
                n = it + NS_ITERS * step
                for j in range(3):
                    v.wait_ge(s("ns_A_copied"), START + at(n, 3, j + 1))
                    v.scalar_tensor_tensor(A_b[j], A_s[j], NS_B, a_ident, ALU.mult, ALU.add).then_inc(s("ns_A_poly"), 1)
                for j in range(3):
                    v.wait_ge(s("ns_A2"), START + at(n, 3, j + 1))
                    v.wait_ge(s("ns_A_poly"), START + at(n, 3, j + 1))
                    v.scalar_tensor_tensor(B_s[j], PS[:, j, P:2 * P], NS_C, A_b[j], ALU.mult, ALU.add).then_inc(s("ns_B"), 1)
                for j in range(3):
                    v.wait_ge(s("ns_XTB"), START + at(n, 3, j + 1))
                    v.tensor_copy(X[j], PS[:, 3 + j, :]).then_inc(s("ns_X"), 1)
            n = NS_ITERS * (step + 1)
            v.wait_ge(s("ns_X"), START + 3 * n)
            v.wait_ge(s("ns_XT"), START + 3 * n)
            flat = lambda a: a.rearrange("p a b -> p (a b)")
            for dst, src in ((th_g[:], X[0]), (th_v[:], X[1]), (th_pT[:], X[2]), (flat(th_p[:]), flat(XT[2]))):
                v.scalar_tensor_tensor(dst, src, -LR, dst, ALU.mult, ALU.add).then_inc(s("theta_ready"), 1)

        def apply_pe(pe):
            pe.wait_ge(s("theta_ready"), START + 8)
            with pe.Fori(0, B) as b:
                def down(c):
                    pe.wait_ge(s("q_hidden"), START + at(b, 4, c + 1))
                    if c == 0:
                        pe.wait_ge(s("q_down_copied"), START + b)
                    mm = pe.matmul(PS[:, 4, :], th_p[:, c, :], hT[:, c, :], start=c == 0, stop=c == 3)
                    if c == 3:
                        mm.then_inc(s("q_down"), 1)

                for c in range(4):
                    pe.wait_ge(s("q_hidden"), START + reuse(b, 4, c, 2))
                    pe.matmul(PS[:, c % 2, :], th_g[:, c * P:(c + 1) * P], qT[:, b, :], start=True, stop=True).then_inc(s("q_proj"), 1)
                    pe.matmul(PS[:, 2 + c % 2, :], th_v[:, c * P:(c + 1) * P], qT[:, b, :], start=True, stop=True).then_inc(s("q_proj"), 1)
                    if c >= 1:
                        down(c - 1)
                down(3)
                pe.wait_ge(s("q_down_copied"), START + b + 1)
                pe.wait_ge(s("x_ready"), START + x_of("ttt") + b)
                pe.matmul(PS[:, 5, :], tpw[:], dp, start=True, stop=True).then_inc(s("q_out"), 1)

        def apply_act(act):
            with act.Fori(0, B) as b:
                for c in range(4):
                    act.wait_ge(s("q_proj"), START + at(b, 8, 2 * c + 1))
                    act.wait_ge(s("q_hidden"), START + reuse(b, 4, c, 2))
                    act.activation(sg[:, c % 2, :], PS[:, c % 2, :], ACT.Silu).then_inc(s("q_silu"), 1)
                act.wait_ge(s("q_down"), START + b + 1)
                act.wait_ge(s("q_out"), START + b)
                act.activation(dp, PS[:, 4, :], ACT.Copy).then_inc(s("q_down_copied"), 1)

        def apply_dve(v):
            with v.Fori(0, B) as b:
                for c in range(4):
                    v.wait_ge(s("q_silu"), START + at(b, 4, c + 1))
                    v.wait_ge(s("q_proj"), START + at(b, 8, 2 * c + 2))
                    if c == 0:
                        v.wait_ge(s("q_down"), START + b)
                    v.tensor_tensor(hT[:, c, :], sg[:, c % 2, :], PS[:, 2 + c % 2, :], ALU.mult).then_inc(s("q_hidden"), 1)
                v.wait_ge(s("q_out"), START + b + 1)
                v.scalar_tensor_tensor(xT[:, b, :], PS[:, 5, :], tcol[:, 7:8], xT[:, b, :], ALU.add, ALU.add).then_inc(s("x_ready"), 1)

        block = ctx.enter_context(nc.Block())
        run = STAGES[1:]

        @block.sync
        def _(sp):
            load_sync(sp)
            if "ffn1" in run:
                sp.wait_ge(s("x_ready"), START + x_of("attn"))
                sp.dma_start(wqkv, I["wqkv"]).then_inc(s("ffn_loaded"), 16)
                sp.dma_start(wswap, I["wswap"]).then_inc(s("ffn_loaded"), 16)
            if "attn" in run:
                attn_proj_sync(sp)
                attn_sync(sp)
            for m in range(2):
                if f"moe{m}" in run:
                    load_experts(sp, m)
            sp.wait_ge(s("x_ready"), START + B * len(STAGES))
            sp.dma_start(out, xT[:]).then_inc(s("out_stored"), 16)
            sp.wait_ge(s("out_stored"), START + 16)
            sp.wait_ge(s("mask_stored"), START + 32)

        @block.tensor
        def _(pe):
            pe.wait_ge(s("consts"), START + 7)
            for st in run:
                if st[:3] == "ffn":
                    f = int(st[3])
                    pe.wait_ge(s("x_ready"), START + x_of(st))
                    pe.wait_ge(s("ffn_loaded"), START + 48)
                    pe.wait_ge(s("pads_zero"), START + 5 * (f + 1))
                    ffn_pe(pe, f)
                elif st == "attn":
                    attn_proj_pe(pe)
                    attn_pe(pe)
                    attn_out_pe(pe)
                elif st[:3] == "moe":
                    pe.wait_ge(s("comb3_zero"), START + int(st[3]) + 1)
                    moe_pe(pe, int(st[3]))
                else:
                    ttt_proj_pe(pe)
                    for step in range(TTT_STEPS):
                        grad_pe(pe, step)
                        ns_pe(pe, step)
                    apply_pe(pe)

        @block.scalar
        def _(act):
            load_act(act)
            for st in run:
                if st[:3] == "ffn":
                    f = int(st[3])
                    act.wait_ge(s("x_ready"), START + x_of(st))
                    act.wait_ge(s("pads_zero"), START + 5 * (f + 1))
                    ffn_act(act, f)
                elif st == "attn":
                    attn_proj_act(act)
                    attn_act(act)
                elif st[:3] == "moe":
                    moe_act(act, int(st[3]))
                else:
                    ttt_proj_act(act)
                    for step in range(TTT_STEPS):
                        grad_act(act, step)
                        ns_act(act, step)
                    apply_act(act)

        @block.vector
        def _(v):
            load_dve(v)
            v.wait_ge(s("rot_scaled"), START + 8)
            for st in run:
                if st[:3] == "ffn":
                    f = int(st[3])
                    v.wait_ge(s("x_ready"), START + x_of(st))
                    v.wait_ge(s("mask_stored"), START + 32)
                    v.wait_ge(s("pads_zero"), START + 5 * (f + 1))
                    ffn_dve(v, f)
                elif st == "attn":
                    attn_proj_dve(v)
                    attn_dve(v)
                    attn_out_dve(v)
                elif st[:3] == "moe":
                    v.wait_ge(s("late_loads"), START + 176)
                    v.wait_ge(s("comb3_zero"), START + int(st[3]) + 1)
                    moe_dve(v, int(st[3]))
                else:
                    ttt_proj_dve(v)
                    for step in range(TTT_STEPS):
                        grad_dve(v, step)
                        ns_dve(v, step)
                    apply_dve(v)

        @block.gpsimd
        def _(g):
            for name in sorted(sems):
                g.sem_inc(sems[name], START)
            for st in run:
                g.wait_ge(s("x_ready"), START + x_of(st))
                if st[:3] == "ffn":
                    f = int(st[3])
                    ffn_zero_pads(g, f)
                    ffn_pool(g, f)
                elif st == "attn":
                    attn_pool(g)
                elif st[:3] == "moe":
                    moe_pool(g, int(st[3]))
                else:
                    for step in range(TTT_STEPS):
                        grad_pool(g, step)


def _layouts(i):
    f = lambda a: np.ascontiguousarray(np.asarray(a))
    cols = lambda *v: f(np.stack(v, -1))
    two = lambda a: np.concatenate([a, a], -1)
    swap = lambda a: np.concatenate([a[..., DH // 2:], a[..., :DH // 2]], -1)
    g = {k: np.asarray(v) for k, v in i.items()}
    wqkv = g["L0_ffn_wqkv"]
    qk = wqkv[:, :, :2 * INNER].reshape(DEPTH, D, 2 * HEADS, 2, DH // 2)[:, :, :, ::-1]
    pad = lambda a, n: np.concatenate([a, np.zeros(a.shape[:-1] + (n - a.shape[-1],), a.dtype)], -1)
    b1 = g["L0_ffn_b1"]
    b1a, b1g = (pad(b, 3 * P).reshape(DEPTH, 3, P) for b in (b1[:, :HID], b1[:, HID:]))
    qs, ks = g["L0_ffn_q_scale"], g["L0_ffn_k_scale"]
    fc = np.zeros((P, DEPTH, 16), wqkv.dtype)
    vecs = [two(qs), two(swap(qs)), two(ks), two(swap(ks)), g["L0_ffn_ln_g"], g["L0_ffn_ln_b"], g["L0_ffn_b2"]]
    vecs += [b1a[:, c] for c in range(3)] + [b1g[:, c] for c in range(3)]
    for n, v in enumerate(vecs):
        fc[:, :, n] = v.T
    w2 = pad(g["L0_ffn_w2"].transpose(0, 2, 1), 3 * P).reshape(DEPTH, D, 3, P).transpose(3, 0, 2, 1)
    ac = np.zeros((P, 8), wqkv.dtype)
    for n, k in enumerate(("L0_attn_bq", "L0_attn_bk", "L0_attn_bo")):
        ac[:, n] = g[k]
    ac[:, 3] = g["L0_attn_temperature"]
    ph = np.zeros((NH, 8), wqkv.dtype)
    ph[:, 0:3] = g["L0_attn_phase"]
    ph[:, 3] = g["L0_attn_threshold"]
    tc = np.zeros((P, 8), wqkv.dtype)
    for n, v in enumerate([np.tile(g["L1_attn_" + k], NH) for k in ("qn_scale", "qn_bias", "kn_scale", "kn_bias")]
                          + list(g["L1_attn_qkv_b"].reshape(3, D)) + [g["L1_attn_proj_b"]]):
        tc[:, n] = v
    return {
        "xT": f(g["L0_attn_x"].transpose(2, 0, 1)),
        "con": shape_constants(), "rot": rotary_tables(), "pos": position_tables(), "phase": ph,
        "wqkv": f(wqkv.transpose(1, 0, 2)),
        "wswap": f(qk.transpose(1, 0, 2, 3, 4)),
        "wo": f(g["L0_ffn_wo"].reshape(DEPTH, NCH, P, D).transpose(2, 0, 1, 3)),
        "w1": f(g["L0_ffn_w1"].transpose(1, 0, 2)),
        "w2": f(w2), "fcol": fc,
        "aw": f(np.stack([g["L0_attn_W" + k] for k in "qkvo"], 1)),
        "acol": ac, "bv_row": f(np.tile(g["L0_attn_bv"][None], (P, 1))),
        "gu": f(g["L1_ffn_gate_up_w"].transpose(1, 0, 2)),
        "dn": f(g["L1_ffn_down_w"].reshape(E, FCH, P, D).transpose(2, 0, 1, 3)),
        "sgu": f(g["L1_ffn_shared_gate_up_w"]), "sdn": f(g["L1_ffn_shared_down_w"]), "rw": f(g["L1_ffn_router_w"]),
        "mcol": cols(g["L1_ffn_ln_gamma"], g["L1_ffn_ln_beta"]),
        "tqkv": f(g["L1_attn_qkv_w"]), "tcol": tc,
        "th_g": f(g["L1_attn_ttt_gate"]), "th_v": f(g["L1_attn_ttt_val"]), "th_pT": f(g["L1_attn_ttt_proj"].T),
        "th_p": f(g["L1_attn_ttt_proj"].reshape(4, P, D).transpose(1, 0, 2)),
        "tpw": f(g["L1_attn_proj_w"]),
    }


def kernel(**inputs):
    import concourse.bacc as bacc
    from concourse.bass_utils import run_bass_kernel_spmd

    nc = bacc.Bacc("TRN2", target_bir_lowering=False, num_devices=1)
    arrays = _layouts(inputs)
    aps = {k: nc.dram_tensor("in_" + k, a.shape, F32, kind="ExternalInput").ap() for k, a in arrays.items()}
    out = nc.dram_tensor("out_xT", (D, B, L), F32, kind="ExternalOutput").ap()
    build(nc, aps, out)
    r = run_bass_kernel_spmd(nc, [{"in_" + k: a for k, a in arrays.items()}], core_ids=[0])
    return np.ascontiguousarray(np.asarray(r.results[0]["out_xT"]).transpose(1, 2, 0))
```
